# Optimizing a Trainium2 kernel written in Bass

```python
import numpy as np
import jax
import jax.numpy as jnp

def _softmax(x, axis=-1):
    return jax.nn.softmax(x, axis=axis)

def _gelu(x):
    return jax.nn.gelu(x, approximate=True)

def _silu(x):
    return jax.nn.silu(x)

def _sigmoid(x):
    return jax.nn.sigmoid(x)

def _layernorm(x, axis=-1, eps=1e-05):
    m = jnp.mean(x, axis=axis, keepdims=True)
    v = jnp.var(x, axis=axis, keepdims=True)
    return (x - m) / jnp.sqrt(v + eps)

def _scatter_add(tgt, idx, src, axis=0):
    return tgt.at[idx].add(src)

def _segment_sum(src, seg, n):
    return jax.ops.segment_sum(src, seg, n)
kernel_name = 'mk_lm_tower_d2_tok_ids1024_r4_3ff071'

def setup_inputs(seed: int=0):
    np.random.seed(seed)
    _w = jnp.asarray

    def _rec_inputs():
        import jax
        import jax.numpy as jnp
        _rk = jax.random.key(seed)
        x = jax.random.randint(jax.random.fold_in(_rk, 1), (16, 256), 0, 267694, jnp.int32)
        return x
    x = _rec_inputs()

    def _L0_tok_setup():
        import jax, jax.numpy as jnp
        import numpy as np
        CUTOFF_ENDS = [0, 5000, 10000, 50000, 267735]
        D_PROJ = 256
        EMB_SCALE = float(D_PROJ) ** 0.5
        key = jax.random.key(seed)
        ks = jax.random.split(key, 10)
        d_embs = [256, 64, 64, 16]
        sizes = [CUTOFF_ENDS[i + 1] - CUTOFF_ENDS[i] for i in range(4)]
        inp = jax.random.randint(ks[0], (8, 512), 0, CUTOFF_ENDS[-1], dtype=jnp.int64)
        out = {'inp': inp}
        for i in range(4):
            out[f'emb_{i}'] = jax.random.normal(ks[1 + i], (sizes[i], d_embs[i]), dtype=jnp.float32)
            out[f'proj_{i}'] = jax.random.normal(ks[5 + i], (D_PROJ, d_embs[i]), dtype=jnp.float32) * 0.02
        return out
    _L0_tok_all = _L0_tok_setup()
    _L0_tok_in = {k: v for k, v in _L0_tok_all.items() if k in ('emb_0', 'emb_1', 'emb_2', 'emb_3', 'proj_0', 'proj_1', 'proj_2', 'proj_3')}
    del _L0_tok_all

    def _L0_attn_setup():
        import jax, jax.numpy as jnp
        import numpy as np
        from math import sqrt
        D_MODEL = 256
        B, T = (4, 1024)
        key = jax.random.key(seed)
        kx, kqk, kvo = jax.random.split(key, 3)
        x = jax.random.normal(kx, (B, T, D_MODEL), dtype=jnp.float32)
        limit = sqrt(6.0 / (2 * D_MODEL))
        QK = jax.random.uniform(kqk, (D_MODEL, D_MODEL), minval=-limit, maxval=limit, dtype=jnp.float32)
        VO = jax.random.uniform(kvo, (D_MODEL, D_MODEL), minval=-limit, maxval=limit, dtype=jnp.float32)
        return {'x': x, 'QK': QK, 'VO': VO}
    _L0_attn_all = _L0_attn_setup()
    _L0_attn_in = {k: v for k, v in _L0_attn_all.items() if k in ('QK', 'VO')}
    del _L0_attn_all

    def _L0_ffn_setup():
        import jax, jax.numpy as jnp
        import numpy as np
        E = 8
        K = 2
        CAP_FACTOR = 1.0
        key = jax.random.key(seed)
        ks = jax.random.split(key, 5)
        B, T, C, H = (4, 512, 256, 1024)
        x = jax.random.normal(ks[0], (B, T, C), dtype=jnp.float32)
        Wr = jax.random.normal(ks[1], (C, E), dtype=jnp.float32) * 0.02
        br = jnp.zeros((E,), jnp.float32)
        W1 = jax.random.normal(ks[2], (E, C, H), dtype=jnp.float32) * 0.02
        b1 = jnp.zeros((E, H), jnp.float32)
        W2 = jax.random.normal(ks[3], (E, H, C), dtype=jnp.float32) * 0.02
        b2 = jnp.zeros((E, C), jnp.float32)
        return {'x': x, 'Wr': Wr, 'br': br, 'W1': W1, 'b1': b1, 'W2': W2, 'b2': b2}
    _L0_ffn_all = _L0_ffn_setup()
    _L0_ffn_in = {k: v for k, v in _L0_ffn_all.items() if k in ('Wr', 'br', 'W1', 'b1', 'W2', 'b2')}
    del _L0_ffn_all

    def _L1_attn_setup():
        import jax, jax.numpy as jnp
        import numpy as np
        import math
        EMBED_DIM = 256
        N_HEADS = 16
        HEAD_DIM = EMBED_DIM // N_HEADS
        NUM_FEATURES = 32
        R_NODES = 2
        EPS = 1e-06
        C_CONST = 2.0 + EPS
        CHUNK = 128

        def _compute_features(z, omega, quad_nodes, quad_weights):
            R, M = (omega.shape[0], omega.shape[-1])
            nrm = jnp.linalg.norm(z, axis=-1, keepdims=True)
            zn = z / jnp.maximum(nrm, 1e-12)
            proj = jnp.einsum('bhtd,rhdm->rbhtm', zn, omega)
            inv_sqrt_m = 1.0 / math.sqrt(M)
            poly = proj ** 2 * inv_sqrt_m
            s = quad_nodes.reshape(R, 1, 1, 1, 1)
            sqrt_2s = jnp.sqrt(2.0 * jnp.maximum(quad_nodes, 0.0)).reshape(R, 1, 1, 1, 1)
            exp_arg = jnp.clip(proj * sqrt_2s - s, -20.0, 20.0)
            prf = jnp.exp(exp_arg) * inv_sqrt_m
            sqw = jnp.sqrt(jnp.maximum(quad_weights, 0.0)).reshape(R, 1, 1, 1, 1)
            fused = poly * prf * sqw
            B, H, T = (z.shape[0], z.shape[1], z.shape[2])
            return jnp.transpose(fused, (1, 2, 3, 0, 4)).reshape(B, H, T, R * M)

        def _forward(x, w_qkv, b_qkv, w_out, b_out, omega, quad_nodes, quad_weights):
            B, T, C = x.shape
            H, D = (N_HEADS, HEAD_DIM)
            qkv = x @ w_qkv.T + b_qkv
            q, k, v = jnp.split(qkv, 3, axis=-1)

            def to_bhtd(t):
                return jnp.transpose(t.reshape(B, T, H, D), (0, 2, 1, 3)).astype(jnp.float32)
            q, k, v = (to_bhtd(q), to_bhtd(k), to_bhtd(v))
            qf = _compute_features(q, omega, quad_nodes, quad_weights)
            kf = _compute_features(k, omega, quad_nodes, quad_weights)
            F_dim = qf.shape[-1]
            nc = T // CHUNK

            def to_chunks(t):
                new_shape = (t.shape[0], t.shape[1], nc, CHUNK) + t.shape[3:]
                return jnp.moveaxis(t.reshape(new_shape), 2, 0)
            qf_c, kf_c, v_c = (to_chunks(qf), to_chunks(kf), to_chunks(v))
            kv0 = jnp.zeros((B, H, F_dim, D), dtype=jnp.float32)
            k0 = jnp.zeros((B, H, F_dim), dtype=jnp.float32)

            def step(carry, inp):
                kv_s, k_s = carry
                qc, kc, vc = inp
                kv_prod = jnp.einsum('bhtf,bhtd->bhtfd', kc, vc)
                kv_cum = jnp.cumsum(kv_prod, axis=2) + kv_s[:, :, None]
                k_cum = jnp.cumsum(kc, axis=2) + k_s[:, :, None]
                ctx = jnp.einsum('bhtf,bhtfd->bhtd', qc, kv_cum)
                den = jnp.maximum(jnp.einsum('bhtf,bhtf->bht', qc, k_cum), 1e-06)
                out_c = ctx / den[..., None]
                return ((kv_cum[:, :, -1], k_cum[:, :, -1]), out_c)
            _, out_chunks = jax.lax.scan(step, (kv0, k0), (qf_c, kf_c, v_c))
            out = jnp.moveaxis(out_chunks, 0, 2).reshape(B, H, T, D)
            out = jnp.transpose(out, (0, 2, 1, 3)).reshape(B, T, C)
            return out @ w_out.T + b_out
        key = jax.random.key(seed)
        ks = jax.random.split(key, 8)
        B, T = (2, 1024)
        x = jax.random.normal(ks[0], (B, T, EMBED_DIM), dtype=jnp.float32)
        w_qkv = jax.random.normal(ks[1], (3 * EMBED_DIM, EMBED_DIM), dtype=jnp.float32) * 0.02
        b_qkv = jnp.zeros((3 * EMBED_DIM,), dtype=jnp.float32)
        w_out = jax.random.normal(ks[2], (EMBED_DIM, EMBED_DIM), dtype=jnp.float32) * 0.02
        b_out = jnp.zeros((EMBED_DIM,), dtype=jnp.float32)
        omega = jax.random.normal(ks[3], (R_NODES, N_HEADS, HEAD_DIM, NUM_FEATURES), dtype=jnp.float32)
        nodes, weights = np.polynomial.laguerre.laggauss(R_NODES)
        quad_nodes = jnp.asarray(nodes, dtype=jnp.float32) / C_CONST
        quad_weights = jnp.asarray(weights, dtype=jnp.float32) / C_CONST
        return {'x': x, 'w_qkv': w_qkv, 'b_qkv': b_qkv, 'w_out': w_out, 'b_out': b_out, 'omega': omega, 'quad_nodes': quad_nodes, 'quad_weights': quad_weights}
    _L1_attn_all = _L1_attn_setup()
    _L1_attn_in = {k: v for k, v in _L1_attn_all.items() if k in ('w_qkv', 'b_qkv', 'w_out', 'b_out', 'omega', 'quad_nodes', 'quad_weights')}
    del _L1_attn_all

    def _L1_ffn_setup():
        import jax, jax.numpy as jnp
        import numpy as np
        D = 256
        H = 512
        E = 8
        B, T = (4, 512)
        LN_EPS = 1e-05
        key = jax.random.key(seed)
        k = jax.random.split(key, 6)
        std = 0.02
        return {'x': jax.random.normal(k[0], (B, T, D), dtype=jnp.float32), 'gate_w': jax.random.normal(k[1], (E, D), dtype=jnp.float32) * std, 'expert_w1': jax.random.normal(k[2], (E, D, H), dtype=jnp.float32) * std, 'expert_w2': jax.random.normal(k[3], (E, H, D), dtype=jnp.float32) * std, 'ln_gamma': jnp.ones((D,), dtype=jnp.float32), 'ln_beta': jnp.zeros((D,), dtype=jnp.float32)}
    _L1_ffn_all = _L1_ffn_setup()
    _L1_ffn_in = {k: v for k, v in _L1_ffn_all.items() if k in ('gate_w', 'expert_w1', 'expert_w2', 'ln_gamma', 'ln_beta')}
    del _L1_ffn_all
    return {'x': x, 'L0_tok_emb_0': _L0_tok_in['emb_0'], 'L0_tok_emb_1': _L0_tok_in['emb_1'], 'L0_tok_emb_2': _L0_tok_in['emb_2'], 'L0_tok_emb_3': _L0_tok_in['emb_3'], 'L0_tok_proj_0': _L0_tok_in['proj_0'], 'L0_tok_proj_1': _L0_tok_in['proj_1'], 'L0_tok_proj_2': _L0_tok_in['proj_2'], 'L0_tok_proj_3': _L0_tok_in['proj_3'], 'L0_attn_QK': _L0_attn_in['QK'], 'L0_attn_VO': _L0_attn_in['VO'], 'L0_ffn_Wr': _L0_ffn_in['Wr'], 'L0_ffn_br': _L0_ffn_in['br'], 'L0_ffn_W1': _L0_ffn_in['W1'], 'L0_ffn_b1': _L0_ffn_in['b1'], 'L0_ffn_W2': _L0_ffn_in['W2'], 'L0_ffn_b2': _L0_ffn_in['b2'], 'L1_attn_w_qkv': _L1_attn_in['w_qkv'], 'L1_attn_b_qkv': _L1_attn_in['b_qkv'], 'L1_attn_w_out': _L1_attn_in['w_out'], 'L1_attn_b_out': _L1_attn_in['b_out'], 'L1_attn_omega': _L1_attn_in['omega'], 'L1_attn_quad_nodes': _L1_attn_in['quad_nodes'], 'L1_attn_quad_weights': _L1_attn_in['quad_weights'], 'L1_ffn_gate_w': _L1_ffn_in['gate_w'], 'L1_ffn_expert_w1': _L1_ffn_in['expert_w1'], 'L1_ffn_expert_w2': _L1_ffn_in['expert_w2'], 'L1_ffn_ln_gamma': _L1_ffn_in['ln_gamma'], 'L1_ffn_ln_beta': _L1_ffn_in['ln_beta']}

def reference(x, L0_tok_emb_0, L0_tok_emb_1, L0_tok_emb_2, L0_tok_emb_3, L0_tok_proj_0, L0_tok_proj_1, L0_tok_proj_2, L0_tok_proj_3, L0_attn_QK, L0_attn_VO, L0_ffn_Wr, L0_ffn_br, L0_ffn_W1, L0_ffn_b1, L0_ffn_W2, L0_ffn_b2, L1_attn_w_qkv, L1_attn_b_qkv, L1_attn_w_out, L1_attn_b_out, L1_attn_omega, L1_attn_quad_nodes, L1_attn_quad_weights, L1_ffn_gate_w, L1_ffn_expert_w1, L1_ffn_expert_w2, L1_ffn_ln_gamma, L1_ffn_ln_beta):
    import jax
    import jax.numpy as jnp

    def _L0_tok_ref(inp, emb_0, emb_1, emb_2, emb_3, proj_0, proj_1, proj_2, proj_3):
        import jax, jax.numpy as jnp
        import numpy as np
        CUTOFF_ENDS = [0, 5000, 10000, 50000, 267735]
        D_PROJ = 256
        EMB_SCALE = float(D_PROJ) ** 0.5
        embs = [emb_0, emb_1, emb_2, emb_3]
        projs = [proj_0, proj_1, proj_2, proj_3]
        flat = inp.reshape(-1)
        out = jnp.zeros((flat.shape[0], D_PROJ), jnp.float32)
        for i in range(4):
            l, r = (CUTOFF_ENDS[i], CUTOFF_ENDS[i + 1])
            mask = (flat >= l) & (flat < r)
            idx = jnp.clip(flat - l, 0, r - l - 1)
            e = jnp.einsum('nd,pd->np', embs[i][idx], projs[i])
            out = jnp.where(mask[:, None], e, out)
        out = out * EMB_SCALE
        return out.reshape(*inp.shape, D_PROJ)

    def _L0_attn_ref(x, QK, VO):
        import jax, jax.numpy as jnp
        import numpy as np
        from math import sqrt
        D_MODEL = 256
        B, T = (4, 1024)
        d_model = QK.shape[0]
        xQK = jnp.einsum('btd,de->bte', x, QK)
        scores = jnp.einsum('bte,bue->btu', xQK, x) / sqrt(d_model)
        attn = jax.nn.softmax(scores, axis=2)
        av = jnp.einsum('btu,bud->btd', attn, x)
        return jnp.einsum('btd,de->bte', av, VO)

    def _L0_ffn_ref(x, Wr, br, W1, b1, W2, b2):
        import jax, jax.numpy as jnp
        import numpy as np
        E = 8
        K = 2
        CAP_FACTOR = 1.0
        B, T, C = x.shape
        N = B * T
        xf = x.reshape(N, C)
        logits = xf @ Wr + br
        topv, topi = jax.lax.top_k(logits, K)
        gates = jax.nn.softmax(topv, axis=-1)
        rw = jnp.zeros((N, E), xf.dtype).at[jnp.arange(N)[:, None], topi].set(gates)
        cap = int(N * K / E * CAP_FACTOR)
        sel = jax.nn.one_hot(topi, E, dtype=jnp.int32).sum(1)
        rank = jnp.cumsum(sel, axis=0) - sel
        keep = (sel > 0) & (rank < cap)
        tok = jnp.broadcast_to(jnp.arange(N, dtype=jnp.int32)[:, None], (N, E))
        eid = jnp.broadcast_to(jnp.arange(E, dtype=jnp.int32)[None, :], (N, E))
        rank_c = jnp.where(keep, rank, cap)
        buf = jnp.full((E, cap), N, dtype=jnp.int32)
        buf = buf.at[eid, rank_c].set(tok, mode='drop')
        xpad = jnp.concatenate([xf, jnp.zeros((1, C), xf.dtype)], axis=0)
        xg = xpad[buf]
        h = jax.nn.gelu(jnp.einsum('ecd,edh->ech', xg, W1) + b1[:, None, :], approximate=False)
        out = jnp.einsum('ech,ehd->ecd', h, W2) + b2[:, None, :]
        rw_pad = jnp.concatenate([rw, jnp.zeros((1, E), rw.dtype)], axis=0)
        w = rw_pad[buf, jnp.arange(E, dtype=jnp.int32)[:, None]]
        weighted = out * w[..., None]
        final = jnp.zeros((N + 1, C), xf.dtype).at[buf.reshape(-1)].add(weighted.reshape(-1, C))
        return final[:N].reshape(B, T, C)

    def _L1_attn_ref(x, w_qkv, b_qkv, w_out, b_out, omega, quad_nodes, quad_weights):
        import jax, jax.numpy as jnp
        import numpy as np
        import math
        EMBED_DIM = 256
        N_HEADS = 16
        HEAD_DIM = EMBED_DIM // N_HEADS
        NUM_FEATURES = 32
        R_NODES = 2
        EPS = 1e-06
        C_CONST = 2.0 + EPS
        CHUNK = 128

        def _compute_features(z, omega, quad_nodes, quad_weights):
            R, M = (omega.shape[0], omega.shape[-1])
            nrm = jnp.linalg.norm(z, axis=-1, keepdims=True)
            zn = z / jnp.maximum(nrm, 1e-12)
            proj = jnp.einsum('bhtd,rhdm->rbhtm', zn, omega)
            inv_sqrt_m = 1.0 / math.sqrt(M)
            poly = proj ** 2 * inv_sqrt_m
            s = quad_nodes.reshape(R, 1, 1, 1, 1)
            sqrt_2s = jnp.sqrt(2.0 * jnp.maximum(quad_nodes, 0.0)).reshape(R, 1, 1, 1, 1)
            exp_arg = jnp.clip(proj * sqrt_2s - s, -20.0, 20.0)
            prf = jnp.exp(exp_arg) * inv_sqrt_m
            sqw = jnp.sqrt(jnp.maximum(quad_weights, 0.0)).reshape(R, 1, 1, 1, 1)
            fused = poly * prf * sqw
            B, H, T = (z.shape[0], z.shape[1], z.shape[2])
            return jnp.transpose(fused, (1, 2, 3, 0, 4)).reshape(B, H, T, R * M)

        def _forward(x, w_qkv, b_qkv, w_out, b_out, omega, quad_nodes, quad_weights):
            B, T, C = x.shape
            H, D = (N_HEADS, HEAD_DIM)
            qkv = x @ w_qkv.T + b_qkv
            q, k, v = jnp.split(qkv, 3, axis=-1)

            def to_bhtd(t):
                return jnp.transpose(t.reshape(B, T, H, D), (0, 2, 1, 3)).astype(jnp.float32)
            q, k, v = (to_bhtd(q), to_bhtd(k), to_bhtd(v))
            qf = _compute_features(q, omega, quad_nodes, quad_weights)
            kf = _compute_features(k, omega, quad_nodes, quad_weights)
            F_dim = qf.shape[-1]
            nc = T // CHUNK

            def to_chunks(t):
                new_shape = (t.shape[0], t.shape[1], nc, CHUNK) + t.shape[3:]
                return jnp.moveaxis(t.reshape(new_shape), 2, 0)
            qf_c, kf_c, v_c = (to_chunks(qf), to_chunks(kf), to_chunks(v))
            kv0 = jnp.zeros((B, H, F_dim, D), dtype=jnp.float32)
            k0 = jnp.zeros((B, H, F_dim), dtype=jnp.float32)

            def step(carry, inp):
                kv_s, k_s = carry
                qc, kc, vc = inp
                kv_prod = jnp.einsum('bhtf,bhtd->bhtfd', kc, vc)
                kv_cum = jnp.cumsum(kv_prod, axis=2) + kv_s[:, :, None]
                k_cum = jnp.cumsum(kc, axis=2) + k_s[:, :, None]
                ctx = jnp.einsum('bhtf,bhtfd->bhtd', qc, kv_cum)
                den = jnp.maximum(jnp.einsum('bhtf,bhtf->bht', qc, k_cum), 1e-06)
                out_c = ctx / den[..., None]
                return ((kv_cum[:, :, -1], k_cum[:, :, -1]), out_c)
            _, out_chunks = jax.lax.scan(step, (kv0, k0), (qf_c, kf_c, v_c))
            out = jnp.moveaxis(out_chunks, 0, 2).reshape(B, H, T, D)
            out = jnp.transpose(out, (0, 2, 1, 3)).reshape(B, T, C)
            return out @ w_out.T + b_out
        return _forward(x, w_qkv, b_qkv, w_out, b_out, omega, quad_nodes, quad_weights)

    def _L1_ffn_ref(x, gate_w, expert_w1, expert_w2, ln_gamma, ln_beta):
        import jax, jax.numpy as jnp
        import numpy as np
        D = 256
        H = 512
        E = 8
        B, T = (4, 512)
        LN_EPS = 1e-05
        Bb, Tt, Dd = x.shape
        x_flat = x.reshape(Bb * Tt, Dd)
        gate_logits = x_flat @ gate_w.T
        gate_probs = jax.nn.softmax(gate_logits, axis=-1)
        top_val = jnp.max(gate_probs, axis=-1)
        top_idx = jnp.argmax(gate_probs, axis=-1)
        top_val = top_val / (top_val + 1e-08)
        onehot = jax.nn.one_hot(top_idx, expert_w1.shape[0], dtype=x.dtype)
        xe = jnp.einsum('ne,nd->end', onehot, x_flat)
        he = jax.nn.gelu(jnp.einsum('end,edh->enh', xe, expert_w1), approximate=False)
        ye = jnp.einsum('enh,ehd->end', he, expert_w2)
        out_flat = jnp.einsum('end,ne->nd', ye, onehot) * top_val[:, None]
        out = out_flat.reshape(Bb, Tt, Dd)
        mu = jnp.mean(out, axis=-1, keepdims=True)
        var = jnp.mean((out - mu) ** 2, axis=-1, keepdims=True)
        out = (out - mu) * jax.lax.rsqrt(var + LN_EPS) * ln_gamma + ln_beta
        return out
    h = _L0_tok_ref(x, L0_tok_emb_0, L0_tok_emb_1, L0_tok_emb_2, L0_tok_emb_3, L0_tok_proj_0, L0_tok_proj_1, L0_tok_proj_2, L0_tok_proj_3)
    h = h + _L0_attn_ref(_layernorm(h, axis=-1), L0_attn_QK, L0_attn_VO)
    h = h + _L0_ffn_ref(_layernorm(h, axis=-1), L0_ffn_Wr, L0_ffn_br, L0_ffn_W1, L0_ffn_b1, L0_ffn_W2, L0_ffn_b2)
    h = h + _L1_attn_ref(_layernorm(h, axis=-1), L1_attn_w_qkv, L1_attn_b_qkv, L1_attn_w_out, L1_attn_b_out, L1_attn_omega, L1_attn_quad_nodes, L1_attn_quad_weights)
    h = h + _L1_ffn_ref(_layernorm(h, axis=-1), L1_ffn_gate_w, L1_ffn_expert_w1, L1_ffn_expert_w2, L1_ffn_ln_gamma, L1_ffn_ln_beta)
    return h

_drawn_inputs = setup_inputs


def setup_inputs(seed=0):
    import zlib

    import numpy as np

    out = dict(_drawn_inputs(seed))
    spreads = {'L0_ffn_br': (0.0, 0.1),
     'L0_ffn_b1': (0.0, 0.1),
     'L0_ffn_b2': (0.0, 0.1),
     'L1_attn_b_qkv': (0.0, 0.1),
     'L1_attn_b_out': (0.0, 0.1),
     'L1_ffn_ln_gamma': (1.0, 0.2),
     'L1_ffn_ln_beta': (0.0, 0.1)}
    factors = {}
    for name, (base, spread) in spreads.items():
        noise = np.random.default_rng([zlib.crc32(name.encode()), seed]).standard_normal(out[name].shape)
        drawn = base * np.exp(spread * noise) if base else spread * noise
        out[name] = jnp.asarray(drawn.astype(out[name].dtype))
    for name, factor in factors.items():
        out[name] = (out[name] * factor).astype(out[name].dtype)
    return out
```

```python
from contextlib import ExitStack

import concourse.bass as bass
from concourse import mybir

F32 = mybir.dt.float32
I32 = mybir.dt.int32
U32 = mybir.dt.uint32
ALU = mybir.AluOpType
ACT = mybir.ActivationFunctionType
AX = mybir.AxisListType

P = 128
B, T, D = 16, 256, 256
PAIRS = B // 2
TT = T // P
N = B * T
TILES = N // P
DC = D // P
CUTS = [0, 5000, 10000, 50000, 267735]
EMB_D = [256, 64, 64, 16]
EMB_AT = [0, 256, 320, 384]
CAT = 512
KC = CAT // P
NOWHERE = 1 << 20
EXP = 8
HID0, CAP = 1024, N * 2 // EXP
HID1 = 512
HEADS, HD, FEAT = 16, 16, 32
NF = 2 * FEAT
REGION = N + P
MOE1_FLIGHT = 4
MOE1_TILES = -(-((N + EXP * (P - 1)) // P) // MOE1_FLIGHT) * MOE1_FLIGHT
LN_EPS = 1e-5
ATT_SCALE = 1.0 / D ** 0.5
EMB_SCALE = float(D) ** 0.5
RSQRT_MAGIC = 0x5F3759DF
EXP_LO, EXP_HI = 2.061153622438558e-09, 485165195.4097903
FRONT_STEPS, MIDDLE_STEPS, BACK_STEPS = 114, 142, 36


def turn(j, p):
    return 2 * j + p + 1


def wait_apart(eng, passed, sem, value):
    eng.wait_ge(sem, value)
    eng.sem_inc(passed, 1)


class Steps:

    def __init__(self, eng, sem, passed):
        self.eng, self.sem, self.passed, self.base, self.n = eng, sem, passed, 0, 0

    def begin(self, base):
        self.base, self.n = base, 0

    def __call__(self, ins):
        ins.then_inc(self.sem, 1)
        self.n += 1

    def wait(self):
        self.eng.wait_ge(self.sem, self.base + self.n)

    def wait_apart(self):
        wait_apart(self.eng, self.passed, self.sem, self.base + self.n)

    def run(self, ins):
        self(ins)
        self.wait()


class Chip:
    pass


def rsqrt(dve, step, out, val, tmp):
    step.run(dve.tensor_scalar(out.bitcast(I32), val.bitcast(I32), 1, None, ALU.logical_shift_right))
    step.run(dve.tensor_scalar(out.bitcast(I32), out.bitcast(I32), -1.0, float(RSQRT_MAGIC), ALU.mult, ALU.add))
    for _ in range(3):
        step.run(dve.scalar_tensor_tensor(tmp, out, -0.5, out, ALU.mult, ALU.mult))
        step.run(dve.tensor_tensor(tmp, tmp, val, ALU.mult))
        step.run(dve.scalar_tensor_tensor(out, tmp, 1.5, out, ALU.add, ALU.mult))


def layer_norm(dve, step, out, x, w, last=None):
    for t in range(TT):
        step(dve.bn_stats(w.stats[:, t, :], x[:, t, :]))
    step.wait_apart()
    for t in range(TT):
        step(dve.bn_aggr(w.mv[:, t, :], w.stats[:, t, :]))
    step.wait()
    step.run(dve.tensor_scalar(w.var[:], w.mv[:, :, 1], LN_EPS, None, ALU.add))
    rsqrt(dve, step, w.rstd[:], w.var[:], w.tmp[:])
    for t in range(TT):
        ins = dve.tensor_scalar(out[:, t, :], x[:, t, :], w.mv[:, t, 0:1], w.rstd[:, t:t + 1],
                                ALU.subtract, ALU.mult)
        if last is not None and t == TT - 1:
            ins.then_inc(last, 1)
        else:
            step(ins)


class Norm:

    def __init__(self, sb, name):
        self.stats = sb(f"{name}_stats", [P, TT, 6])
        self.mv = sb(f"{name}_mv", [P, TT, 2])
        self.var = sb(f"{name}_var", [P, TT])
        self.rstd = sb(f"{name}_rstd", [P, TT])
        self.tmp = sb(f"{name}_tmp", [P, TT])


def scope(nc, ctx, prefix):
    def sb(name, shape, dt=F32):
        return ctx.enter_context(nc.sbuf_tensor(f"{prefix}_{name}", shape, dt))

    def sem(name):
        return ctx.enter_context(nc.semaphore(f"{prefix}_{name}"))

    return sb, sem


def rows(ap):
    n = ap.shape[0]
    return ap.rearrange("(a n) -> a n", a=1).to_broadcast([P, n])


def setup(nc, c, a):
    with ExitStack() as ctx:
        sb, sem = scope(nc, ctx, "set")
        ids = sb("ids", [TILES, P], I32)
        ids_f = sb("ids_f", [TILES, P])
        idt = sb("idt", [P, TILES])
        sel = sb("sel", [P, 2, TILES])
        proj = sb("proj", [P, DC, CAT])
        wqkv = sb("wqkv", [P, 6, D])
        wout = sb("wout", [P, DC, D])
        gate = sb("gate", [EXP, D])
        b1 = sb("b1", [EXP * HID0 // P, P])
        zeros = sb("zeros", [P, 2048])
        ld = sem("loaded")
        loads = 0
        z = sem("zeroed")
        consts = sem("consts")
        turned = sem("turned")
        moved = sem("moved")
        direct = sem("direct")
        own = sem("own")
        om_zero = sem("om_zero")
        om_ld = sem("om_loaded")
        zero_rows = sem("zero_rows")

        jobs = [(c.projT[:, k, DC0 * P:(DC0 + 1) * P], proj[:, DC0, k * P:(k + 1) * P])
                for DC0 in range(DC) for k in range(KC)]
        jobs += [(c.wqkvT[:, k, m * P:(m + 1) * P], wqkv[:, m, k * P:(k + 1) * P])
                 for m in range(6) for k in range(DC)]
        jobs += [(c.woutT[:, k, m * P:(m + 1) * P], wout[:, m, k * P:(k + 1) * P])
                 for m in range(DC) for k in range(DC)]
        jobs += [(c.gateT[:, k, :], gate[:, k * P:(k + 1) * P]) for k in range(DC)]
        jobs += [(c.b1T[:], b1[:])]
        LOADS = 4 + 1 + 1 + 1 + 1 + 1
        block = ctx.enter_context(nc.Block())

        @block.sync
        def _(sp):
            sp.dma_start(ids[:], a.x.rearrange("b (u p) -> (b u) p", p=P)).then_inc(ld, 16)
            sp.wait_ge(z, 1)
            for i in range(4):
                sp.dma_start(proj[:, :, EMB_AT[i]:EMB_AT[i] + EMB_D[i]],
                             a.proj[i].rearrange("(u p) d -> p u d", p=P)).then_inc(ld, 16)
            sp.dma_start(wqkv[:], a.w_qkv.rearrange("(u p) d -> p u d", p=P)).then_inc(ld, 16)
            sp.dma_start(wout[:], a.w_out.rearrange("(u p) d -> p u d", p=P)).then_inc(ld, 16)
            sp.dma_start(gate[:], a.gate_w).then_inc(ld, 16)
            sp.dma_start(b1[:], a.b1.rearrange("e (m p) -> (e m) p", p=P)).then_inc(ld, 16)
            sp.dma_start(c.QK[:], a.QK.rearrange("(k p) n -> p k n", p=P)).then_inc(direct, 16)
            sp.dma_start(c.VO[:], a.VO.rearrange("(k p) n -> p k n", p=P)).then_inc(direct, 16)
            sp.dma_start(c.Wr[:], a.Wr.rearrange("(k p) n -> p k n", p=P)).then_inc(direct, 16)
            for buf, src in ((c.br, a.br), (c.bqkv, a.b_qkv), (c.bout, a.b_out), (c.gamma, a.gamma),
                             (c.beta, a.beta), (c.nodes, a.nodes), (c.qw, a.qw)):
                sp.dma_start(buf[:], rows(src)).then_inc(direct, 16)
            sp.wait_ge(zero_rows, 1)
            per = 2048 // D * P
            for i in range(EXP * CAP // per):
                sp.dma_start(a.xg0[i * per:(i + 1) * per, :].rearrange("(p r) d -> p (r d)", p=P),
                             zeros[:]).then_inc(direct, 16)
            sp.dma_start(a.y0[EXP * CAP:EXP * CAP + 1, :], zeros[0:1, 0:D]).then_inc(direct, 16)
            sp.dma_start(a.xg1[EXP * REGION:EXP * REGION + P, :], zeros[:, 0:D]).then_inc(direct, 16)
            sp.wait_ge(om_zero, 1)
            for h in range(HEADS):
                r0 = HD * (h % 8)
                hh = h % 2
                sp.dma_start(c.omega[r0:r0 + HD, h // 8, hh * NF:(hh + 1) * NF].rearrange(
                    "d (r m) -> d r m", r=2), a.omega[:, h].rearrange("r d m -> d r m")).then_inc(om_ld, 16)
            sp.wait_ge(om_ld, 16 * HEADS)
            sp.wait_ge(direct, 16 * (10 + EXP * CAP // per + 2))

        @block.gpsimd
        def _(pool):
            pool.memset(proj[:], 0.0).then_inc(z, 1)
            pool.memset(c.omega[:], 0.0).then_inc(om_zero, 1)
            pool.memset(c.cat[0][:], 0.0)
            pool.memset(c.cat[1][:], 0.0)
            pool.memset(c.ident[:], 0.0).then_inc(own, 1)
            pool.memset(c.ones[:], 1.0).then_inc(own, 1)
            pool.iota(c.iota8[:], [[1, EXP]], base=0, channel_multiplier=0,
                      allow_small_or_imprecise_dtypes=True).then_inc(own, 1)
            pool.iota(c.tile_no[:], [[1, MOE1_TILES]], base=0, channel_multiplier=0,
                      allow_small_or_imprecise_dtypes=True).then_inc(own, 1)
            pool.wait_ge(own, 4)
            pool.affine_select(out=c.ident[:], in_=c.ident[:], compare_op=ALU.not_equal, fill=1.0, base=0,
                               pattern=[[-1, P]], channel_multiplier=1).then_inc(consts, 1)
            pool.affine_select(out=c.before[:], in_=c.ones[:], compare_op=ALU.is_gt, fill=0.0, base=0,
                               pattern=[[1, P]], channel_multiplier=-1).then_inc(own, 1)
            for b in (0, 2):
                pool.affine_select(out=c.causal[:, b, :], in_=c.ones[:], compare_op=ALU.is_ge, fill=0.0, base=0,
                                   pattern=[[1, P]], channel_multiplier=-1)
            pool.tensor_copy(c.causal[:, 1, :], c.ones[:]).then_inc(own, 1)
            pool.wait_ge(own, 6)

        @block.tensor
        def _(pe):
            pe.wait_ge(consts, 1)
            pe.wait_ge(own, 7)
            pe.transpose(c.bank[7][:, 0:TILES], ids_f[:], c.ident[0:TILES, 0:TILES]).then_inc(turned, 1)
            pe.wait_ge(ld, 16 * LOADS)
            for n in range(0, len(jobs), 4):
                if n >= 28:
                    pe.wait_ge(moved, n - 24)
                for k, (dst, src) in enumerate(jobs[n:n + 4]):
                    m = src.shape[0]
                    ins = pe.transpose(c.bank[n // 4 % 7][:, k * P:k * P + m], src, c.ident[0:m, 0:m])
                ins.then_inc(turned, 1)

        @block.vector
        def _(dve):
            step = Steps(dve, sem("dve"), c.passed)
            dve.memset(zeros[:], 0.0).then_inc(zero_rows, 1)
            step(dve.memset(c.zero[:], 0.0))
            step(dve.memset(c.base0[:], 0.0))
            step(dve.memset(c.base1[:], 0.0))
            for q in range(2):
                step(dve.memset(c.vone[q][:], 1.0))
            dve.wait_ge(ld, 16 * LOADS)
            dve.wait_ge(own, 6)
            dve.tensor_copy(ids_f[:], ids[:]).then_inc(own, 1)
            dve.wait_ge(turned, 1)
            step.run(dve.tensor_copy(idt[:], c.bank[7][:, 0:TILES]))
            for i in range(4):
                lo, hi = float(CUTS[i]), float(CUTS[i + 1])
                step.run(dve.tensor_scalar(sel[:, 0, :], idt[:], lo, None, ALU.is_ge))
                step.run(dve.tensor_scalar(sel[:, 1, :], idt[:], hi, None, ALU.is_lt))
                step.run(dve.tensor_tensor(sel[:, 0, :], sel[:, 0, :], sel[:, 1, :], ALU.mult))
                step.run(dve.tensor_scalar(sel[:, 1, :], idt[:], -(lo + NOWHERE), None, ALU.add))
                step.run(dve.tensor_tensor(sel[:, 0, :], sel[:, 0, :], sel[:, 1, :], ALU.mult))
                step.run(dve.tensor_scalar(c.token_row[:, i, 0:TILES], sel[:, 0, :], float(NOWHERE), None, ALU.add))
            for n in range(0, len(jobs), 4):
                dve.wait_ge(turned, n // 4 + 2)
                for k, (dst, src) in enumerate(jobs[n:n + 4]):
                    m = src.shape[0]
                    dve.tensor_copy(dst, c.bank[n // 4 % 7][:, k * P:k * P + m]).then_inc(moved, 1)
            dve.wait_ge(direct, 16 * (10 + EXP * CAP * D // (2048 * P) + 2))
            clip = sb("clip", [P, 2])
            root = sb("root", [P, 2])
            tmp = sb("root_tmp", [P, 2])
            big = sb("root_big", [P, 2])
            for src, scale, dst in ((c.nodes, 2.0, c.f_scale), (c.qw, 1.0, c.f_weight)):
                step.run(dve.tensor_scalar(clip[:], src[:], 0.0, scale, ALU.max, ALU.mult))
                step.run(dve.tensor_scalar(big[:], clip[:], 1e-30, None, ALU.max))
                rsqrt(dve, step, root[:], big[:], tmp[:])
                step.run(dve.tensor_tensor(root[:], root[:], clip[:], ALU.mult))
                f = 1.0 if dst is c.f_scale else 1.0 / FEAT
                for g in range(4):
                    step.run(dve.tensor_scalar(dst[g * 32:(g + 1) * 32, :], root[g * 32:(g + 1) * 32, g % 2:g % 2 + 1],
                                               f, None, ALU.mult))
            for g in range(4):
                step.run(dve.tensor_scalar(c.f_shift[g * 32:(g + 1) * 32, :],
                                           c.nodes[g * 32:(g + 1) * 32, g % 2:g % 2 + 1], -1.0, None, ALU.mult))


def route(dve, step, w, p, logits, K):
    step.wait_apart()
    for t in range(TT):
        step(dve.max(w.best[p][:, t, :], logits[:, t, :]))
    step.wait_apart()
    for t in range(TT):
        step(dve.max_index(w.best_at[p][:, t, :], w.best[p][:, t, :], logits[:, t, :]))
    step.wait()
    step.run(dve.tensor_copy(w.expert[p][:], w.best_at[p][:, :, 0:K].rearrange("p t k -> p k t")))


def places(nc, dve, step, w, p, c, K, base, psum, stride, limit, dump, done):
    KT = K * TT
    step.run(dve.tensor_tensor(w.pos[p][:], psum[:, 0:TT * EXP].rearrange("p (t e) -> p t e", t=TT),
                               base[:].unsqueeze(1).to_broadcast([P, TT, EXP]), ALU.add))
    step.run(dve.tensor_tensor(base[:], base[:], psum[:, TT * EXP:(TT + 1) * EXP], ALU.add))
    for k in range(K):
        step(dve.tensor_tensor(w.taken[p][:, k], w.hot[p][:, k], w.pos[p][:], ALU.mult))
    step.wait()
    step.run(dve.tensor_reduce(w.rank[p][:], w.taken[p][:].rearrange("p k t e -> p (k t) e"), AX.X, ALU.add))
    ex = w.expert[p][:].rearrange("p k t -> p (k t)")
    step.run(dve.scalar_tensor_tensor(w.slot[p][:], ex, float(stride), w.rank[p][:], ALU.mult, ALU.add))
    if limit is None:
        dve.tensor_copy(w.slot_i[p][:], w.slot[p][:]).then_inc(done, 1)
        return
    step.run(dve.tensor_scalar(w.rank[p][:], w.rank[p][:], float(limit), None, ALU.is_lt))
    step.run(dve.scalar_tensor_tensor(w.slot[p][:], w.slot[p][:], -float(dump), w.rank[p][:], ALU.add, ALU.mult))
    dve.tensor_scalar(w.slot_i[p][:], w.slot[p][:], float(dump), None, ALU.add).then_inc(done, 1)


class Routing:
    def __init__(self, sb, K):
        self.best = [sb(f"best{q}", [P, TT, 8]) for q in range(2)]
        self.best_at = [sb(f"best_at{q}", [P, TT, 8], U32) for q in range(2)]
        self.expert = [sb(f"expert{q}", [P, K, TT]) for q in range(2)]
        self.hot = [sb(f"hot{q}", [P, K, TT, EXP]) for q in range(2)]
        self.took = [sb(f"took{q}", [P, TT, EXP]) for q in range(2)]
        self.pos = [sb(f"pos{q}", [P, TT, EXP]) for q in range(2)]
        self.taken = [sb(f"taken{q}", [P, K, TT, EXP]) for q in range(2)]
        self.rank = [sb(f"rank{q}", [P, K * TT]) for q in range(2)]
        self.slot = [sb(f"slot{q}", [P, K * TT]) for q in range(2)]
        self.slot_i = [sb(f"slot_i{q}", [P, K * TT], U32) for q in range(2)]
        self.logits = [sb(f"logits{q}", [P, TT, EXP]) for q in range(2)]


def rank_products(pe, c, psum, took):
    pe.matmul(psum[:, 0:EXP], c.before[:], took[:, 0, :], start=True, stop=True)
    pe.matmul(psum[:, EXP:2 * EXP], c.before[:], took[:, 1, :], start=True, stop=False)
    pe.matmul(psum[:, EXP:2 * EXP], c.ones[:], took[:, 0, :], start=False, stop=True)
    pe.matmul(psum[:, 2 * EXP:3 * EXP], c.ones[:], took[:, 0, :], start=True, stop=False)
    return pe.matmul(psum[:, 2 * EXP:3 * EXP], c.ones[:], took[:, 1, :], start=False, stop=True)


def turn_tiles(pe, c, psum, x, chunks):
    for k in range(chunks):
        for t in range(TT):
            ins = pe.transpose(psum[:, k * T + t * P:k * T + (t + 1) * P], x[:, t, k * P:(k + 1) * P], c.ident[:])
    return ins


def front(nc, c, a):
    with ExitStack() as ctx:
        sb, sem = scope(nc, ctx, "front")
        two = range(2)
        catT = [sb(f"catT{q}", [P, KC, T]) for q in two]
        h = [sb(f"h{q}", [P, TT, D]) for q in two]
        xn = [sb(f"xn{q}", [P, TT, D]) for q in two]
        xn2 = [sb(f"xn2{q}", [P, TT, D]) for q in two]
        xT = [sb(f"xT{q}", [P, DC, T]) for q in two]
        qT = [sb(f"qT{q}", [P, DC, T]) for q in two]
        prob = [sb(f"prob{q}", [P, TT, T]) for q in two]
        probT = [sb(f"probT{q}", [P, TT, T]) for q in two]
        avT = [sb(f"avT{q}", [P, DC, T]) for q in two]
        norm = [Norm(sb, f"norm{q}") for q in two]
        smax = [sb(f"smax{q}", [P, TT]) for q in two]
        total = [sb(f"total{q}", [P, TT]) for q in two]
        rows_now = [sb(f"rows_now{q}", [P, 4, TT], U32) for q in two]
        w = Routing(sb, 2)
        gap = [sb(f"gap{q}", [P, TT]) for q in two]
        egap = [sb(f"egap{q}", [P, TT]) for q in two]
        gate = [sb(f"gate{q}", [P, 2, TT]) for q in two]
        SEMS = ("cat_turned emb_ready emb_left emb_right h_ready x_ready x_turned xT_ready q_made qT_ready s_made "
                "smax_ready prob_ready p_turned pT_ready av_made avT_ready o_made x2_ready x2_turned xT2_ready "
                "l_made took_ready r_made slots_ready gap_ready egap_ready kept").split()
        s = {n: sem(n) for n in SEMS}
        gathered = [sem(f"gathered{q}") for q in two]
        sent = [sem(f"sent{q}") for q in two]
        cleared = sem("cleared")
        block = ctx.enter_context(nc.Block())

        def bank(p, k):
            return c.bank[4 * p + k]

        @block.gpsimd
        def _(pool):
            def gather(p):
                for i in range(4):
                    for t in range(TT):
                        pool.indirect_dma_start(
                            c.cat[p][:, t, EMB_AT[i]:EMB_AT[i] + EMB_D[i]], None, a.emb[i],
                            bass.IndirectOffsetOnAxis(ap=rows_now[p][:, i, t:t + 1], axis=0),
                            bounds_check=CUTS[i + 1] - CUTS[i] - 1, oob_is_err=False).then_inc(gathered[p], 16)

            for p in two:
                pool.tensor_copy(rows_now[p][:], c.token_row[:, :, p * TT:(p + 1) * TT]).then_inc(cleared, 1)
                pool.wait_ge(cleared, p + 1)
                gather(p)

            def pair(j, more):
                for p in two if more else ():
                    pool.wait_ge(s["cat_turned"], turn(j, p))
                    pool.wait_ge(gathered[p], (j + 1) * (16 * 4 * TT))
                    pool.tensor_copy(rows_now[p][:], c.token_row[:, :, bass.ds((j + 1) * (2 * TT) + p * TT, TT)])\
                        .then_inc(cleared, 1)
                    pool.memset(c.cat[p][:, :, 0:400], 0.0).then_inc(cleared, 1)
                    wait_apart(pool, c.passed, cleared, j * 4 + 2 * p + 4)
                    gather(p)
                for p in two:
                    wait_apart(pool, c.passed, s["slots_ready"], turn(j, p))
                    for k in two:
                        for t in range(TT):
                            pool.indirect_dma_start(
                                a.xg0, bass.IndirectOffsetOnAxis(ap=w.slot_i[p][:, k * TT + t:k * TT + t + 1], axis=0),
                                xn2[p][:, t, :], None, bounds_check=EXP * CAP - 1,
                                oob_is_err=False).then_inc(sent[p], 16)
                    pool.tensor_copy(c.place0[:, bass.ds(j * 2 + p, 1), :], w.slot_i[p][:].unsqueeze(1))
                    pool.tensor_copy(c.gates[:, bass.ds(j * 2 + p, 1), :],
                                     gate[p][:].rearrange("p k t -> p (k t)").unsqueeze(1))
                    pool.tensor_copy(c.h[:, bass.ds(j * 2 * TT + p * TT, TT), :], h[p][:]).then_inc(s["kept"], 1)

            with pool.Fori(0, PAIRS - 1) as j:
                pair(j, True)
            pair(PAIRS - 1, False)
            for p in two:
                pool.wait_ge(sent[p], 16 * 2 * TT * PAIRS)

        @block.tensor
        def _(pe):
            with pe.Fori(0, PAIRS) as j:
                for p in two:
                    pe.wait_ge(gathered[p], (j + 1) * (16 * 4 * TT))
                    for k in range(KC):
                        for t in range(TT):
                            ins = pe.transpose(bank(p, k // 2)[:, (k % 2) * T + t * P:(k % 2) * T + (t + 1) * P],
                                               c.cat[p][:, t, k * P:(k + 1) * P], c.ident[:])
                    ins.then_inc(s["cat_turned"], 1)
                for p in two:
                    pe.wait_ge(s["emb_left"], turn(j, p))
                    pe.wait_ge(s["emb_right"], turn(j, p))
                    for t in range(TT):
                        for k in range(KC):
                            ins = pe.matmul(bank(p, 2)[:, t * D:(t + 1) * D], catT[p][:, k, t * P:(t + 1) * P],
                                            c.projT[:, k, :], start=k == 0, stop=k == KC - 1)
                    ins.then_inc(s["emb_ready"], 1)
                for p in two:
                    pe.wait_ge(s["x_ready"], turn(j, p))
                    turn_tiles(pe, c, bank(p, 3), xn[p], DC).then_inc(s["x_turned"], 1)
                for p in two:
                    pe.wait_ge(s["xT_ready"], turn(j, p))
                    for m in range(DC):
                        for k in range(DC):
                            ins = pe.matmul(bank(p, 0)[:, m * T:(m + 1) * T], c.QK[:, k, m * P:(m + 1) * P],
                                            xT[p][:, k, :], start=k == 0, stop=k == DC - 1)
                    ins.then_inc(s["q_made"], 1)
                for p in two:
                    pe.wait_ge(s["qT_ready"], turn(j, p))
                    for t in range(TT):
                        for k in range(DC):
                            ins = pe.matmul(bank(p, 1)[:, t * T:(t + 1) * T], qT[p][:, k, t * P:(t + 1) * P],
                                            xT[p][:, k, :], start=k == 0, stop=k == DC - 1)
                    ins.then_inc(s["s_made"], 1)
                for p in two:
                    pe.wait_ge(s["prob_ready"], TT * j * 2 + TT * (p + 1))
                    turn_tiles(pe, c, bank(p, 2), prob[p], TT).then_inc(s["p_turned"], 1)
                for p in two:
                    pe.wait_ge(s["pT_ready"], turn(j, p))
                    for m in range(DC):
                        for k in range(TT):
                            ins = pe.matmul(bank(p, 3)[:, m * T:(m + 1) * T], xn[p][:, k, m * P:(m + 1) * P],
                                            probT[p][:, k, :], start=k == 0, stop=k == TT - 1)
                    ins.then_inc(s["av_made"], 1)
                for p in two:
                    pe.wait_ge(s["avT_ready"], turn(j, p))
                    for t in range(TT):
                        for k in range(DC):
                            ins = pe.matmul(bank(p, 0)[:, t * D:(t + 1) * D], avT[p][:, k, t * P:(t + 1) * P],
                                            c.VO[:, k, :], start=k == 0, stop=k == DC - 1)
                    ins.then_inc(s["o_made"], 1)
                for p in two:
                    pe.wait_ge(s["x2_ready"], turn(j, p))
                    turn_tiles(pe, c, bank(p, 1), xn2[p], DC).then_inc(s["x2_turned"], 1)
                for p in two:
                    pe.wait_ge(s["xT2_ready"], turn(j, p))
                    for t in range(TT):
                        for k in range(DC):
                            ins = pe.matmul(bank(p, 2)[:, t * EXP:(t + 1) * EXP], xT[p][:, k, t * P:(t + 1) * P],
                                            c.Wr[:, k, :], start=k == 0, stop=k == DC - 1)
                    ins.then_inc(s["l_made"], 1)
                for p in two:
                    pe.wait_ge(s["took_ready"], turn(j, p))
                    rank_products(pe, c, bank(p, 3), w.took[p]).then_inc(s["r_made"], 1)

        @block.scalar
        def _(act):
            def both(x):
                return x[:].rearrange("p k t -> p (k t)")

            with act.Fori(0, PAIRS) as j:
                for p in two:
                    act.wait_ge(s["cat_turned"], turn(j, p))
                    act.activation(catT[p][:, 2:4, :].rearrange("p k t -> p (k t)"), bank(p, 1)[:], ACT.Copy)\
                        .then_inc(s["emb_right"], 1)
                for p in two:
                    act.wait_ge(s["emb_ready"], turn(j, p))
                    act.wait_ge(s["kept"], j * 2)
                    act.activation(both(h[p]), bank(p, 2)[:], ACT.Copy, scale=EMB_SCALE).then_inc(s["h_ready"], 1)
                for p in two:
                    act.wait_ge(s["x_turned"], turn(j, p))
                    act.activation(both(xT[p]), bank(p, 3)[:], ACT.Copy).then_inc(s["xT_ready"], 1)
                for p in two:
                    act.wait_ge(s["q_made"], turn(j, p))
                    act.activation(both(qT[p]), bank(p, 0)[:], ACT.Copy).then_inc(s["qT_ready"], 1)
                for p in two:
                    act.wait_ge(s["smax_ready"], turn(j, p))
                    for t in range(TT):
                        act.activation(prob[p][:, t, :], bank(p, 1)[:, t * T:(t + 1) * T], ACT.Exp,
                                       bias=smax[p][:, t:t + 1], scale=ATT_SCALE,
                                       accum_out=total[p][:, t:t + 1]).then_inc(s["prob_ready"], 1)
                for p in two:
                    act.wait_ge(s["p_turned"], turn(j, p))
                    act.activation(both(probT[p]), bank(p, 2)[:], ACT.Copy).then_inc(s["pT_ready"], 1)
                for p in two:
                    act.wait_ge(s["av_made"], turn(j, p))
                    act.activation(both(avT[p]), bank(p, 3)[:], ACT.Copy).then_inc(s["avT_ready"], 1)
                for p in two:
                    act.wait_ge(s["x2_turned"], turn(j, p))
                    act.activation(both(xT[p]), bank(p, 1)[:], ACT.Copy).then_inc(s["xT2_ready"], 1)
                for p in two:
                    act.wait_ge(s["gap_ready"], turn(j, p))
                    act.activation(egap[p][:], gap[p][:], ACT.Exp).then_inc(s["egap_ready"], 1)

        @block.vector
        def _(dve):
            step = Steps(dve, sem("dve"), c.passed)
            with dve.Fori(0, PAIRS) as j:
                step.begin(j * FRONT_STEPS)
                for p in two:
                    dve.wait_ge(s["cat_turned"], turn(j, p))
                    dve.tensor_copy(catT[p][:, 0:2, :].rearrange("p k t -> p (k t)"), bank(p, 0)[:])\
                        .then_inc(s["emb_left"], 1)
                for p in two:
                    dve.wait_ge(s["h_ready"], turn(j, p))
                    layer_norm(dve, step, xn[p], h[p], norm[p], s["x_ready"])
                for p in two:
                    dve.wait_ge(s["s_made"], turn(j, p))
                    step.run(dve.tensor_reduce(smax[p][:], bank(p, 1)[:].rearrange("p (t u) -> p t u", t=TT),
                                               AX.X, ALU.max))
                    dve.tensor_scalar(smax[p][:], smax[p][:], -ATT_SCALE, None, ALU.mult)\
                        .then_inc(s["smax_ready"], 1)
                for p in two:
                    dve.wait_ge(s["prob_ready"], TT * j * 2 + TT * (p + 1))
                    step.run(dve.reciprocal(total[p][:], total[p][:]))
                    dve.wait_ge(s["o_made"], turn(j, p))
                    for t in range(TT):
                        step(dve.scalar_tensor_tensor(h[p][:, t, :], bank(p, 0)[:, t * D:(t + 1) * D],
                                                      total[p][:, t:t + 1], h[p][:, t, :], ALU.mult, ALU.add))
                    step.wait()
                    dve.wait_ge(sent[p], j * (16 * 2 * TT))
                    layer_norm(dve, step, xn2[p], h[p], norm[p], s["x2_ready"])
                for p in two:
                    dve.wait_ge(s["l_made"], turn(j, p))
                    step(dve.tensor_tensor(w.logits[p][:], bank(p, 2)[:, 0:TT * EXP].rearrange(
                        "p (t e) -> p t e", t=TT), c.br[:].unsqueeze(1).to_broadcast([P, TT, EXP]), ALU.add))
                    route(dve, step, w, p, w.logits[p], 2)
                    dve.tensor_tensor(gap[p][:], w.best[p][:, :, 1], w.best[p][:, :, 0], ALU.subtract)\
                        .then_inc(s["gap_ready"], 1)
                    for k in two:
                        step(dve.tensor_tensor(w.hot[p][:, k], c.iota8[:].unsqueeze(1).to_broadcast([P, TT, EXP]),
                                               w.expert[p][:, k, :].unsqueeze(2).to_broadcast([P, TT, EXP]),
                                               ALU.is_equal))
                    step.wait()
                    dve.tensor_tensor(w.took[p][:], w.hot[p][:, 0], w.hot[p][:, 1], ALU.add)\
                        .then_inc(s["took_ready"], 1)
                for p in two:
                    dve.wait_ge(s["egap_ready"], turn(j, p))
                    step.run(dve.tensor_scalar(gap[p][:], egap[p][:], 1.0, None, ALU.add))
                    step.run(dve.reciprocal(gate[p][:, 0, :], gap[p][:]))
                    step(dve.tensor_tensor(gate[p][:, 1, :], gate[p][:, 0, :], egap[p][:], ALU.mult))
                    dve.wait_ge(s["r_made"], turn(j, p))
                    places(nc, dve, step, w, p, c, 2, c.base0, bank(p, 3), CAP, CAP, EXP * CAP,
                           s["slots_ready"])
                assert step.n == FRONT_STEPS, step.n


def moe2(nc, c, a):
    with ExitStack() as ctx:
        sb, sem = scope(nc, ctx, "moe2")
        two = range(2)
        G = 512
        GROUPS = CAP // G
        GT = G // P
        HC = HID0 // P
        W1 = [sb(f"W1{q}", [P, DC, HID0]) for q in two]
        W2 = [sb(f"W2{q}", [P, HC, D]) for q in two]
        b2 = [sb(f"b2{q}", [P, D]) for q in two]
        x = [sb(f"x{q}", [P, GT, D]) for q in two]
        xT = [sb(f"xT{q}", [P, DC, G]) for q in two]
        hT = [sb(f"hT{q}", [P, HC, G]) for q in two]
        y = [sb(f"y{q}", [P, GT, D]) for q in two]
        w_loaded = [sem(f"w_loaded{q}") for q in two]
        x_loaded = [sem(f"x_loaded{q}") for q in two]
        stored = [sem(f"stored{q}") for q in two]
        names = "x_turned xT_left xT_right h_made h_ready y_made y_ready".split()
        s = {n: sem(n) for n in names}
        EXPERTS = EXP // 2
        block = ctx.enter_context(nc.Block())

        def unit(j, p, g):
            return j * (2 * GROUPS) + p * GROUPS + g

        @block.sync
        def _(sp):
            def load_w(e, p):
                def of(ap):
                    return ap[bass.ds(e, 1)] if not isinstance(e, int) else ap[e:e + 1]
                sp.dma_start(W1[p][:], of(a.W1).rearrange("e (k p) n -> p (e k) n", p=P)).then_inc(w_loaded[p], 16)
                sp.dma_start(W2[p][:], of(a.W2).rearrange("e (k p) n -> p (e k) n", p=P)).then_inc(w_loaded[p], 16)
                sp.dma_start(b2[p][:], of(a.b2).to_broadcast([P, D])).then_inc(w_loaded[p], 16)

            def load_x(u, g):
                r = bass.ds(u * G, G) if not isinstance(u, int) else slice(u * G, (u + 1) * G)
                sp.dma_start(x[g][:], a.xg0[r, :].rearrange("(t p) d -> p t d", p=P)).then_inc(x_loaded[g], 16)

            load_x(0, 0)
            load_w(0, 0)
            load_x(1, 1)
            load_w(1, 1)

            def pair(j, more):
                for g in range(GROUPS):
                    sp.wait_ge(s["x_turned"], unit(j, 0, g) + 1)
                    load_x(unit(j, 1, g), g)
                if not more:
                    return
                for p in two:
                    if p == 0:
                        for g in range(GROUPS):
                            sp.wait_ge(s["x_turned"], unit(j, 1, g) + 1)
                            load_x(unit(j + 1, 0, g), g)
                            if g == 0:
                                sp.wait_ge(s["y_ready"], unit(j, 1, 0) * GT)
                                load_w((j + 1) * 2, 0)
                    else:
                        sp.wait_ge(s["y_ready"], unit(j + 1, 0, 0) * GT)
                        load_w((j + 1) * 2 + 1, 1)

            with sp.Fori(0, EXPERTS - 1) as j:
                pair(j, True)
            pair(EXPERTS - 1, False)

        @block.gpsimd
        def _(pool):
            with pool.Fori(0, EXPERTS) as j:
                for p in two:
                    for g in range(GROUPS):
                        u = unit(j, p, g)
                        pool.wait_ge(s["y_ready"], (u + 1) * GT)
                        pool.dma_start(a.y0[bass.ds(u * G, G), :].rearrange("(t p) d -> p t d", p=P), y[g][:])\
                            .then_inc(stored[g], 16)
            for g in two:
                pool.wait_ge(stored[g], 16 * EXP)

        @block.tensor
        def _(pe):
            with pe.Fori(0, EXPERTS) as j:
                def turn_x(p, g):
                    pe.wait_ge(x_loaded[g], 16 * (2 * j + p + 1))
                    for k in range(DC):
                        for t in range(GT):
                            ins = pe.transpose(c.bank[k][:, t * P:(t + 1) * P], x[g][:, t, k * P:(k + 1) * P],
                                               c.ident[:])
                    ins.then_inc(s["x_turned"], 1)

                for p in two:
                    pe.wait_ge(w_loaded[p], 48 * (j + 1))
                    for g in range(GROUPS):
                        u = unit(j, p, g)
                        if (p, g) == (0, 0):
                            turn_x(0, 0)
                        pe.wait_ge(s["xT_left"], u + 1)
                        pe.wait_ge(s["xT_right"], u + 1)
                        for m in range(HC):
                            if m >= 3:
                                pe.wait_ge(s["h_ready"], u * HC + m - 2)
                            for k in range(DC):
                                ins = pe.matmul(c.bank[2 + m % 3][:], W1[p][:, k, m * P:(m + 1) * P], xT[g][:, k, :],
                                                start=k == 0, stop=k == DC - 1)
                            ins.then_inc(s["h_made"], 1)
                        if (p, g) != (1, 1):
                            turn_x(p + (g + 1) // GROUPS, (g + 1) % GROUPS)
                        pe.wait_ge(s["h_ready"], (u + 1) * HC)
                        for t in range(GT):
                            pe.wait_ge(s["y_ready"], u * GT + max(t - 1, 0))
                            for k in range(HC):
                                ins = pe.matmul(c.bank[6 + t % 2][:, 0:D], hT[g][:, k, t * P:(t + 1) * P], W2[p][:, k, :],
                                                start=k == 0, stop=k == HC - 1)
                            ins.then_inc(s["y_made"], 1)

        @block.scalar
        def _(act):
            with act.Fori(0, EXPERTS) as j:
                def move(p, g):
                    u = unit(j, p, g)
                    act.wait_ge(s["x_turned"], u + 1)
                    act.activation(xT[g][:, 1, :], c.bank[1][:], ACT.Copy).then_inc(s["xT_right"], 1)

                for p in two:
                    for g in range(GROUPS):
                        u = unit(j, p, g)
                        if (p, g) == (0, 0):
                            move(0, 0)
                        for m in range(HC):
                            wait_apart(act, c.passed, s["h_made"], u * HC + m + 1)
                            act.activation(hT[g][:, m, :], c.bank[2 + m % 3][:], ACT.Gelu,
                                           bias=c.b1T[:, bass.ds((2 * j + p) * HC + m, 1)])\
                                .then_inc(s["h_ready"], 1)
                        if (p, g) != (1, 1):
                            move(p + (g + 1) // GROUPS, (g + 1) % GROUPS)

        @block.vector
        def _(dve):
            with dve.Fori(0, EXPERTS) as j:
                def move(p, g):
                    u = unit(j, p, g)
                    dve.wait_ge(s["x_turned"], u + 1)
                    dve.tensor_copy(xT[g][:, 0, :], c.bank[0][:]).then_inc(s["xT_left"], 1)

                for p in two:
                    dve.wait_ge(w_loaded[p], 48 * (j + 1))
                    for g in range(GROUPS):
                        u = unit(j, p, g)
                        if (p, g) == (0, 0):
                            move(0, 0)
                        if (p, g) != (1, 1):
                            move(p + (g + 1) // GROUPS, (g + 1) % GROUPS)
                        dve.wait_ge(stored[g], (2 * j + p) * 16)
                        for t in range(GT):
                            dve.wait_ge(s["y_made"], u * GT + t + 1)
                            dve.tensor_tensor(y[g][:, t, :], c.bank[6 + t % 2][:, 0:D], b2[p][:], ALU.add)\
                                .then_inc(s["y_ready"], 1)


def middle(nc, c, a):
    with ExitStack() as ctx:
        sb, sem = scope(nc, ctx, "mid")
        two = range(2)
        GP = HEADS // 2
        UNITS = 2 * GP
        RING = 4
        V1 = HD + 1
        yrow = [sb(f"yrow{q}", [P, 2, TT, D]) for q in two]
        h = [sb(f"h{q}", [P, TT, D]) for q in two]
        place_now = [sb(f"place_now{q}", [P, 2 * TT], U32) for q in two]
        gate_now = [sb(f"gate_now{q}", [P, 2 * TT]) for q in two]
        xn = [sb(f"xn{q}", [P, TT, D]) for q in two]
        xT = [sb(f"xT{q}", [P, DC, T]) for q in two]
        qk = [sb(f"qk{q}", [P, TT, 2 * D]) for q in two]
        sq = [y[:].rearrange("p k t d -> p k (t d)") for y in yrow]
        NG = TT * 2 * HEADS
        ss = [sb(f"ss{q}", [P, NG]) for q in two]
        rn = [sb(f"rn{q}", [P, NG]) for q in two]
        rtmp = [sb(f"rtmp{q}", [P, NG]) for q in two]
        zT = [sb(f"zT{q}", [P, DC, 2 * T]) for q in two]
        ex = [sb(f"ex{n}", [P, 2 * T]) for n in range(RING)]
        pr2 = [sb(f"pr2{n}", [P, 2 * T]) for n in range(RING)]
        feat = [sb(f"feat{n}", [P, 2 * T]) for n in range(RING)]
        attn = [sb(f"attn{n}", [P, 2, 3, P]) for n in range(RING)]
        den = [sb(f"den{q}", [P, TT, HEADS]) for q in two]
        ctxv = xn
        norm = [Norm(sb, f"norm{q}") for q in two]
        w = Routing(sb, 1)
        nbest = [sb(f"nbest{q}", [P, TT]) for q in two]
        prob = [sb(f"prob{q}", [P, TT, EXP]) for q in two]
        psum_p = [sb(f"psum{q}", [P, TT]) for q in two]
        tv = [sb(f"tv{q}", [P, TT]) for q in two]
        SEMS = ("h_loaded h_ready x_ready x_turned xT_ready qkv_made qk_ready sq_ready z_ready z_turned zT_left "
                "zT_right f_made ex_ready pr2_ready clipped feat_ready a_made a_masked av_made ctx_ready "
                "ctx_turned ctxT_ready o_made bout_added x2_ready x2_turned xT2_ready l_made took_ready r_made "
                "slots_ready nbest_ready prob_ready kept").split()
        s = {n: sem(n) for n in SEMS}
        fetched = [sem(f"fetched{q}") for q in two]
        sent = [sem(f"sent{q}") for q in two]
        copied = sem("copied")
        w_loaded = sem("w_loaded")
        block = ctx.enter_context(nc.Block())

        def bank(p, k):
            return c.bank[4 * p + k]

        def f_bank(u):
            return c.bank[u % 2]

        def a_banks(u):
            return c.ps[:, 2 + 2 * (u % 2):4 + 2 * (u % 2), :]

        @block.sync
        def _(sp):
            for e in range(EXP):
                sp.dma_start(c.W1[:, 2 * e:2 * e + 2, :], a.ew1[e].rearrange("(k p) n -> p k n", p=P))\
                    .then_inc(w_loaded, 16)
                sp.dma_start(c.W2[:, 4 * e:4 * e + 4, :], a.ew2[e].rearrange("(k p) n -> p k n", p=P))\
                    .then_inc(w_loaded, 16)
            sp.wait_ge(w_loaded, 16 * 2 * EXP)

        @block.gpsimd
        def _(pool):
            def index(b, p):
                pool.tensor_copy(place_now[p][:].unsqueeze(1), c.place0[:, bass.ds(b, 1), :]
                                 if not isinstance(b, int) else c.place0[:, b:b + 1, :])
                pool.tensor_copy(gate_now[p][:].unsqueeze(1), c.gates[:, bass.ds(b, 1), :]
                                 if not isinstance(b, int) else c.gates[:, b:b + 1, :]).then_inc(copied, 1)

            def fetch(p, n):
                pool.indirect_dma_start(yrow[p][:, n // TT, n % TT, :], None, a.y0,
                                        bass.IndirectOffsetOnAxis(ap=place_now[p][:, n:n + 1], axis=0),
                                        bounds_check=EXP * CAP, oob_is_err=False).then_inc(fetched[p], 16)

            for p in two:
                index(p, p)
                pool.wait_ge(copied, p + 1)
                for n in range(2 * TT):
                    fetch(p, n)

            def pair(j, more):
                for p in two:
                    pool.wait_ge(s["x_ready"], turn(j, p))
                    pool.tensor_tensor(h[p][:], h[p][:], c.bout[:].unsqueeze(1).to_broadcast([P, TT, D]), ALU.add)\
                        .then_inc(s["bout_added"], 1)
                for u in range(UNITS):
                    if u % 8 == 0:
                        pool.wait_ge(s["ex_ready"], j * UNITS + u + 1)
                    if more and u % 8 == 0:
                        p = u // 8
                        pool.wait_ge(fetched[p], (j + 1) * (16 * 2 * TT))
                        index((j + 1) * 2 + p, p)
                        wait_apart(pool, c.passed, copied, (j + 1) * 2 + p + 1)
                    if more and u % 8 in (1, 3, 5, 7):
                        fetch(u // 8, u % 8 // 2)
                for p in two:
                    wait_apart(pool, c.passed, s["slots_ready"], turn(j, p))
                    for t in range(TT):
                        pool.indirect_dma_start(a.xg1, bass.IndirectOffsetOnAxis(ap=w.slot_i[p][:, t:t + 1], axis=0),
                                                xn[p][:, t, :], None, bounds_check=EXP * REGION - 1,
                                                oob_is_err=False).then_inc(sent[p], 16)
                    pool.tensor_copy(c.expert1[:, bass.ds(j * 2 + p, 1), :], w.expert[p][:])
                    pool.tensor_copy(c.rank1[:, bass.ds(j * 2 + p, 1), :], w.rank[p][:].unsqueeze(1))
                    pool.tensor_copy(c.topv[:, bass.ds(j * 2 + p, 1), :], tv[p][:].unsqueeze(1))
                    pool.tensor_tensor(c.h[:, bass.ds(j * 2 * TT + p * TT, TT), :], h[p][:],
                                       c.beta[:].unsqueeze(1).to_broadcast([P, TT, D]), ALU.add)\
                        .then_inc(s["kept"], 1)

            with pool.Fori(0, PAIRS - 1) as j:
                pair(j, True)
            pair(PAIRS - 1, False)
            for p in two:
                pool.wait_ge(sent[p], 16 * TT * PAIRS)

        @block.tensor
        def _(pe):
            def products(u, j):
                p, g = u // GP, u % GP
                r = 32 * (g % 4)
                if u >= 2:
                    pe.wait_ge(s["pr2_ready"], j * UNITS + u - 1)
                    pe.wait_ge(s["ex_ready"], j * UNITS + u - 1)
                pe.matmul(f_bank(u), c.omega[r:r + 32, g // 4, :], zT[p][r:r + 32, g // 4, :],
                          start=True, stop=True).then_inc(s["f_made"], 1)

            def scores(u, j):
                pe.wait_ge(s["feat_ready"], j * UNITS + u + 1)
                if u >= 2:
                    pe.wait_ge(s["a_masked"], j * UNITS + u - 1)
                f = feat[u % RING]
                for hh in two:
                    r = slice(NF * hh, NF * (hh + 1))
                    out = a_banks(u)[:, hh, :]
                    pe.matmul(out[:, 0:T], f[r, T:T + P], f[r, 0:T], start=True, stop=True)
                    ins = pe.matmul(out[:, T:T + P], f[r, T + P:2 * T], f[r, P:T], start=True, stop=True)
                ins.then_inc(s["a_made"], 1)

            def values(u, j):
                p, g = u // GP, u % GP
                pe.wait_ge(s["a_masked"], j * UNITS + u + 1)
                if u == GP:
                    pe.wait_ge(s["ctx_ready"], turn(j, 0))
                at = attn[u % RING]
                for hh in two:
                    head = 2 * g + hh
                    cols = slice(head * V1, (head + 1) * V1)
                    pe.matmul(c.bank[6][:, cols], at[:, hh, 0, :], c.vone[p][:, 0, head, :], start=True, stop=True)
                    pe.matmul(c.bank[7][:, cols], at[:, hh, 1, :], c.vone[p][:, 0, head, :], start=True, stop=False)
                    ins = pe.matmul(c.bank[7][:, cols], at[:, hh, 2, :], c.vone[p][:, 1, head, :],
                                    start=False, stop=True)
                ins.then_inc(s["av_made"], 1)

            with pe.Fori(0, PAIRS) as j:
                for p in two:
                    pe.wait_ge(s["x_ready"], turn(j, p))
                    turn_tiles(pe, c, bank(p, 0), xn[p], DC).then_inc(s["x_turned"], 1)
                for p in two:
                    pe.wait_ge(s["xT_ready"], turn(j, p))
                    for t in range(TT):
                        for k in range(DC):
                            pe.matmul(bank(p, 1 + t)[:], xT[p][:, k, t * P:(t + 1) * P], c.wqkvT[:, k, 0:2 * D],
                                      start=k == 0, stop=k == DC - 1)
                    for t in range(TT):
                        for k in range(DC):
                            ins = pe.matmul(bank(p, 3)[:, t * D:(t + 1) * D], xT[p][:, k, t * P:(t + 1) * P],
                                            c.wqkvT[:, k, 2 * D:3 * D], start=k == 0, stop=k == DC - 1)
                    ins.then_inc(s["qkv_made"], 1)
                for p in two:
                    pe.wait_ge(s["z_ready"], turn(j, p))
                    for k in range(DC):
                        for part in two:
                            for t in range(TT):
                                col = part * D + k * P
                                ins = pe.transpose(bank(p, 1 + k)[:, part * T + t * P:part * T + (t + 1) * P],
                                                   qk[p][:, t, col:col + P], c.ident[:])
                    ins.then_inc(s["z_turned"], 1)
                pe.wait_ge(s["zT_left"], turn(j, 1))
                pe.wait_ge(s["zT_right"], turn(j, 1))
                for u in range(UNITS + 3):
                    if u < UNITS:
                        products(u, j)
                    if 2 <= u < UNITS + 2:
                        scores(u - 2, j)
                    if u >= 3:
                        values(u - 3, j)
                for p in two:
                    pe.wait_ge(s["ctx_ready"], turn(j, p))
                    turn_tiles(pe, c, bank(p, 0), ctxv[p], DC).then_inc(s["ctx_turned"], 1)
                for p in two:
                    pe.wait_ge(s["ctxT_ready"], turn(j, p))
                    for t in range(TT):
                        for k in range(DC):
                            ins = pe.matmul(bank(p, 1)[:, t * D:(t + 1) * D], xT[p][:, k, t * P:(t + 1) * P],
                                            c.woutT[:, k, :], start=k == 0, stop=k == DC - 1)
                    ins.then_inc(s["o_made"], 1)
                for p in two:
                    pe.wait_ge(s["x2_ready"], turn(j, p))
                    turn_tiles(pe, c, bank(p, 2), xn[p], DC).then_inc(s["x2_turned"], 1)
                for p in two:
                    pe.wait_ge(s["xT2_ready"], turn(j, p))
                    for t in range(TT):
                        for k in range(DC):
                            ins = pe.matmul(bank(p, 3)[:, t * EXP:(t + 1) * EXP], xT[p][:, k, t * P:(t + 1) * P],
                                            c.gateT[:, k, :], start=k == 0, stop=k == DC - 1)
                    ins.then_inc(s["l_made"], 1)
                for p in two:
                    pe.wait_ge(s["took_ready"], turn(j, p))
                    rank_products(pe, c, bank(p, 1), w.hot[p][:, 0]).then_inc(s["r_made"], 1)

        @block.scalar
        def _(act):
            with act.Fori(0, PAIRS) as j:
                for p in two:
                    if p == 0:
                        wait_apart(act, c.passed, s["kept"], j * 2)
                    act.activation(h[p][:], c.h[:, bass.ds(j * 2 * TT + p * TT, TT), :], ACT.Copy)\
                        .then_inc(s["h_loaded"], 1)
                for p in two:
                    act.wait_ge(s["x_turned"], turn(j, p))
                    act.activation(xT[p][:].rearrange("p k t -> p (k t)"), bank(p, 0)[:], ACT.Copy)\
                        .then_inc(s["xT_ready"], 1)
                for p in two:
                    act.wait_ge(s["qk_ready"], turn(j, p))
                    act.activation(sq[p], qk[p][:], ACT.Square).then_inc(s["sq_ready"], 1)
                for p in two:
                    act.wait_ge(s["z_turned"], turn(j, p))
                    act.activation(zT[p][:, 0, :], bank(p, 1)[:], ACT.Copy).then_inc(s["zT_left"], 1)
                for u in range(UNITS):
                    if u < UNITS:
                        act.wait_ge(s["f_made"], j * UNITS + u + 1)
                        if u >= RING:
                            act.wait_ge(s["feat_ready"], j * UNITS + u - RING + 1)
                        act.activation(ex[u % RING][:], f_bank(u), ACT.Exp, scale=c.f_scale[:], bias=c.f_shift[:])\
                            .then_inc(s["ex_ready"], 1)
                        act.activation(pr2[u % RING][:], f_bank(u), ACT.Square).then_inc(s["pr2_ready"], 1)
                for p in two:
                    act.wait_ge(s["ctx_turned"], turn(j, p))
                    act.activation(xT[p][:].rearrange("p k t -> p (k t)"), bank(p, 0)[:], ACT.Copy)\
                        .then_inc(s["ctxT_ready"], 1)
                for p in two:
                    act.wait_ge(s["x2_turned"], turn(j, p))
                    act.activation(xT[p][:].rearrange("p k t -> p (k t)"), bank(p, 2)[:], ACT.Copy)\
                        .then_inc(s["xT2_ready"], 1)
                for p in two:
                    act.wait_ge(s["nbest_ready"], turn(j, p))
                    for t in range(TT):
                        act.activation(prob[p][:, t, :], w.logits[p][:, t, :], ACT.Exp, bias=nbest[p][:, t:t + 1],
                                       accum_out=psum_p[p][:, t:t + 1]).then_inc(s["prob_ready"], 1)

        @block.vector
        def _(dve):
            step = Steps(dve, sem("dve"), c.passed)

            def context(j, p):
                dve.wait_ge(s["av_made"], j * UNITS + (p + 1) * GP)
                av = c.ps[:, 6:8, 0:HEADS * V1].rearrange("p t (h e) -> p t h e", e=V1)
                step.run(dve.tensor_scalar(den[p][:], av[:, :, :, HD], 1e-6, None, ALU.max))
                step.run(dve.reciprocal(den[p][:], den[p][:]))
                dve.tensor_tensor(ctxv[p][:].rearrange("p t (h e) -> p t h e", e=HD), av[:, :, :, 0:HD],
                                  den[p][:].unsqueeze(3).to_broadcast([P, TT, HEADS, HD]), ALU.mult)\
                    .then_inc(s["ctx_ready"], 1)

            with dve.Fori(0, PAIRS) as j:
                step.begin(j * MIDDLE_STEPS)
                for p in two:
                    dve.wait_ge(fetched[p], (j + 1) * (16 * 2 * TT))
                    dve.wait_ge(s["h_loaded"], turn(j, p))
                    for k in two:
                        for t in range(TT):
                            n = k * TT + t
                            step(dve.scalar_tensor_tensor(h[p][:, t, :], yrow[p][:, k, t, :], gate_now[p][:, n:n + 1],
                                                          h[p][:, t, :], ALU.mult, ALU.add))
                        step.wait()
                    dve.wait_ge(sent[p], j * (16 * TT))
                    layer_norm(dve, step, xn[p], h[p], norm[p], s["x_ready"])
                for p in two:
                    dve.wait_ge(s["qkv_made"], turn(j, p))
                    dve.tensor_tensor(qk[p][:], c.ps[:, 4 * p + 1:4 * p + 3, :],
                                      c.bqkv[:, 0:2 * D].unsqueeze(1).to_broadcast([P, TT, 2 * D]), ALU.add)\
                        .then_inc(s["qk_ready"], 1)
                    for t in range(TT):
                        step(dve.tensor_tensor(c.vone[p][:, t, :, 0:HD],
                                               bank(p, 3)[:, t * D:(t + 1) * D].rearrange("p (h e) -> p h e", e=HD),
                                               c.bqkv[:, 2 * D:3 * D].rearrange("p (h e) -> p h e", e=HD), ALU.add))
                for p in two:
                    dve.wait_ge(s["sq_ready"], turn(j, p))
                    step.run(dve.tensor_reduce(ss[p][:], sq[p].rearrange("p t (g e) -> p (t g) e", e=HD),
                                               AX.X, ALU.add))
                    step.run(dve.tensor_scalar(ss[p][:], ss[p][:], 1e-24, None, ALU.max))
                    rsqrt(dve, step, rn[p][:], ss[p][:], rtmp[p][:])
                    z = qk[p][:].rearrange("p t (g e) -> p (t g) e", e=HD)
                    dve.tensor_tensor(z, z, rn[p][:].unsqueeze(2).to_broadcast([P, NG, HD]), ALU.mult)\
                        .then_inc(s["z_ready"], 1)
                for p in two:
                    dve.wait_ge(s["z_turned"], turn(j, p))
                    dve.tensor_copy(zT[p][:, 1, :], bank(p, 2)[:]).then_inc(s["zT_right"], 1)
                for u in range(UNITS + 3):
                    if u < UNITS:
                        dve.wait_ge(s["ex_ready"], j * UNITS + u + 1)
                        dve.tensor_scalar(ex[u % RING][:], ex[u % RING][:], EXP_LO, EXP_HI, ALU.max, ALU.min)\
                            .then_inc(s["clipped"], 1)
                    if u >= 1 and u - 1 < UNITS:
                        v = u - 1
                        dve.wait_ge(s["clipped"], j * UNITS + v + 1)
                        dve.wait_ge(s["pr2_ready"], j * UNITS + v + 1)
                        if v >= RING:
                            dve.wait_ge(s["a_made"], j * UNITS + v - RING + 1)
                        dve.scalar_tensor_tensor(feat[v % RING][:], ex[v % RING][:], c.f_weight[:], pr2[v % RING][:],
                                                 ALU.mult, ALU.mult).then_inc(s["feat_ready"], 1)
                    if u >= 3:
                        v = u - 3
                        dve.wait_ge(s["a_made"], j * UNITS + v + 1)
                        if v >= RING:
                            dve.wait_ge(s["av_made"], j * UNITS + v - RING + 1)
                        dve.tensor_tensor(
                            attn[v % RING][:].rearrange("p h b t -> p h (b t)"), a_banks(v)[:, :, 0:3 * P],
                            c.causal[:].rearrange("p b t -> p (b t)").unsqueeze(1).to_broadcast([P, 2, 3 * P]),
                            ALU.mult)\
                            .then_inc(s["a_masked"], 1)
                    if u == GP + 3:
                        context(j, 0)
                context(j, 1)
                for p in two:
                    dve.wait_ge(s["bout_added"], turn(j, p))
                    dve.wait_ge(s["o_made"], turn(j, p))
                    step.run(dve.tensor_tensor(h[p][:].rearrange("p t d -> p (t d)"), bank(p, 1)[:],
                                               h[p][:].rearrange("p t d -> p (t d)"), ALU.add))
                    layer_norm(dve, step, xn[p], h[p], norm[p], s["x2_ready"])
                for p in two:
                    dve.wait_ge(s["l_made"], turn(j, p))
                    step(dve.tensor_copy(w.logits[p][:], bank(p, 3)[:, 0:TT * EXP].rearrange(
                        "p (t e) -> p t e", t=TT)))
                    route(dve, step, w, p, w.logits[p], 1)
                    dve.tensor_scalar(nbest[p][:], w.best[p][:, :, 0], -1.0, None, ALU.mult)\
                        .then_inc(s["nbest_ready"], 1)
                    dve.tensor_tensor(w.hot[p][:, 0], c.iota8[:].unsqueeze(1).to_broadcast([P, TT, EXP]),
                                      w.expert[p][:, 0, :].unsqueeze(2).to_broadcast([P, TT, EXP]),
                                      ALU.is_equal).then_inc(s["took_ready"], 1)
                for p in two:
                    dve.wait_ge(s["prob_ready"], TT * j * 2 + TT * (p + 1))
                    step.run(dve.reciprocal(psum_p[p][:], psum_p[p][:]))
                    step.run(dve.tensor_scalar(tv[p][:], psum_p[p][:], 1e-8, None, ALU.add))
                    step.run(dve.reciprocal(tv[p][:], tv[p][:]))
                    step(dve.tensor_tensor(tv[p][:], tv[p][:], psum_p[p][:], ALU.mult))
                    dve.wait_ge(s["r_made"], turn(j, p))
                    places(nc, dve, step, w, p, c, 1, c.base1, bank(p, 1), REGION, None, None, s["slots_ready"])
                assert step.n == MIDDLE_STEPS, step.n


def moe1(nc, c, a):
    with ExitStack() as ctx:
        sb, sem = scope(nc, ctx, "moe1")
        UN, MT = MOE1_FLIGHT, MOE1_TILES
        HC = HID1 // P
        count_i = sb("count_i", [P, EXP], I32)
        tiles_i = sb("tiles_i", [P, EXP], I32)
        tail_i = sb("tail_i", [P, EXP], I32)
        tiles = sb("tiles", [P, EXP])
        cum = sb("cum", [P, EXP])
        past = sb("past", [P, MT, EXP])
        ej = sb("ej", [P, MT])
        before = sb("before", [P, MT])
        row = sb("row", [P, MT])
        row_in = sb("row_in", [P, MT], I32)
        hot = sb("hot", [P, TILES, EXP])
        first = sb("first", [P, TILES])
        e_i = sb("e_i", [P, MT], I32)
        q4 = range(UN)
        x = [sb(f"x{q}", [P, D]) for q in q4]
        xT = [sb(f"xT{q}", [P, DC, P]) for q in q4]
        g = [sb(f"g{q}", [P, HID1]) for q in q4]
        gT = [sb(f"gT{q}", [P, HC, P]) for q in q4]
        y = [sb(f"y{q}", [P, D]) for q in q4]
        tables = sem("tables")
        tails = sem("tails")
        loaded = [sem(f"loaded{q}") for q in q4]
        stored = [sem(f"stored{q}") for q in q4]
        names = "x_turned xT_ready h_made g_ready g_turned gT_ready y_made y_ready".split()
        s = {n: sem(n) for n in names}
        block = ctx.enter_context(nc.Block())

        def done(i, q):
            return i * UN + q + 1

        @block.sync
        def _(sp):
            sp.wait_ge(tables, 1)
            for e in range(EXP):
                r = sp.value_load(tail_i[0:1, e:e + 1], min_val=e * REGION, max_val=e * REGION + N)
                sp.dma_start(a.xg1[bass.ds(r, P), :], c.zero[:, 0:D]).then_inc(tails, 16)
            sp.wait_ge(tails, 16 * EXP)

            def load(t, q):
                r = sp.value_load(row_in[0:1, bass.ds(t, 1)] if not isinstance(t, int) else row_in[0:1, t:t + 1],
                                  min_val=0, max_val=EXP * REGION)
                sp.dma_start(x[q][:], a.xg1[bass.ds(r, P), :]).then_inc(loaded[q], 16)

            for q in q4:
                load(q, q)
            with sp.Fori(0, MT // UN - 1) as i:
                for q in q4:
                    sp.wait_ge(s["x_turned"], done(i, q))
                    load((i + 1) * UN + q, q)

        @block.gpsimd
        def _(pool):
            with pool.Fori(0, MT // UN) as i:
                for q in q4:
                    pool.wait_ge(s["y_ready"], done(i, q))
                    pool.dma_start(a.y1[bass.ds((i * UN + q) * P, P), :], y[q][:]).then_inc(stored[q], 16)
            for q in q4:
                pool.wait_ge(stored[q], 16 * (MT // UN))

        @block.tensor
        def _(pe):
            def bank(q, k):
                return c.bank[2 * q + k]

            pe.wait_ge(tables, 1)
            with pe.Fori(0, MT // UN) as i:
                e = [pe.value_load(e_i[0:1, bass.ds(i * UN + q, 1)], min_val=0, max_val=EXP - 1) for q in q4]
                for q in q4:
                    pe.wait_ge(loaded[q], 16 * (i + 1))
                    for k in range(DC):
                        ins = pe.transpose(bank(q, 0)[:, k * P:(k + 1) * P], x[q][:, k * P:(k + 1) * P], c.ident[:])
                    ins.then_inc(s["x_turned"], 1)
                for q in q4:
                    pe.wait_ge(s["xT_ready"], done(i, q))
                    if q < UN:
                        pe.wait_ge(s["y_ready"], i * UN)
                    for k in range(DC):
                        ins = pe.matmul(bank(q, 1)[:], xT[q][:, k, :], c.W1[:, bass.ds(e[q] * DC + k, 1), :],
                                        start=k == 0, stop=k == DC - 1)
                    ins.then_inc(s["h_made"], 1)
                for q in q4:
                    pe.wait_ge(s["g_ready"], done(i, q))
                    for k in range(HC):
                        ins = pe.transpose(bank(q, 0)[:, k * P:(k + 1) * P], g[q][:, k * P:(k + 1) * P], c.ident[:])
                    ins.then_inc(s["g_turned"], 1)
                for q in q4:
                    pe.wait_ge(s["gT_ready"], done(i, q))
                    for k in range(HC):
                        ins = pe.matmul(bank(q, 1)[:, 0:D], gT[q][:, k, :], c.W2[:, bass.ds(e[q] * HC + k, 1), :],
                                        start=k == 0, stop=k == HC - 1)
                    ins.then_inc(s["y_made"], 1)

        @block.scalar
        def _(act):
            with act.Fori(0, MT // UN) as i:
                for q in q4:
                    act.wait_ge(s["h_made"], done(i, q))
                    act.activation(g[q][:], c.bank[2 * q + 1][:], ACT.Gelu).then_inc(s["g_ready"], 1)
                for q in q4:
                    act.wait_ge(s["y_made"], done(i, q))
                    act.wait_ge(stored[q], 16 * i)
                    act.activation(y[q][:], c.bank[2 * q + 1][:, 0:D], ACT.Copy).then_inc(s["y_ready"], 1)

        @block.vector
        def _(dve):
            step = Steps(dve, sem("dve"), c.passed)
            step.run(dve.tensor_copy(count_i[:], c.base1[:]))
            step.run(dve.tensor_scalar(tiles[:], c.base1[:], float(P - 1), None, ALU.add))
            step.run(dve.tensor_copy(tiles_i[:], tiles[:]))
            step.run(dve.tensor_scalar(tiles_i[:], tiles_i[:], 7, None, ALU.logical_shift_right))
            step.run(dve.tensor_copy(tiles[:], tiles_i[:]))
            step.run(dve.tensor_copy(cum[:], tiles[:]))
            for e in range(1, EXP):
                step.run(dve.tensor_tensor(cum[:, e:e + 1], cum[:, e - 1:e], tiles[:, e:e + 1], ALU.add))
            step.run(dve.tensor_tensor(past[:], c.tile_no[:].unsqueeze(2).to_broadcast([P, MT, EXP]),
                                       cum[:].unsqueeze(1).to_broadcast([P, MT, EXP]), ALU.is_ge))
            step.run(dve.tensor_reduce(ej[:], past[:], AX.X, ALU.add))
            step.run(dve.tensor_tensor(past[:], past[:], tiles[:].unsqueeze(1).to_broadcast([P, MT, EXP]), ALU.mult))
            step.run(dve.tensor_reduce(before[:], past[:], AX.X, ALU.add))
            step.run(dve.tensor_tensor(before[:], c.tile_no[:], before[:], ALU.subtract))
            step.run(dve.tensor_scalar(before[:], before[:], float(P), None, ALU.mult))
            step.run(dve.scalar_tensor_tensor(row[:], ej[:], float(REGION), before[:], ALU.mult, ALU.add))
            step.run(dve.tensor_scalar(row_in[:], row[:], float(EXP * REGION), None, ALU.min))
            step.run(dve.tensor_scalar(e_i[:], ej[:], float(EXP - 1), None, ALU.min))
            step.run(dve.tensor_tensor(hot[:], c.iota8[:].unsqueeze(1).to_broadcast([P, TILES, EXP]),
                                       c.expert1[:].rearrange("p b t -> p (b t)").unsqueeze(2)
                                       .to_broadcast([P, TILES, EXP]), ALU.is_equal))
            step.run(dve.tensor_tensor(tiles[:], cum[:], tiles[:], ALU.subtract))
            step.run(dve.tensor_tensor(hot[:], hot[:], tiles[:].unsqueeze(1).to_broadcast([P, TILES, EXP]), ALU.mult))
            step.run(dve.tensor_reduce(first[:], hot[:], AX.X, ALU.add))
            step.run(dve.scalar_tensor_tensor(c.place1[:].rearrange("p b t -> p (b t)"), first[:], float(P),
                                              c.rank1[:].rearrange("p b t -> p (b t)"), ALU.mult, ALU.add))
            step.run(dve.scalar_tensor_tensor(cum[:], c.iota8[:], float(REGION), c.base1[:], ALU.mult, ALU.add))
            dve.tensor_copy(tail_i[:], cum[:]).then_inc(tables, 1)
            with dve.Fori(0, MT // UN) as i:
                for q in q4:
                    dve.wait_ge(s["x_turned"], done(i, q))
                    dve.tensor_copy(xT[q][:].rearrange("p k t -> p (k t)"), c.bank[2 * q][:, 0:D])\
                        .then_inc(s["xT_ready"], 1)
                for q in q4:
                    dve.wait_ge(s["g_turned"], done(i, q))
                    dve.tensor_copy(gT[q][:].rearrange("p k t -> p (k t)"), c.bank[2 * q][:])\
                        .then_inc(s["gT_ready"], 1)


def back(nc, c, a):
    with ExitStack() as ctx:
        sb, sem = scope(nc, ctx, "back")
        two = range(2)
        yrow = [sb(f"yrow{q}", [P, TT, D]) for q in two]
        yv = [sb(f"yv{q}", [P, TT, D]) for q in two]
        o = [sb(f"o{q}", [P, TT, D]) for q in two]
        place_now = [sb(f"place_now{q}", [P, TT], U32) for q in two]
        tv = [sb(f"tv{q}", [P, TT]) for q in two]
        norm = [Norm(sb, f"norm{q}") for q in two]
        fetched = [sem(f"fetched{q}") for q in two]
        stored = [sem(f"stored{q}") for q in two]
        copied = sem("copied")
        names = "y_scaled normed out_ready".split()
        s = {n: sem(n) for n in names}
        block = ctx.enter_context(nc.Block())

        @block.sync
        def _(sp):
            with sp.Fori(0, PAIRS) as j:
                for p in two:
                    sp.wait_ge(s["out_ready"], turn(j, p))
                    sp.dma_start(a.out[bass.ds(j * 2 + p, 1)].rearrange("b (t p) d -> p (b t) d", p=P), o[p][:])\
                        .then_inc(stored[p], 16)
            for p in two:
                sp.wait_ge(stored[p], 16 * PAIRS)

        @block.gpsimd
        def _(pool):
            with pool.Fori(0, PAIRS) as j:
                for p in two:
                    pool.wait_ge(s["y_scaled"], j * 2 * TT)
                    pool.wait_ge(fetched[p], j * (16 * TT))
                    pool.tensor_copy(place_now[p][:].unsqueeze(1), c.place1[:, bass.ds(j * 2 + p, 1), :])
                    pool.tensor_copy(tv[p][:].unsqueeze(1), c.topv[:, bass.ds(j * 2 + p, 1), :]).then_inc(copied, 1)
                    wait_apart(pool, c.passed, copied, turn(j, p))
                    for t in range(TT):
                        pool.indirect_dma_start(yrow[p][:, t, :], None, a.y1,
                                                bass.IndirectOffsetOnAxis(ap=place_now[p][:, t:t + 1], axis=0),
                                                bounds_check=MOE1_TILES * P - 1, oob_is_err=False)\
                            .then_inc(fetched[p], 16)

        @block.scalar
        def _(act):
            with act.Fori(0, PAIRS) as j:
                for p in two:
                    act.wait_ge(copied, turn(j, p))
                    act.wait_ge(fetched[p], (j + 1) * (16 * TT))
                    act.wait_ge(s["normed"], 2 * j)
                    for t in range(TT):
                        act.activation(yv[p][:, t, :], yrow[p][:, t, :], ACT.Copy, scale=tv[p][:, t:t + 1])\
                            .then_inc(s["y_scaled"], 1)

        @block.vector
        def _(dve):
            step = Steps(dve, sem("dve"), c.passed)
            with dve.Fori(0, PAIRS) as j:
                step.begin(j * BACK_STEPS)
                for p in two:
                    dve.wait_ge(s["y_scaled"], TT * j * 2 + TT * (p + 1))
                    dve.wait_ge(stored[p], 16 * j)
                    layer_norm(dve, step, o[p], yv[p], norm[p], s["normed"])
                    dve.wait_ge(s["normed"], turn(j, p))
                    step.run(dve.tensor_tensor(o[p][:], o[p][:], c.gamma[:].unsqueeze(1).to_broadcast([P, TT, D]),
                                               ALU.mult))
                    dve.tensor_tensor(o[p][:], o[p][:], c.h[:, bass.ds(j * 2 * TT + p * TT, TT), :], ALU.add)\
                        .then_inc(s["out_ready"], 1)
                assert step.n == BACK_STEPS, step.n


def lm_tower(nc, ins, out):
    a = Chip()
    a.out = out
    a.x = ins["x"]
    a.emb = [ins[f"L0_tok_emb_{i}"] for i in range(4)]
    a.proj = [ins[f"L0_tok_proj_{i}"] for i in range(4)]
    a.QK, a.VO = ins["L0_attn_QK"], ins["L0_attn_VO"]
    a.Wr, a.br = ins["L0_ffn_Wr"], ins["L0_ffn_br"]
    a.W1, a.b1, a.W2, a.b2 = (ins[f"L0_ffn_{n}"] for n in ("W1", "b1", "W2", "b2"))
    a.w_qkv, a.b_qkv, a.w_out, a.b_out, a.omega, a.nodes, a.qw = (
        ins[f"L1_attn_{n}"] for n in ("w_qkv", "b_qkv", "w_out", "b_out", "omega", "quad_nodes", "quad_weights"))
    a.gate_w, a.ew1, a.ew2, a.gamma, a.beta = (
        ins[f"L1_ffn_{n}"] for n in ("gate_w", "expert_w1", "expert_w2", "ln_gamma", "ln_beta"))
    a.xg0 = nc.dram_tensor("rows_moe2", [EXP * CAP, D], F32, kind="Internal").ap()
    a.y0 = nc.dram_tensor("out_moe2", [EXP * CAP + 1, D], F32, kind="Internal").ap()
    a.xg1 = nc.dram_tensor("rows_moe1", [EXP * REGION + P, D], F32, kind="Internal").ap()
    a.y1 = nc.dram_tensor("out_moe1", [MOE1_TILES * P, D], F32, kind="Internal").ap()
    c = Chip()
    with ExitStack() as ctx:
        sb, sem = scope(nc, ctx, "all")
        c.passed = sem("passed")
        MT = MOE1_TILES
        c.ps = ctx.enter_context(nc.psum_tensor("banks", [P, 8, 512], F32))
        c.bank = [c.ps[:, k, :] for k in range(8)]
        c.h = sb("h", [P, TILES, D])
        c.zero = sb("zero", [P, D])
        c.ident, c.ones, c.before = (sb(n, [P, P]) for n in ("ident", "ones", "before"))
        c.causal = sb("causal", [P, 3, P])
        c.iota8 = sb("iota8", [P, EXP])
        c.tile_no = sb("tile_no", [P, MT])
        c.place0 = sb("place0", [P, B, 2 * TT], U32)
        c.gates = sb("gates", [P, B, 2 * TT])
        c.expert1, c.rank1 = sb("expert1", [P, B, TT]), sb("rank1", [P, B, TT])
        c.place1 = sb("place1", [P, B, TT], U32)
        c.topv = sb("topv", [P, B, TT])
        c.base0, c.base1 = sb("base0", [P, EXP]), sb("base1", [P, EXP])
        c.Wr, c.br = sb("Wr", [P, DC, EXP]), sb("br", [P, EXP])
        c.wqkvT, c.bqkv = sb("wqkvT", [P, DC, 3 * D]), sb("bqkv", [P, 3 * D])
        c.woutT, c.bout = sb("woutT", [P, DC, D]), sb("bout", [P, D])
        c.omega = sb("omega", [P, DC, P])
        c.nodes, c.qw = sb("nodes", [P, 2]), sb("qw", [P, 2])
        c.f_scale, c.f_shift, c.f_weight = (sb(n, [P, 1]) for n in ("f_scale", "f_shift", "f_weight"))
        c.b1T = sb("b1T", [P, EXP * HID0 // P])
        c.gateT = sb("gateT", [P, DC, EXP])
        c.gamma, c.beta = sb("gamma", [P, D]), sb("beta", [P, D])
        c.vone = [sb(f"vone{q}", [P, TT, HEADS, HD + 1]) for q in range(2)]
        with ExitStack() as early:
            sb, _ = scope(nc, early, "early")
            c.cat = [sb(f"cat{q}", [P, TT, CAT]) for q in range(2)]
            c.token_row = sb("token_row", [P, 4, TILES], U32)
            c.projT = sb("projT", [P, KC, D])
            c.QK, c.VO = sb("QK", [P, DC, D]), sb("VO", [P, DC, D])
            setup(nc, c, a)
            front(nc, c, a)
        moe2(nc, c, a)
        with ExitStack() as late:
            sb, _ = scope(nc, late, "late")
            c.W1, c.W2 = sb("W1", [P, DC * EXP, HID1]), sb("W2", [P, HID1 // P * EXP, D])
            middle(nc, c, a)
            moe1(nc, c, a)
            back(nc, c, a)


_INS = ['x', 'L0_tok_emb_0', 'L0_tok_emb_1', 'L0_tok_emb_2', 'L0_tok_emb_3', 'L0_tok_proj_0', 'L0_tok_proj_1',
        'L0_tok_proj_2', 'L0_tok_proj_3', 'L0_attn_QK', 'L0_attn_VO', 'L0_ffn_Wr', 'L0_ffn_br', 'L0_ffn_W1',
        'L0_ffn_b1', 'L0_ffn_W2', 'L0_ffn_b2', 'L1_attn_w_qkv', 'L1_attn_b_qkv', 'L1_attn_w_out', 'L1_attn_b_out',
        'L1_attn_omega', 'L1_attn_quad_nodes', 'L1_attn_quad_weights', 'L1_ffn_gate_w', 'L1_ffn_expert_w1',
        'L1_ffn_expert_w2', 'L1_ffn_ln_gamma', 'L1_ffn_ln_beta']


def kernel(**inputs):
    import numpy as _np
    import concourse.bacc as _bacc
    from concourse import mybir as _mybir
    from concourse.bass_utils import run_bass_kernel_spmd as _run

    nc = _bacc.Bacc("TRN2", target_bir_lowering=False, num_devices=1)
    arrays, args = {}, {}
    for name in _INS:
        arr = _np.ascontiguousarray(inputs[name])
        arrays[f"in_{name}_dram"] = arr
        args[name] = nc.dram_tensor(f"in_{name}_dram", arr.shape, _mybir.dt.from_np(arr.dtype), kind="ExternalInput").ap()
    out = nc.dram_tensor("out_0_dram", (B, T, D), _mybir.dt.from_np(_np.dtype("float32")), kind="ExternalOutput").ap()
    lm_tower(nc, args, out)
    r = _run(nc, [arrays], core_ids=[0])
    return r.results[0]["out_0_dram"]
```

```python
from contextlib import ExitStack

import concourse.bass as bass
from concourse import mybir

F32 = mybir.dt.float32
I32 = mybir.dt.int32
U32 = mybir.dt.uint32
ALU = mybir.AluOpType
ACT = mybir.ActivationFunctionType
AX = mybir.AxisListType

P = 128
B, T, D = 16, 256, 256
PAIRS = B // 2
TT = T // P
PT = 2 * TT
N = B * T
TILES = N // P
DC = D // P
CUTS = [0, 5000, 10000, 50000, 267735]
EMB_D = [256, 64, 64, 16]
EMB_AT = [0, 256, 320, 384]
CAT = 512
KC = CAT // P
NOWHERE = 1 << 20
EXP = 8
HID0, CAP = 1024, N * 2 // EXP
HID1 = 512
HEADS, HD, FEAT = 16, 16, 32
NF = 2 * FEAT
REGION = N + P
MOE1_FLIGHT = 4
MOE1_TILES = -(-((N + EXP * (P - 1)) // P) // MOE1_FLIGHT) * MOE1_FLIGHT
LN_EPS = 1e-5
ATT_SCALE = 1.0 / D ** 0.5
EMB_SCALE = float(D) ** 0.5
RSQRT_MAGIC = 0x5F3759DF
EXP_LO, EXP_HI = 2.061153622438558e-09, 485165195.4097903
FRONT_STEPS, PREPARE_STEPS, HEADS_STEPS, SELECT_STEPS, BACK_STEPS = 71, 43, 2, 42, 50


def turn(j, p):
    return 2 * j + p + 1


def wait_apart(eng, passed, sem, value):
    eng.wait_ge(sem, value)
    eng.sem_inc(passed, 1)


class Steps:

    def __init__(self, eng, sem, passed):
        self.eng, self.sem, self.passed, self.base, self.n = eng, sem, passed, 0, 0

    def begin(self, base):
        self.base, self.n = base, 0

    def __call__(self, ins):
        ins.then_inc(self.sem, 1)
        self.n += 1

    def wait(self):
        self.eng.wait_ge(self.sem, self.base + self.n)

    def wait_apart(self):
        wait_apart(self.eng, self.passed, self.sem, self.base + self.n)

    def run(self, ins):
        self(ins)
        self.wait()


class Chip:
    pass


def rsqrt(dve, step, out, val, tmp):
    step.run(dve.tensor_scalar(out.bitcast(I32), val.bitcast(I32), 1, None, ALU.logical_shift_right))
    step.run(dve.tensor_scalar(out.bitcast(I32), out.bitcast(I32), -1.0, float(RSQRT_MAGIC), ALU.mult, ALU.add))
    for _ in range(3):
        step.run(dve.scalar_tensor_tensor(tmp, out, -0.5, out, ALU.mult, ALU.mult))
        step.run(dve.tensor_tensor(tmp, tmp, val, ALU.mult))
        step.run(dve.scalar_tensor_tensor(out, tmp, 1.5, out, ALU.add, ALU.mult))


def layer_norm(dve, step, out, x, w, last=None):
    for t in range(TT):
        step(dve.bn_stats(w.stats[:, t, :], x[:, t, :]))
    step.wait_apart()
    for t in range(TT):
        step(dve.bn_aggr(w.mv[:, t, :], w.stats[:, t, :]))
    step.wait()
    step.run(dve.tensor_scalar(w.var[:], w.mv[:, :, 1], LN_EPS, None, ALU.add))
    rsqrt(dve, step, w.rstd[:], w.var[:], w.tmp[:])
    for t in range(TT):
        ins = dve.tensor_scalar(out[:, t, :], x[:, t, :], w.mv[:, t, 0:1], w.rstd[:, t:t + 1],
                                ALU.subtract, ALU.mult)
        if last is not None and t == TT - 1:
            ins.then_inc(last, 1)
        else:
            step(ins)


class Norm:

    def __init__(self, sb, name):
        self.stats = sb(f"{name}_stats", [P, TT, 6])
        self.mv = sb(f"{name}_mv", [P, TT, 2])
        self.var = sb(f"{name}_var", [P, TT])
        self.rstd = sb(f"{name}_rstd", [P, TT])
        self.tmp = sb(f"{name}_tmp", [P, TT])


def scope(nc, ctx, prefix):
    def sb(name, shape, dt=F32):
        return ctx.enter_context(nc.sbuf_tensor(f"{prefix}_{name}", shape, dt))

    def sem(name):
        return ctx.enter_context(nc.semaphore(f"{prefix}_{name}"))

    return sb, sem


def rows(ap):
    n = ap.shape[0]
    return ap.rearrange("(a n) -> a n", a=1).to_broadcast([P, n])


def setup(nc, c, a):
    with ExitStack() as ctx:
        sb, sem = scope(nc, ctx, "set")
        ids = sb("ids", [TILES, P], I32)
        ids_f = sb("ids_f", [TILES, P])
        idt = sb("idt", [P, TILES])
        sel = sb("sel", [P, 2, TILES])
        proj = sb("proj", [P, DC, CAT])
        wqkv = sb("wqkv", [P, 6, D])
        wout = sb("wout", [P, DC, D])
        gate = sb("gate", [EXP, D])
        b1 = sb("b1", [EXP * HID0 // P, P])
        zeros = sb("zeros", [P, 2048])
        ld = sem("loaded")
        loads = 0
        z = sem("zeroed")
        consts = sem("consts")
        turned = sem("turned")
        moved = sem("moved")
        direct = sem("direct")
        own = sem("own")
        om_zero = sem("om_zero")
        om_ld = sem("om_loaded")
        zero_rows = sem("zero_rows")

        jobs = [(c.projT[:, k, DC0 * P:(DC0 + 1) * P], proj[:, DC0, k * P:(k + 1) * P])
                for DC0 in range(DC) for k in range(KC)]
        jobs += [(c.wqkvT[:, k, m * P:(m + 1) * P], wqkv[:, m, k * P:(k + 1) * P])
                 for m in range(6) for k in range(DC)]
        jobs += [(c.woutT[:, k, m * P:(m + 1) * P], wout[:, m, k * P:(k + 1) * P])
                 for m in range(DC) for k in range(DC)]
        jobs += [(c.gateT[:, k, :], gate[:, k * P:(k + 1) * P]) for k in range(DC)]
        jobs += [(c.b1T[:], b1[:])]
        LOADS = 4 + 1 + 1 + 1 + 1 + 1
        block = ctx.enter_context(nc.Block())

        @block.sync
        def _(sp):
            sp.dma_start(ids[:], a.x.rearrange("b (u p) -> (b u) p", p=P)).then_inc(ld, 16)
            sp.wait_ge(z, 1)
            for i in range(4):
                sp.dma_start(proj[:, :, EMB_AT[i]:EMB_AT[i] + EMB_D[i]],
                             a.proj[i].rearrange("(u p) d -> p u d", p=P)).then_inc(ld, 16)
            sp.dma_start(wqkv[:], a.w_qkv.rearrange("(u p) d -> p u d", p=P)).then_inc(ld, 16)
            sp.dma_start(wout[:], a.w_out.rearrange("(u p) d -> p u d", p=P)).then_inc(ld, 16)
            sp.dma_start(gate[:], a.gate_w).then_inc(ld, 16)
            sp.dma_start(b1[:], a.b1.rearrange("e (m p) -> (e m) p", p=P)).then_inc(ld, 16)
            sp.dma_start(c.QK[:], a.QK.rearrange("(k p) n -> p k n", p=P)).then_inc(direct, 16)
            sp.dma_start(c.VO[:], a.VO.rearrange("(k p) n -> p k n", p=P)).then_inc(direct, 16)
            sp.dma_start(c.Wr[:], a.Wr.rearrange("(k p) n -> p k n", p=P)).then_inc(direct, 16)
            for buf, src in ((c.br, a.br), (c.bqkv, a.b_qkv), (c.bout, a.b_out), (c.gamma, a.gamma),
                             (c.beta, a.beta), (c.nodes, a.nodes), (c.qw, a.qw)):
                sp.dma_start(buf[:], rows(src)).then_inc(direct, 16)
            sp.wait_ge(zero_rows, 1)
            per = 2048 // D * P
            for i in range(EXP * CAP // per):
                sp.dma_start(a.xg0[i * per:(i + 1) * per, :].rearrange("(p r) d -> p (r d)", p=P),
                             zeros[:]).then_inc(direct, 16)
            sp.dma_start(a.y0[EXP * CAP:EXP * CAP + 1, :], zeros[0:1, 0:D]).then_inc(direct, 16)
            sp.dma_start(a.xg1[EXP * REGION:EXP * REGION + P, :], zeros[:, 0:D]).then_inc(direct, 16)
            sp.wait_ge(om_zero, 1)
            for h in range(HEADS):
                r0 = HD * (h % 8)
                hh = h % 2
                sp.dma_start(c.omega[r0:r0 + HD, h // 2, hh * NF:(hh + 1) * NF].rearrange(
                    "d (r m) -> d r m", r=2), a.omega[:, h].rearrange("r d m -> d r m")).then_inc(om_ld, 16)
            sp.wait_ge(om_ld, 16 * HEADS)
            sp.wait_ge(direct, 16 * (10 + EXP * CAP // per + 2))

        @block.gpsimd
        def _(pool):
            pool.memset(proj[:], 0.0).then_inc(z, 1)
            pool.memset(c.omega[:], 0.0).then_inc(om_zero, 1)
            pool.memset(c.ident[:], 0.0).then_inc(own, 1)
            pool.memset(c.ones[:], 1.0).then_inc(own, 1)
            pool.iota(c.iota8[:], [[1, EXP]], base=0, channel_multiplier=0,
                      allow_small_or_imprecise_dtypes=True).then_inc(own, 1)
            pool.iota(c.tile_no[:], [[1, MOE1_TILES]], base=0, channel_multiplier=0,
                      allow_small_or_imprecise_dtypes=True).then_inc(own, 1)
            pool.wait_ge(own, 4)
            pool.affine_select(out=c.ident[:], in_=c.ident[:], compare_op=ALU.not_equal, fill=1.0, base=0,
                               pattern=[[-1, P]], channel_multiplier=1).then_inc(consts, 1)
            pool.affine_select(out=c.before[:], in_=c.ones[:], compare_op=ALU.is_gt, fill=0.0, base=0,
                               pattern=[[1, P]], channel_multiplier=-1).then_inc(own, 1)
            for b in (0, 2):
                pool.affine_select(out=c.causal[:, b, :], in_=c.ones[:], compare_op=ALU.is_ge, fill=0.0, base=0,
                                   pattern=[[1, P]], channel_multiplier=-1)
            pool.tensor_copy(c.causal[:, 1, :], c.ones[:]).then_inc(own, 1)
            pool.wait_ge(own, 6)

        @block.tensor
        def _(pe):
            pe.wait_ge(consts, 1)
            pe.wait_ge(own, 7)
            pe.transpose(c.bank[7][:, 0:TILES], ids_f[:], c.ident[0:TILES, 0:TILES]).then_inc(turned, 1)
            pe.wait_ge(ld, 16 * LOADS)
            for n in range(0, len(jobs), 4):
                if n >= 28:
                    pe.wait_ge(moved, n - 24)
                for k, (dst, src) in enumerate(jobs[n:n + 4]):
                    m = src.shape[0]
                    ins = pe.transpose(c.bank[n // 4 % 7][:, k * P:k * P + m], src, c.ident[0:m, 0:m])
                ins.then_inc(turned, 1)

        @block.vector
        def _(dve):
            step = Steps(dve, sem("dve"), c.passed)
            dve.memset(zeros[:], 0.0).then_inc(zero_rows, 1)
            step(dve.memset(c.zero[:], 0.0))
            step(dve.memset(c.base0[:], 0.0))
            step(dve.memset(c.base1[:], 0.0))
            dve.wait_ge(ld, 16 * LOADS)
            dve.wait_ge(own, 6)
            dve.tensor_copy(ids_f[:], ids[:]).then_inc(own, 1)
            dve.wait_ge(turned, 1)
            step.run(dve.tensor_copy(idt[:], c.bank[7][:, 0:TILES]))
            for i in range(4):
                lo, hi = float(CUTS[i]), float(CUTS[i + 1])
                step.run(dve.tensor_scalar(sel[:, 0, :], idt[:], lo, None, ALU.is_ge))
                step.run(dve.tensor_scalar(sel[:, 1, :], idt[:], hi, None, ALU.is_lt))
                step.run(dve.tensor_tensor(sel[:, 0, :], sel[:, 0, :], sel[:, 1, :], ALU.mult))
                step.run(dve.tensor_scalar(sel[:, 1, :], idt[:], -(lo + NOWHERE), None, ALU.add))
                step.run(dve.tensor_tensor(sel[:, 0, :], sel[:, 0, :], sel[:, 1, :], ALU.mult))
                step.run(dve.tensor_scalar(c.token_row[:, i, 0:TILES], sel[:, 0, :], float(NOWHERE), None, ALU.add))
            for n in range(0, len(jobs), 4):
                dve.wait_ge(turned, n // 4 + 2)
                for k, (dst, src) in enumerate(jobs[n:n + 4]):
                    m = src.shape[0]
                    dve.tensor_copy(dst, c.bank[n // 4 % 7][:, k * P:k * P + m]).then_inc(moved, 1)
            dve.wait_ge(direct, 16 * (10 + EXP * CAP * D // (2048 * P) + 2))
            clip = sb("clip", [P, 2])
            root = sb("root", [P, 2])
            tmp = sb("root_tmp", [P, 2])
            big = sb("root_big", [P, 2])
            for src, scale, dst in ((c.nodes, 2.0, c.f_scale), (c.qw, 1.0, c.f_weight)):
                step.run(dve.tensor_scalar(clip[:], src[:], 0.0, scale, ALU.max, ALU.mult))
                step.run(dve.tensor_scalar(big[:], clip[:], 1e-30, None, ALU.max))
                rsqrt(dve, step, root[:], big[:], tmp[:])
                step.run(dve.tensor_tensor(root[:], root[:], clip[:], ALU.mult))
                f = 1.0 if dst is c.f_scale else 1.0 / FEAT
                for g in range(4):
                    step.run(dve.tensor_scalar(dst[g * 32:(g + 1) * 32, :], root[g * 32:(g + 1) * 32, g % 2:g % 2 + 1],
                                               f, None, ALU.mult))
            for g in range(4):
                step.run(dve.tensor_scalar(c.f_shift[g * 32:(g + 1) * 32, :],
                                           c.nodes[g * 32:(g + 1) * 32, g % 2:g % 2 + 1], -1.0, None, ALU.mult))


def first(i):
    return isinstance(i, int) and i == 0


def pair_tiles(ap, j, n=None):
    if n is None:
        return ap[:, bass.ds(j * PT, PT), :] if not isinstance(j, int) else ap[:, j * PT:(j + 1) * PT, :]
    return ap[:, bass.ds(j * PT + n, 1), :] if not isinstance(j, int) else ap[:, j * PT + n:j * PT + n + 1, :]


def two_tiles(ap, j, p):
    return ap[:, bass.ds(j * PT + p * TT, TT), :] if not isinstance(j, int) else \
        ap[:, j * PT + p * TT:j * PT + (p + 1) * TT, :]


class PairNorm:

    def __init__(self, sb, name):
        self.stats = sb(f"{name}_stats", [P, PT, 6])
        self.mv = sb(f"{name}_mv", [P, PT, 2])
        self.var = sb(f"{name}_var", [P, PT])
        self.rstd = sb(f"{name}_rstd", [P, PT])
        self.tmp = sb(f"{name}_tmp", [P, PT])


def pair_norm(dve, step, out, x, w, last, before_out=None):
    for n in range(PT):
        step(dve.bn_stats(w.stats[:, n, :], x(n)))
    step.wait_apart()
    for n in range(PT):
        step(dve.bn_aggr(w.mv[:, n, :], w.stats[:, n, :]))
    step.wait()
    step.run(dve.tensor_scalar(w.var[:], w.mv[:, :, 1], LN_EPS, None, ALU.add))
    rsqrt(dve, step, w.rstd[:], w.var[:], w.tmp[:])
    if before_out is not None:
        before_out()
    for n in range(PT):
        ins = dve.tensor_scalar(out(n), x(n), w.mv[:, n, 0:1], w.rstd[:, n:n + 1], ALU.subtract, ALU.mult)
        if n == PT - 1:
            ins.then_inc(last, 1)
        else:
            step(ins)


class PairRouting:

    def __init__(self, sb, K):
        self.best = sb("best", [P, PT, 8])
        self.best_at = sb("best_at", [P, PT, 8], U32)
        self.expert = sb("expert", [P, K, PT])
        self.hot = sb("hot", [P, K, PT, EXP])
        self.took = sb("took", [P, PT, EXP])
        self.pos = sb("pos", [P, PT, EXP])
        self.taken = sb("taken", [P, K, PT, EXP])
        self.rank = sb("rank", [P, K * PT])
        self.slot = sb("slot", [P, K * PT])
        self.slot_i = sb("slot_i", [P, K * PT], U32)
        self.logits = sb("logits", [P, PT, EXP])


def pair_route(dve, step, w, K):
    step.wait_apart()
    for n in range(PT):
        step(dve.max(w.best[:, n, :], w.logits[:, n, :]))
    step.wait_apart()
    for n in range(PT):
        step(dve.max_index(w.best_at[:, n, :], w.best[:, n, :], w.logits[:, n, :]))
    step.wait()
    step.run(dve.tensor_copy(w.expert[:], w.best_at[:, :, 0:K].rearrange("p t k -> p k t")))


def pair_ranks(pe, c, psum, took):
    for n in range(PT + 1):
        out = psum[:, n * EXP:(n + 1) * EXP]
        if n < PT:
            ins = pe.matmul(out, c.before[:], took[:, n, :], start=True, stop=n == 0)
        for m in range(n):
            ins = pe.matmul(out, c.ones[:], took[:, m, :], start=n == PT and m == 0, stop=m == n - 1)
    return ins


def pair_places(dve, step, w, K, base, psum, stride, limit, dump, done):
    step.run(dve.tensor_tensor(w.pos[:], psum[:, 0:PT * EXP].rearrange("p (t e) -> p t e", t=PT),
                               base[:].unsqueeze(1).to_broadcast([P, PT, EXP]), ALU.add))
    step(dve.tensor_tensor(base[:], base[:], psum[:, PT * EXP:(PT + 1) * EXP], ALU.add))
    for k in range(K):
        step(dve.tensor_tensor(w.taken[:, k], w.hot[:, k], w.pos[:], ALU.mult))
    step.wait()
    step.run(dve.tensor_reduce(w.rank[:], w.taken[:].rearrange("p k t e -> p (k t) e"), AX.X, ALU.add))
    ex = w.expert[:].rearrange("p k t -> p (k t)")
    step.run(dve.scalar_tensor_tensor(w.slot[:], ex, float(stride), w.rank[:], ALU.mult, ALU.add))
    if limit is None:
        dve.tensor_copy(w.slot_i[:], w.slot[:]).then_inc(done, 1)
        return
    step.run(dve.tensor_scalar(w.rank[:], w.rank[:], float(limit), None, ALU.is_lt))
    step.run(dve.scalar_tensor_tensor(w.slot[:], w.slot[:], -float(dump), w.rank[:], ALU.add, ALU.mult))
    dve.tensor_scalar(w.slot_i[:], w.slot[:], float(dump), None, ALU.add).then_inc(done, 1)


def turn_tiles(pe, c, psum, x, chunks):
    for k in range(chunks):
        for t in range(TT):
            ins = pe.transpose(psum[:, k * T + t * P:k * T + (t + 1) * P], x[:, t, k * P:(k + 1) * P], c.ident[:])
    return ins


def front(nc, c, a):
    with ExitStack() as ctx:
        sb, sem = scope(nc, ctx, "front")
        two = range(2)
        row_now = sb("row_now", [P, 4, PT], U32)
        catT = [sb(f"catT{q}", [P, KC, T]) for q in two]
        xn_next = sb("xn_next", [P, PT, D])
        xn = sb("xn", [P, PT, D])
        xn2 = sb("xn2", [P, PT, D])
        rows_out = sb("rows_out", [P, PT, D])
        xT = [sb(f"xT{q}", [P, DC, T]) for q in two]
        x2T = [sb(f"x2T{q}", [P, DC, T]) for q in two]
        qT = [sb(f"qT{q}", [P, DC, T]) for q in two]
        prob = [sb(f"prob{q}", [P, TT, T]) for q in two]
        probT = [sb(f"probT{q}", [P, TT, T]) for q in two]
        avT = [sb(f"avT{q}", [P, DC, T]) for q in two]
        norm, norm2 = PairNorm(sb, "norm"), PairNorm(sb, "norm2")
        smax = sb("smax", [P, PT])
        nmax = sb("nmax", [P, PT])
        total = sb("total", [P, PT])
        w = PairRouting(sb, 2)
        gap = sb("gap", [P, PT])
        egap = sb("egap", [P, PT])
        gate = sb("gate", [P, 2, PT])
        SEMS = ("indexed cleared cat_turned catT_ready emb_ready h_ready x_ready x_kept x_turned xT_ready "
                "q_made qT_ready s_made nmax_ready prob_ready p_turned pT_ready av_made avT_ready o_made o_part o_added "
                "x2_ready x2_turned x2T_ready rows_ready l_made took_ready r_made slots_ready gap_ready egap_ready "
                "kept").split()
        s = {n: sem(n) for n in SEMS}
        gathered = sem("gathered")
        sent = sem("sent")
        block = ctx.enter_context(nc.Block())
        Q, S, E, X = 0, 2, 4, 6

        def flat(x):
            return x[:].rearrange("p k t -> p (k t)")

        @block.gpsimd
        def _(pool):
            def gather(j):
                wait_apart(pool, c.passed, s["indexed"], j + 1)
                wait_apart(pool, c.passed, s["cleared"], j + 1)
                for i in range(4):
                    for n in range(PT):
                        pool.indirect_dma_start(
                            c.cat[:, n, EMB_AT[i]:EMB_AT[i] + EMB_D[i]], None, a.emb[i],
                            bass.IndirectOffsetOnAxis(ap=row_now[:, i, n:n + 1], axis=0),
                            bounds_check=CUTS[i + 1] - CUTS[i] - 1, oob_is_err=False).then_inc(gathered, 16)

            def send(j):
                wait_apart(pool, c.passed, s["rows_ready"], j + 1)
                wait_apart(pool, c.passed, s["slots_ready"], j + 1)
                for k in two:
                    for n in range(PT):
                        pool.indirect_dma_start(
                            a.xg0, bass.IndirectOffsetOnAxis(ap=w.slot_i[:, k * PT + n:k * PT + n + 1], axis=0),
                            rows_out[:, n, :], None, bounds_check=EXP * CAP - 1,
                            oob_is_err=False).then_inc(sent, 16)
                pool.tensor_copy(c.place0[:, bass.ds(j, 1), :], w.slot_i[:].unsqueeze(1))
                pool.tensor_copy(c.gates[:, bass.ds(j, 1), :], gate[:].rearrange("p (a k) n -> p a (k n)", a=1))\
                    .then_inc(s["kept"], 1)

            with pool.Fori(0, 3) as j:
                gather(j)
            with pool.Fori(1, PAIRS - 2) as j:
                gather(j + 2)
                send(j - 1)
            with pool.Fori(PAIRS - 3, PAIRS) as j:
                send(j)
            pool.wait_ge(sent, 16 * 2 * PT * PAIRS)

        @block.tensor
        def _(pe):
            def turn_rows(j, p):
                if p == 0:
                    pe.wait_ge(gathered, (j + 1) * (16 * 4 * PT))
                    if not first(j):
                        pe.wait_ge(s["h_ready"], turn(j - 1, 1))
                else:
                    pe.wait_ge(s["catT_ready"], turn(j, 0))
                for k in range(KC):
                    for t in range(TT):
                        ins = pe.transpose(c.bank[E + k // 2][:, (k % 2) * T + t * P:(k % 2) * T + (t + 1) * P],
                                           c.cat[:, p * TT + t, k * P:(k + 1) * P], c.ident[:])
                ins.then_inc(s["cat_turned"], 1)

            def embed(j, p):
                pe.wait_ge(s["catT_ready"], turn(j, 1))
                for t in range(TT):
                    for k in range(KC):
                        ins = pe.matmul(c.bank[E + p][:, t * D:(t + 1) * D], catT[p][:, k, t * P:(t + 1) * P],
                                        c.projT[:, k, :], start=k == 0, stop=k == KC - 1)
                ins.then_inc(s["emb_ready"], 1)

            def turn_x(j):
                pe.wait_ge(s["x_ready"], j + 1)
                for p in two:
                    turn_tiles(pe, c, c.bank[X + p], xn_next[:, p * TT:(p + 1) * TT], DC).then_inc(s["x_turned"], 1)

            def queries(j):
                if not first(j):
                    pe.wait_ge(s["o_added"], j)
                for p in two:
                    pe.wait_ge(s["xT_ready"], turn(j, p))
                    for m in range(DC):
                        for k in range(DC):
                            ins = pe.matmul(c.bank[Q + p][:, m * T:(m + 1) * T], c.QK[:, k, m * P:(m + 1) * P],
                                            xT[p][:, k, :], start=k == 0, stop=k == DC - 1)
                    ins.then_inc(s["q_made"], 1)

            def scores(j):
                for p in two:
                    pe.wait_ge(s["qT_ready"], turn(j, p))
                    for t in range(TT):
                        for k in range(DC):
                            ins = pe.matmul(c.bank[S + p][:, t * T:(t + 1) * T], qT[p][:, k, t * P:(t + 1) * P],
                                            xT[p][:, k, :], start=k == 0, stop=k == DC - 1)
                ins.then_inc(s["s_made"], 1)

            def turn_x2(j):
                pe.wait_ge(s["x2_ready"], j + 1)
                for p in two:
                    turn_tiles(pe, c, c.bank[X + p], xn2[:, p * TT:(p + 1) * TT], DC).then_inc(s["x2_turned"], 1)

            def router(j):
                pe.wait_ge(s["x2T_ready"], turn(j, 1))
                for n in range(PT):
                    for k in range(DC):
                        t = n % TT
                        ins = pe.matmul(c.bank[X][:, n * EXP:(n + 1) * EXP], x2T[n // TT][:, k, t * P:(t + 1) * P],
                                        c.Wr[:, k, :], start=k == 0, stop=k == DC - 1)
                ins.then_inc(s["l_made"], 1)

            def average(j):
                for p in two:
                    pe.wait_ge(s["prob_ready"], j * PT + (p + 1) * TT)
                    turn_tiles(pe, c, c.bank[Q + p], prob[p], TT).then_inc(s["p_turned"], 1)
                for p in two:
                    pe.wait_ge(s["pT_ready"], turn(j, p))
                    if p == 0:
                        pe.wait_ge(s["x_kept"], j + 1)
                    for m in range(DC):
                        for k in range(TT):
                            ins = pe.matmul(c.bank[S + p][:, m * T:(m + 1) * T],
                                            xn[:, p * TT + k, m * P:(m + 1) * P],
                                            probT[p][:, k, :], start=k == 0, stop=k == TT - 1)
                    ins.then_inc(s["av_made"], 1)

            def project(j):
                for p in two:
                    pe.wait_ge(s["avT_ready"], turn(j, p))
                    for t in range(TT):
                        for k in range(DC):
                            ins = pe.matmul(c.bank[Q + p][:, t * D:(t + 1) * D], avT[p][:, k, t * P:(t + 1) * P],
                                            c.VO[:, k, :], start=k == 0, stop=k == DC - 1)
                ins.then_inc(s["o_made"], 1)

            def ranks(j):
                pe.wait_ge(s["took_ready"], j + 1)
                pair_ranks(pe, c, c.bank[X + 1], w.took).then_inc(s["r_made"], 1)

            def pair(j, before, after):
                queries(j)
                if after:
                    turn_rows(j + 1, 0)
                scores(j)
                if after:
                    turn_rows(j + 1, 1)
                if before:
                    turn_x2(j - 1)
                if after:
                    embed(j + 1, 0)
                if before:
                    router(j - 1)
                if after:
                    embed(j + 1, 1)
                average(j)
                project(j)
                if before:
                    ranks(j - 1)
                if after:
                    if before:
                        pe.wait_ge(s["slots_ready"], j)
                    turn_x(j + 1)

            turn_rows(0, 0)
            turn_rows(0, 1)
            embed(0, 0)
            embed(0, 1)
            turn_x(0)
            pair(0, False, True)
            with pe.Fori(1, PAIRS - 1) as j:
                pair(j, True, True)
            pair(PAIRS - 1, True, False)
            turn_x2(PAIRS - 1)
            router(PAIRS - 1)
            ranks(PAIRS - 1)

        @block.scalar
        def _(act):
            def copy_rows(j, p):
                act.wait_ge(s["cat_turned"], turn(j, p))
                if not first(j):
                    act.wait_ge(s["emb_ready"], turn(j - 1, p))
                act.activation(catT[p][:].rearrange("p (b k) t -> p b (k t)", b=2), c.ps[:, E:E + 2, :], ACT.Copy)\
                    .then_inc(s["catT_ready"], 1)

            def hidden(j, p):
                wait_apart(act, c.passed, s["emb_ready"], turn(j, p))
                act.activation(two_tiles(c.h, j, p), c.bank[E + p][:].rearrange("p (t d) -> p t d", t=TT), ACT.Copy,
                               scale=EMB_SCALE).then_inc(s["h_ready"], 1)

            def copy_x(j):
                for p in two:
                    act.wait_ge(s["x_turned"], turn(j, p))
                    act.activation(flat(xT[p]), c.bank[X + p][:], ACT.Copy).then_inc(s["xT_ready"], 1)
                if not first(j):
                    act.wait_ge(s["av_made"], turn(j - 1, 1))
                act.activation(xn[:], xn_next[:], ACT.Copy).then_inc(s["x_kept"], 1)

            def rows_copy(j):
                if not first(j):
                    act.wait_ge(sent, j * (16 * 2 * PT))
                act.activation(rows_out[:], xn2[:], ACT.Copy).then_inc(s["rows_ready"], 1)

            def copy_x2(j):
                for p in two:
                    act.wait_ge(s["x2_turned"], turn(j, p))
                    act.activation(flat(x2T[p]), c.bank[X + p][:], ACT.Copy).then_inc(s["x2T_ready"], 1)

            def egaps(j):
                act.wait_ge(s["gap_ready"], j + 1)
                act.activation(egap[:], gap[:], ACT.Exp).then_inc(s["egap_ready"], 1)

            def pair(j, before, after):
                for p in two:
                    act.wait_ge(s["q_made"], turn(j, p))
                    act.activation(flat(qT[p]), c.bank[Q + p][:], ACT.Copy).then_inc(s["qT_ready"], 1)
                if after:
                    copy_rows(j + 1, 0)
                    copy_rows(j + 1, 1)
                act.wait_ge(s["nmax_ready"], j + 1)
                for n in range(PT):
                    t = n % TT
                    act.activation(prob[n // TT][:, t, :], c.bank[S + n // TT][:, t * T:(t + 1) * T], ACT.Exp,
                                   bias=nmax[:, n:n + 1], scale=ATT_SCALE,
                                   accum_out=total[:, n:n + 1]).then_inc(s["prob_ready"], 1)
                if before:
                    copy_x2(j - 1)
                if after:
                    hidden(j + 1, 0)
                    hidden(j + 1, 1)
                if before:
                    rows_copy(j - 1)
                for p in two:
                    act.wait_ge(s["p_turned"], turn(j, p))
                    act.activation(flat(probT[p]), c.bank[Q + p][:], ACT.Copy).then_inc(s["pT_ready"], 1)
                if before:
                    egaps(j - 1)
                for p in two:
                    act.wait_ge(s["av_made"], turn(j, p))
                    act.activation(flat(avT[p]), c.bank[S + p][:], ACT.Copy).then_inc(s["avT_ready"], 1)
                if after:
                    copy_x(j + 1)

            copy_rows(0, 0)
            copy_rows(0, 1)
            hidden(0, 0)
            hidden(0, 1)
            copy_x(0)
            pair(0, False, True)
            with act.Fori(1, PAIRS - 1) as j:
                pair(j, True, True)
            pair(PAIRS - 1, True, False)
            copy_x2(PAIRS - 1)
            rows_copy(PAIRS - 1)
            egaps(PAIRS - 1)

        @block.vector
        def _(dve):
            step = Steps(dve, sem("dve"), c.passed)

            def index(j):
                at = bass.ds(j * PT, PT) if not isinstance(j, int) else slice(j * PT, (j + 1) * PT)
                dve.tensor_copy(row_now[:], c.token_row[:, :, at]).then_inc(s["indexed"], 1)

            def clear(j):
                dve.wait_ge(s["cat_turned"], turn(j - 1, 1))
                dve.memset(c.cat[:, :, 0:400], 0.0).then_inc(s["cleared"], 1)
                index(j)

            def norm_x(j):
                wait_apart(dve, c.passed, s["h_ready"], turn(j, 1))

                def free():
                    if not first(j):
                        dve.wait_ge(s["x_kept"], j)
                        dve.wait_ge(s["x_turned"], turn(j - 1, 1))
                pair_norm(dve, step, lambda n: xn_next[:, n:n + 1, :], lambda n: pair_tiles(c.h, j, n), norm,
                          s["x_ready"], free)

            def maxima(j):
                dve.wait_ge(s["s_made"], j + 1)
                step.run(dve.tensor_reduce(smax[:], c.ps[:, S:S + 2, :].rearrange("p s (t u) -> p (s t) u", t=TT),
                                           AX.X, ALU.max))
                dve.tensor_scalar(nmax[:], smax[:], -ATT_SCALE, None, ALU.mult).then_inc(s["nmax_ready"], 1)

            def add_norm(j):
                step.run(dve.reciprocal(total[:], total[:]))
                dve.wait_ge(s["o_made"], j + 1)
                for n in range(PT):
                    hn = pair_tiles(c.h, j, n)
                    t = n % TT
                    dve.scalar_tensor_tensor(
                        hn, c.bank[Q + n // TT][:, t * D:(t + 1) * D].unsqueeze(1), total[:, n:n + 1], hn,
                        ALU.mult, ALU.add).then_inc(s["o_part"], 1)
                wait_apart(dve, c.passed, s["o_part"], (j + 1) * PT)
                dve.sem_inc(s["o_added"], 1)

                def free():
                    if not first(j):
                        dve.wait_ge(s["rows_ready"], j)
                pair_norm(dve, step, lambda n: xn2[:, n:n + 1, :], lambda n: pair_tiles(c.h, j, n), norm2,
                          s["x2_ready"], free)

            def choose(j):
                dve.wait_ge(s["l_made"], j + 1)
                step(dve.tensor_tensor(w.logits[:], c.bank[X][:, 0:PT * EXP].rearrange("p (t e) -> p t e", t=PT),
                                       c.br[:].unsqueeze(1).to_broadcast([P, PT, EXP]), ALU.add))
                pair_route(dve, step, w, 2)
                dve.tensor_tensor(gap[:], w.best[:, :, 1], w.best[:, :, 0], ALU.subtract).then_inc(s["gap_ready"], 1)
                for k in two:
                    step(dve.tensor_tensor(w.hot[:, k], c.iota8[:].unsqueeze(1).to_broadcast([P, PT, EXP]),
                                           w.expert[:, k, :].unsqueeze(2).to_broadcast([P, PT, EXP]),
                                           ALU.is_equal))
                step.wait()
                dve.tensor_tensor(w.took[:], w.hot[:, 0], w.hot[:, 1], ALU.add).then_inc(s["took_ready"], 1)

            def place(j):
                if not first(j):
                    dve.wait_ge(s["kept"], j)
                    dve.wait_ge(sent, j * (16 * 2 * PT))
                dve.wait_ge(s["egap_ready"], j + 1)
                step.run(dve.tensor_scalar(gap[:], egap[:], 1.0, None, ALU.add))
                step.run(dve.reciprocal(gate[:, 0, :], gap[:]))
                step(dve.tensor_tensor(gate[:, 1, :], gate[:, 0, :], egap[:], ALU.mult))
                dve.wait_ge(s["r_made"], j + 1)
                pair_places(dve, step, w, 2, c.base0, c.bank[X + 1], CAP, CAP, EXP * CAP, s["slots_ready"])

            dve.memset(c.cat[:], 0.0).then_inc(s["cleared"], 1)
            index(0)
            step.begin(0)
            clear(1)
            norm_x(0)
            maxima(0)
            clear(2)
            norm_x(1)
            start = step.n
            with dve.Fori(1, PAIRS - 2) as j:
                step.begin((j - 1) * FRONT_STEPS + start)
                add_norm(j - 1)
                maxima(j)
                clear(j + 2)
                choose(j - 1)
                norm_x(j + 1)
                place(j - 1)
                assert step.n == FRONT_STEPS, step.n
            step.begin((PAIRS - 3) * FRONT_STEPS + start)
            for j in (PAIRS - 2, PAIRS - 1):
                add_norm(j - 1)
                maxima(j)
                choose(j - 1)
                if j == PAIRS - 2:
                    norm_x(j + 1)
                place(j - 1)
            add_norm(PAIRS - 1)
            choose(PAIRS - 1)
            place(PAIRS - 1)


def moe2(nc, c, a):
    with ExitStack() as ctx:
        sb, sem = scope(nc, ctx, "moe2")
        two = range(2)
        G = 512
        GROUPS = CAP // G
        GT = G // P
        HC = HID0 // P
        W1 = [sb(f"W1{q}", [P, DC, HID0]) for q in two]
        W2 = [sb(f"W2{q}", [P, HC, D]) for q in two]
        b2 = [sb(f"b2{q}", [P, D]) for q in two]
        x = [sb(f"x{q}", [P, GT, D]) for q in two]
        xT = [sb(f"xT{q}", [P, DC, G]) for q in two]
        hT = [sb(f"hT{q}", [P, HC, G]) for q in two]
        y = [sb(f"y{q}", [P, GT, D]) for q in two]
        w_loaded = [sem(f"w_loaded{q}") for q in two]
        x_loaded = [sem(f"x_loaded{q}") for q in two]
        stored = sem("stored")
        names = "x_turned xT_left xT_right h_made h_ready y_made y_ready y_stored".split()
        s = {n: sem(n) for n in names}
        EXPERTS = EXP // 2
        block = ctx.enter_context(nc.Block())

        def unit(j, p, g):
            return j * (2 * GROUPS) + p * GROUPS + g

        @block.sync
        def _(sp):
            def load_w(e, p):
                def of(ap):
                    return ap[bass.ds(e, 1)] if not isinstance(e, int) else ap[e:e + 1]
                sp.dma_start(W1[p][:], of(a.W1).rearrange("e (k p) n -> p (e k) n", p=P)).then_inc(w_loaded[p], 16)
                sp.dma_start(W2[p][:], of(a.W2).rearrange("e (k p) n -> p (e k) n", p=P)).then_inc(w_loaded[p], 16)
                sp.dma_start(b2[p][:], of(a.b2).to_broadcast([P, D])).then_inc(w_loaded[p], 16)

            def load_x(u, g):
                r = bass.ds(u * G, G) if not isinstance(u, int) else slice(u * G, (u + 1) * G)
                sp.dma_start(x[g][:], a.xg0[r, :].rearrange("(t p) d -> p t d", p=P)).then_inc(x_loaded[g], 16)

            load_x(0, 0)
            load_w(0, 0)
            load_x(1, 1)
            load_w(1, 1)

            def pair(j, more):
                for g in range(GROUPS):
                    sp.wait_ge(s["x_turned"], unit(j, 0, g) + 1)
                    load_x(unit(j, 1, g), g)
                if not more:
                    return
                for p in two:
                    if p == 0:
                        for g in range(GROUPS):
                            sp.wait_ge(s["x_turned"], unit(j, 1, g) + 1)
                            load_x(unit(j + 1, 0, g), g)
                            if g == 0:
                                sp.wait_ge(s["y_ready"], unit(j, 1, 0) * GT + 1)
                                load_w((j + 1) * 2, 0)
                    else:
                        sp.wait_ge(s["y_ready"], unit(j + 1, 0, 0) * GT + 1)
                        load_w((j + 1) * 2 + 1, 1)

            with sp.Fori(0, EXPERTS - 1) as j:
                pair(j, True)
            pair(EXPERTS - 1, False)

        @block.gpsimd
        def _(pool):
            pool.sem_inc(s["y_stored"], 2)
            with pool.Fori(0, EXPERTS) as j:
                for p in two:
                    for g in range(GROUPS):
                        u = unit(j, p, g)
                        pool.wait_ge(s["y_ready"], (u + 1) * GT + 1)
                        pool.dma_start(a.y0[bass.ds(u * G, G), :].rearrange("(t p) d -> p t d", p=P), y[g][:])\
                            .then_inc(stored, 16)
                        pool.wait_ge(stored, (u + 1) * 16)
                        pool.sem_inc(s["y_stored"], 1)

        @block.tensor
        def _(pe):
            with pe.Fori(0, EXPERTS) as j:
                def turn_x(p, g):
                    pe.wait_ge(x_loaded[g], 16 * (2 * j + p + 1))
                    for k in range(DC):
                        for t in range(GT):
                            ins = pe.transpose(c.bank[k][:, t * P:(t + 1) * P], x[g][:, t, k * P:(k + 1) * P],
                                               c.ident[:])
                    ins.then_inc(s["x_turned"], 1)

                for p in two:
                    pe.wait_ge(w_loaded[p], 48 * (j + 1))
                    for g in range(GROUPS):
                        u = unit(j, p, g)
                        if (p, g) == (0, 0):
                            turn_x(0, 0)
                        pe.wait_ge(s["xT_left"], u + 1)
                        pe.wait_ge(s["xT_right"], u + 1)
                        for m in range(HC):
                            if m >= 3:
                                pe.wait_ge(s["h_ready"], u * HC + m - 2)
                            for k in range(DC):
                                ins = pe.matmul(c.bank[2 + m % 3][:], W1[p][:, k, m * P:(m + 1) * P], xT[g][:, k, :],
                                                start=k == 0, stop=k == DC - 1)
                            ins.then_inc(s["h_made"], 1)
                        if (p, g) != (1, 1):
                            turn_x(p + (g + 1) // GROUPS, (g + 1) % GROUPS)
                        pe.wait_ge(s["h_ready"], (u + 1) * HC)
                        for t in range(GT):
                            pe.wait_ge(s["y_ready"], u * GT + max(t - 1, 0) + 1)
                            for k in range(HC):
                                ins = pe.matmul(c.bank[6 + t % 2][:, 0:D], hT[g][:, k, t * P:(t + 1) * P], W2[p][:, k, :],
                                                start=k == 0, stop=k == HC - 1)
                            ins.then_inc(s["y_made"], 1)

        @block.scalar
        def _(act):
            with act.Fori(0, EXPERTS) as j:
                def move(p, g):
                    u = unit(j, p, g)
                    act.wait_ge(s["x_turned"], u + 1)
                    act.activation(xT[g][:, 1, :], c.bank[1][:], ACT.Copy).then_inc(s["xT_right"], 1)

                for p in two:
                    for g in range(GROUPS):
                        u = unit(j, p, g)
                        if (p, g) == (0, 0):
                            move(0, 0)
                        for m in range(HC):
                            wait_apart(act, c.passed, s["h_made"], u * HC + m + 1)
                            act.activation(hT[g][:, m, :], c.bank[2 + m % 3][:], ACT.Gelu,
                                           bias=c.b1T[:, bass.ds((2 * j + p) * HC + m, 1)])\
                                .then_inc(s["h_ready"], 1)
                        if (p, g) != (1, 1):
                            move(p + (g + 1) // GROUPS, (g + 1) % GROUPS)

        @block.vector
        def _(dve):
            dve.sem_inc(s["y_ready"], 1)
            with dve.Fori(0, EXPERTS) as j:
                def move(p, g):
                    u = unit(j, p, g)
                    dve.wait_ge(s["x_turned"], u + 1)
                    dve.tensor_copy(xT[g][:, 0, :], c.bank[0][:]).then_inc(s["xT_left"], 1)

                for p in two:
                    dve.wait_ge(w_loaded[p], 48 * (j + 1))
                    for g in range(GROUPS):
                        u = unit(j, p, g)
                        if (p, g) == (0, 0):
                            move(0, 0)
                        if (p, g) != (1, 1):
                            move(p + (g + 1) // GROUPS, (g + 1) % GROUPS)
                        dve.wait_ge(s["y_stored"], u + 1)
                        for t in range(GT):
                            dve.wait_ge(s["y_made"], u * GT + t + 1)
                            dve.tensor_tensor(y[g][:, t, :], c.bank[6 + t % 2][:, 0:D], b2[p][:], ALU.add)\
                                .then_inc(s["y_ready"], 1)



def prepare(nc, c, a):
    with ExitStack() as ctx:
        sb, sem = scope(nc, ctx, "prep")
        two = range(2)
        yrow = sb("yrow", [P, 2 * PT, D])
        place_now = sb("place_now", [P, 2 * PT], U32)
        gate_now = sb("gate_now", [P, 2 * PT])
        xn = sb("xn", [P, PT, D])
        xT = [sb(f"xT{q}", [P, DC, T]) for q in two]
        qk = sb("qk", [P, 2, TT, 2 * D])
        sq = sb("sq", [P, TT, 2 * D])
        NG = TT * 2 * HEADS
        ss = sb("ss", [P, 2, NG])
        rn = sb("rn", [P, 2 * NG])
        rtmp = sb("rtmp", [P, 2 * NG])
        norm = PairNorm(sb, "norm")
        SEMS = ("x_ready x_turned xT_ready qkv_made qk_ready v_ready sq_ready sq_read z_ready z_turned zT_ready "
                "bout_added copied ones_set").split()
        s = {n: sem(n) for n in SEMS}
        fetched = sem("fetched")
        block = ctx.enter_context(nc.Block())
        X_BANK = (0, 4)

        def bank(p, k):
            return c.bank[4 * p + k]

        @block.gpsimd
        def _(pool):
            pool.memset(c.vmem[:], 1.0).then_inc(s["ones_set"], 1)

            def fetch(j):
                at = bass.ds(j, 1) if not isinstance(j, int) else slice(j, j + 1)
                pool.tensor_copy(place_now[:].unsqueeze(1), c.place0[:, at, :])
                pool.tensor_copy(gate_now[:].unsqueeze(1), c.gates[:, at, :]).then_inc(s["copied"], 1)
                wait_apart(pool, c.passed, s["copied"], j + 1)
                for n in range(2 * PT):
                    pool.indirect_dma_start(
                        yrow[:, n, :], None, a.y0,
                        bass.IndirectOffsetOnAxis(ap=place_now[:, n:n + 1], axis=0),
                        bounds_check=EXP * CAP, oob_is_err=False).then_inc(fetched, 16)

            def add_bout(j):
                hj = pair_tiles(c.h, j)
                pool.tensor_tensor(hj, hj, c.bout[:].unsqueeze(1).to_broadcast([P, PT, D]), ALU.add)\
                    .then_inc(s["bout_added"], 1)

            fetch(0)
            with pool.Fori(0, PAIRS - 1) as j:
                pool.wait_ge(s["x_ready"], j + 1)
                fetch(j + 1)
                add_bout(j)
            pool.wait_ge(s["x_ready"], PAIRS)
            add_bout(PAIRS - 1)
            pool.wait_ge(s["bout_added"], PAIRS)

        @block.tensor
        def _(pe):
            def turn_x(j, last_z=None):
                pe.wait_ge(s["x_ready"], j + 1)
                for p in two:
                    if p == 0 and last_z is not None:
                        pe.wait_ge(s["zT_ready"], last_z)
                    ins = turn_tiles(pe, c, c.bank[X_BANK[p]], xn[:, p * TT:(p + 1) * TT], DC)
                    ins.then_inc(s["x_turned"], 1)

            def qkv(j):
                for p in two:
                    pe.wait_ge(s["xT_ready"], turn(j, p))
                    if not first(j):
                        pe.wait_ge(s["qk_ready"], turn(j - 1, p))
                        pe.wait_ge(s["v_ready"], turn(j - 1, p))
                    for t in range(TT):
                        for k in range(DC):
                            pe.matmul(bank(p, 1 + t)[:], xT[p][:, k, t * P:(t + 1) * P], c.wqkvT[:, k, 0:2 * D],
                                      start=k == 0, stop=k == DC - 1)
                    for t in range(TT):
                        for k in range(DC):
                            ins = pe.matmul(bank(p, 3)[:, t * D:(t + 1) * D], xT[p][:, k, t * P:(t + 1) * P],
                                            c.wqkvT[:, k, 2 * D:3 * D], start=k == 0, stop=k == DC - 1)
                    ins.then_inc(s["qkv_made"], 1)

            def turn_z(j):
                pe.wait_ge(s["z_ready"], j + 1)
                for p in two:
                    if p == 1:
                        pe.wait_ge(s["zT_ready"], j * 4 + 2)
                    for k in range(DC):
                        for part in two:
                            for t in range(TT):
                                col = part * D + k * P
                                ins = pe.transpose(c.bank[X_BANK[k]][:, part * T + t * P:part * T + (t + 1) * P],
                                                   qk[:, p, t, col:col + P], c.ident[:])
                        ins.then_inc(s["z_turned"], 1)

            pe.sem_inc(s["z_turned"], 1)
            turn_x(0)
            qkv(0)
            pe.wait_ge(s["xT_ready"], 2)
            turn_x(1)
            with pe.Fori(0, PAIRS - 2) as j:
                qkv(j + 1)
                turn_z(j)
                turn_x(j + 2, (j + 1) * 4)
            with pe.Fori(PAIRS - 2, PAIRS - 1) as j:
                qkv(j + 1)
                turn_z(j)
            pe.wait_ge(s["zT_ready"], (PAIRS - 1) * 4)
            turn_z(PAIRS - 1)

        @block.scalar
        def _(act):
            def copy_x(j):
                for p in two:
                    act.wait_ge(s["x_turned"], turn(j, p))
                    if not first(j):
                        act.wait_ge(s["qkv_made"], turn(j - 1, p))
                    act.activation(xT[p][:].rearrange("p k t -> p (k t)"), c.bank[X_BANK[p]][:], ACT.Copy)\
                        .then_inc(s["xT_ready"], 1)

            def square_copy_z(j):
                for p in two:
                    act.wait_ge(s["qk_ready"], turn(j, p))
                    act.wait_ge(s["sq_read"], turn(j, p))
                    act.activation(sq[:], qk[:, p], ACT.Square).then_inc(s["sq_ready"], 1)

            def copy_z(j):
                for p in two:
                    for k in range(DC):
                        act.wait_ge(s["z_turned"], j * 4 + p * 2 + k + 2)
                        b = bass.ds(j * 2 + p, 1) if not isinstance(j, int) else slice(j * 2 + p, j * 2 + p + 1)
                        act.activation(c.zT[:, b, k, :], c.bank[X_BANK[k]][:].unsqueeze(1), ACT.Copy)\
                            .then_inc(s["zT_ready"], 1)

            act.sem_inc(s["sq_read"], 1)
            copy_x(0)
            copy_x(1)
            with act.Fori(0, PAIRS - 2) as j:
                square_copy_z(j)
                copy_z(j)
                copy_x(j + 2)
            for j in (PAIRS - 2, PAIRS - 1):
                square_copy_z(j)
                copy_z(j)

        @block.vector
        def _(dve):
            step = Steps(dve, sem("dve"), c.passed)

            def sum_norm(j):
                dve.wait_ge(fetched, (j + 1) * (16 * 2 * PT))
                for k in two:
                    for n in range(PT):
                        r = k * PT + n
                        hn = pair_tiles(c.h, j, n)
                        step(dve.scalar_tensor_tensor(hn, yrow[:, r:r + 1, :],
                                                      gate_now[:, r:r + 1],
                                                      hn, ALU.mult, ALU.add))
                    (step.wait_apart if k else step.wait)()

                def free():
                    if not first(j):
                        dve.wait_ge(s["x_turned"], turn(j - 1, 1))

                pair_norm(dve, step, lambda n: xn[:, n:n + 1, :], lambda n: pair_tiles(c.h, j, n), norm, s["x_ready"],
                          free)

            def add_bias(j):
                for p in two:
                    dve.wait_ge(s["qkv_made"], turn(j, p))
                    if p == 0:
                        dve.wait_ge(s["z_turned"], j * 4 + 1)
                    dve.tensor_tensor(qk[:, p], c.ps[:, 4 * p + 1:4 * p + 3, :],
                                      c.bqkv[:, 0:2 * D].unsqueeze(1).to_broadcast([P, TT, 2 * D]), ALU.add)\
                        .then_inc(s["qk_ready"], 1)
                    b = bass.ds(j * 2 + p, 1) if not isinstance(j, int) else slice(j * 2 + p, j * 2 + p + 1)
                    for t in range(TT):
                        ins = dve.tensor_tensor(c.vone[:, b, t, :, 0:HD],
                                                bank(p, 3)[:, t * D:(t + 1) * D].rearrange(
                                                    "p (a h e) -> p a h e", a=1, e=HD),
                                                c.bqkv[:, 2 * D:3 * D].rearrange("p (a h e) -> p a h e", a=1, e=HD),
                                                ALU.add)
                    ins.then_inc(s["v_ready"], 1)

            def unit(j):
                for p in two:
                    dve.wait_ge(s["sq_ready"], turn(j, p))
                    dve.tensor_reduce(ss[:, p, :], sq[:].rearrange("p t (g e) -> p (t g) e", e=HD), AX.X, ALU.add)\
                        .then_inc(s["sq_read"], 1)
                dve.wait_ge(s["sq_read"], turn(j, 1) + 1)
                flat = ss[:].rearrange("p s g -> p (s g)")
                step.run(dve.tensor_scalar(flat, flat, 1e-24, None, ALU.max))
                rsqrt(dve, step, rn[:], flat, rtmp[:])
                z = qk[:].rearrange("p s t (g e) -> p (s t g) e", e=HD)
                dve.tensor_tensor(z, z, rn[:].unsqueeze(2).to_broadcast([P, 2 * NG, HD]), ALU.mult)\
                    .then_inc(s["z_ready"], 1)

            dve.wait_ge(s["ones_set"], 1)
            step.begin(0)
            sum_norm(0)
            each = step.n
            step.begin(each)
            sum_norm(1)
            with dve.Fori(0, PAIRS - 2) as j:
                step.begin(j * PREPARE_STEPS + 2 * each)
                add_bias(j)
                sum_norm(j + 2)
                unit(j)
                assert step.n == PREPARE_STEPS, step.n
            step.begin((PAIRS - 2) * PREPARE_STEPS + 2 * each)
            for j in (PAIRS - 2, PAIRS - 1):
                add_bias(j)
                unit(j)


def heads(nc, c, a):
    with ExitStack() as ctx:
        sb, sem = scope(nc, ctx, "heads")
        two = range(2)
        GP = HEADS // 2
        RING, AT_RING = 4, 2
        LEAD = 4
        V1 = HD + 1
        ex = [sb(f"ex{n}", [P, 2 * T]) for n in range(RING)]
        pr2 = [sb(f"pr2{n}", [P, 2 * T]) for n in range(RING)]
        feat = [sb(f"feat{n}", [P, 2 * T]) for n in range(RING)]
        attn = [sb(f"attn{n}", [P, 2, 3, P]) for n in range(AT_RING)]
        den = sb("den", [P, TT, HEADS])
        SEMS = "f_made ex_ready pr2_ready clipped feat_ready a_made a_masked av_made den_ready ctx_ready".split()
        s = {n: sem(n) for n in SEMS}
        block = ctx.enter_context(nc.Block())

        def count(i, u):
            return i * GP + u + 1

        def seq(i, u):
            i = i + u // GP
            return (slice(i, i + 1) if isinstance(i, int) else bass.ds(i, 1)), u % GP

        def f_bank(u):
            return c.bank[u % 2]

        def a_banks(u):
            return c.ps[:, 2 + 2 * (u % 2):4 + 2 * (u % 2), :]

        @block.tensor
        def _(pe):
            def products(i, u):
                b, g = seq(i, u)
                if not first(i) or u >= 2:
                    pe.wait_ge(s["pr2_ready"], count(i, u) - 2)
                    pe.wait_ge(s["ex_ready"], count(i, u) - 2)
                pe.matmul(f_bank(u), c.omega[:, g, :], c.zT[:, b, g // 4, :],
                          start=True, stop=True).then_inc(s["f_made"], 1)

            def scores(i, u):
                pe.wait_ge(s["feat_ready"], count(i, u))
                if not first(i) or u >= 2:
                    pe.wait_ge(s["a_masked"], count(i, u) - 2)
                f = feat[u % RING]
                for hh in two:
                    r = slice(NF * hh, NF * (hh + 1))
                    out = a_banks(u)[:, hh, :]
                    pe.matmul(out[:, 0:T], f[r, T:T + P], f[r, 0:T], start=True, stop=True)
                    ins = pe.matmul(out[:, T:T + P], f[r, T + P:2 * T], f[r, P:T], start=True, stop=True)
                ins.then_inc(s["a_made"], 1)

            def values(i, u):
                b, g = seq(i, u)
                pe.wait_ge(s["a_masked"], count(i, u))
                if g == 0 and not first(i):
                    pe.wait_ge(s["ctx_ready"], i)
                at = attn[u % AT_RING]
                for hh in two:
                    head = 2 * g + hh
                    cols = slice(head * V1, (head + 1) * V1)
                    v0, v1 = c.vone[:, b, 0, head, :], c.vone[:, b, 1, head, :]
                    pe.matmul(c.bank[6][:, cols], at[:, hh, 0, :], v0, start=True, stop=True)
                    pe.matmul(c.bank[7][:, cols], at[:, hh, 1, :], v0, start=True, stop=False)
                    ins = pe.matmul(c.bank[7][:, cols], at[:, hh, 2, :], v1, start=False, stop=True)
                ins.then_inc(s["av_made"], 1)

            for u in range(LEAD):
                products(0, u)
                if u >= 2:
                    scores(0, u - 2)
            for u in range(GP):
                products(0, u + LEAD)
                scores(0, u + 2)
                values(0, u)
            with pe.Fori(1, B - 1) as i:
                for u in range(GP):
                    products(i, u + LEAD)
                    scores(i, u + 2)
                    values(i, u)
            with pe.Fori(B - 1, B) as i:
                for u in range(GP):
                    if u + LEAD < GP:
                        products(i, u + LEAD)
                    if u + 2 < GP:
                        scores(i, u + 2)
                    values(i, u)

        @block.scalar
        def _(act):
            def feature_parts(i, u):
                act.wait_ge(s["f_made"], count(i, u))
                if not first(i) or u >= RING:
                    act.wait_ge(s["feat_ready"], count(i, u) - RING)
                act.activation(ex[u % RING][:], f_bank(u), ACT.Exp, scale=c.f_scale[:], bias=c.f_shift[:])\
                    .then_inc(s["ex_ready"], 1)
                act.activation(pr2[u % RING][:], f_bank(u), ACT.Square).then_inc(s["pr2_ready"], 1)

            for u in range(GP):
                feature_parts(0, u)
            with act.Fori(1, B) as i:
                for u in range(GP):
                    feature_parts(i, u)

        @block.vector
        def _(dve):
            def features(i, u):
                dve.wait_ge(s["ex_ready"], count(i, u))
                dve.tensor_scalar(ex[u % RING][:], ex[u % RING][:], EXP_LO, EXP_HI, ALU.max, ALU.min)\
                    .then_inc(s["clipped"], 1)
                dve.wait_ge(s["clipped"], count(i, u))
                dve.wait_ge(s["pr2_ready"], count(i, u))
                if not first(i) or u >= RING:
                    dve.wait_ge(s["a_made"], count(i, u) - RING)
                dve.scalar_tensor_tensor(feat[u % RING][:], ex[u % RING][:], c.f_weight[:], pr2[u % RING][:],
                                         ALU.mult, ALU.mult).then_inc(s["feat_ready"], 1)

            def mask(i, u):
                dve.wait_ge(s["a_made"], count(i, u))
                if not first(i) or u >= AT_RING:
                    dve.wait_ge(s["av_made"], count(i, u) - AT_RING)
                dve.tensor_tensor(
                    attn[u % AT_RING][:].rearrange("p h b t -> p h (b t)"), a_banks(u)[:, :, 0:3 * P],
                    c.causal[:].rearrange("p b t -> p (b t)").unsqueeze(1).to_broadcast([P, 2, 3 * P]),
                    ALU.mult).then_inc(s["a_masked"], 1)

            def context(i):
                dve.wait_ge(s["av_made"], count(i, GP - 1))
                av = c.ps[:, 6:8, 0:HEADS * V1].rearrange("p t (h e) -> p t h e", e=V1)
                dve.tensor_scalar(den[:], av[:, :, :, HD], 1e-6, None, ALU.max).then_inc(s["den_ready"], 1)
                dve.wait_ge(s["den_ready"], i * 2 + 1)
                dve.reciprocal(den[:], den[:]).then_inc(s["den_ready"], 1)
                dve.wait_ge(s["den_ready"], i * 2 + 2)
                out = c.ctx[:, bass.ds(i * TT, TT), :] if not isinstance(i, int) else c.ctx[:, i * TT:(i + 1) * TT, :]
                dve.tensor_tensor(out.rearrange("p t (h e) -> p t h e", e=HD), av[:, :, :, 0:HD],
                                  den[:].unsqueeze(3).to_broadcast([P, TT, HEADS, HD]), ALU.mult)\
                    .then_inc(s["ctx_ready"], 1)

            for u in range(3):
                features(0, u)
            for u in range(GP):
                mask(0, u)
                features(0, u + 3)
            with dve.Fori(1, B - 1) as i:
                for u in range(GP):
                    mask(i, u)
                    if u == 0:
                        context(i - 1)
                    features(i, u + 3)
            with dve.Fori(B - 1, B) as i:
                for u in range(GP):
                    mask(i, u)
                    if u == 0:
                        context(i - 1)
                    if u + 3 < GP:
                        features(i, u + 3)
            context(B - 1)


def select(nc, c, a):
    with ExitStack() as ctx:
        sb, sem = scope(nc, ctx, "sel")
        two = range(2)
        ctx_now = sb("ctx_now", [P, PT, D])
        ctxT = [sb(f"ctxT{q}", [P, DC, T]) for q in two]
        xn = sb("xn", [P, PT, D])
        rows_out = sb("rows_out", [P, PT, D])
        xT = [sb(f"xT{q}", [P, DC, T]) for q in two]
        norm = PairNorm(sb, "norm")
        w = PairRouting(sb, 1)
        nbest = sb("nbest", [P, PT])
        prob = sb("prob", [P, PT, EXP])
        psum_p = sb("psum_p", [P, PT])
        tv = sb("tv", [P, PT])
        SEMS = ("ctx_copied ctx_turned ctxT_ready o_made o_added x2_ready x2_turned xT2_ready rows_ready l_made "
                "took_ready r_made slots_ready nbest_ready prob_ready kept").split()
        s = {n: sem(n) for n in SEMS}
        sent = sem("sent")
        w_loaded = sem("w_loaded")
        block = ctx.enter_context(nc.Block())
        CTX, O, X2, LOGITS, RANKS = 0, 2, 4, 6, 7

        def flat(x):
            return x[:].rearrange("p k t -> p (k t)")

        @block.sync
        def _(sp):
            for e in range(EXP):
                sp.dma_start(c.W1[:, 2 * e:2 * e + 2, :], a.ew1[e].rearrange("(k p) n -> p k n", p=P))\
                    .then_inc(w_loaded, 16)
                sp.dma_start(c.W2[:, 4 * e:4 * e + 4, :], a.ew2[e].rearrange("(k p) n -> p k n", p=P))\
                    .then_inc(w_loaded, 16)
            sp.wait_ge(w_loaded, 16 * 2 * EXP)

        @block.gpsimd
        def _(pool):
            pool.sem_inc(s["kept"], 1)
            with pool.Fori(0, PAIRS) as j:
                wait_apart(pool, c.passed, s["rows_ready"], j + 1)
                wait_apart(pool, c.passed, s["slots_ready"], j + 1)
                for n in range(PT):
                    pool.indirect_dma_start(a.xg1, bass.IndirectOffsetOnAxis(ap=w.slot_i[:, n:n + 1], axis=0),
                                            rows_out[:, n, :], None, bounds_check=EXP * REGION - 1,
                                            oob_is_err=False).then_inc(sent, 16)
                pj = bass.ds(j, 1)
                pool.tensor_copy(c.expert1[:, pj, :], w.expert[:])
                pool.tensor_copy(c.rank1[:, pj, :], w.rank[:].unsqueeze(1))
                pool.tensor_copy(c.topv[:, pj, :], tv[:].unsqueeze(1)).then_inc(s["kept"], 1)
                hj = pair_tiles(c.h, j)
                pool.tensor_tensor(hj, hj, c.beta[:].unsqueeze(1).to_broadcast([P, PT, D]), ALU.add)
            pool.wait_ge(sent, 16 * PT * PAIRS)

        @block.tensor
        def _(pe):
            def project(j, first):
                pe.wait_ge(s["ctx_copied"], j + 1)
                for p in two:
                    if not first:
                        pe.wait_ge(s["ctxT_ready"], turn(j - 1, p))
                    turn_tiles(pe, c, c.bank[CTX + p], ctx_now[:, p * TT:(p + 1) * TT], DC).then_inc(s["ctx_turned"], 1)
                if not first:
                    pe.wait_ge(s["o_added"], j)
                for p in two:
                    pe.wait_ge(s["ctxT_ready"], turn(j, p))
                    for t in range(TT):
                        for k in range(DC):
                            ins = pe.matmul(c.bank[O + p][:, t * D:(t + 1) * D], ctxT[p][:, k, t * P:(t + 1) * P],
                                            c.woutT[:, k, :], start=k == 0, stop=k == DC - 1)
                ins.then_inc(s["o_made"], 1)

            def router(j):
                pe.wait_ge(s["x2_ready"], j + 1)
                for p in two:
                    turn_tiles(pe, c, c.bank[X2 + p], xn[:, p * TT:(p + 1) * TT], DC).then_inc(s["x2_turned"], 1)
                for p in two:
                    pe.wait_ge(s["xT2_ready"], turn(j, p))
                    for t in range(TT):
                        n = p * TT + t
                        for k in range(DC):
                            ins = pe.matmul(c.bank[LOGITS][:, n * EXP:(n + 1) * EXP], xT[p][:, k, t * P:(t + 1) * P],
                                            c.gateT[:, k, :], start=k == 0, stop=k == DC - 1)
                ins.then_inc(s["l_made"], 1)

            def ranks(j):
                pe.wait_ge(s["took_ready"], j + 1)
                pair_ranks(pe, c, c.bank[RANKS], w.hot[:, 0]).then_inc(s["r_made"], 1)

            project(0, True)
            router(0)
            project(1, False)
            with pe.Fori(0, PAIRS - 2) as j:
                ranks(j)
                project(j + 2, False)
                router(j + 1)
            ranks(PAIRS - 2)
            router(PAIRS - 1)
            ranks(PAIRS - 1)

        @block.scalar
        def _(act):
            def contexts(j, first):
                if not first:
                    wait_apart(act, c.passed, s["ctx_turned"], turn(j - 1, 1))
                act.activation(ctx_now[:], pair_tiles(c.ctx, j), ACT.Copy).then_inc(s["ctx_copied"], 1)
                for p in two:
                    act.wait_ge(s["ctx_turned"], turn(j, p))
                    if not first:
                        act.wait_ge(s["o_made"], j)
                    act.activation(flat(ctxT[p]), c.bank[CTX + p][:], ACT.Copy).then_inc(s["ctxT_ready"], 1)

            def turned(j):
                for p in two:
                    act.wait_ge(s["x2_turned"], turn(j, p))
                    act.activation(flat(xT[p]), c.bank[X2 + p][:], ACT.Copy).then_inc(s["xT2_ready"], 1)

            def gates_rows(j, first):
                act.wait_ge(s["nbest_ready"], j + 1)
                for n in range(PT):
                    act.activation(prob[:, n, :], w.logits[:, n, :], ACT.Exp, bias=nbest[:, n:n + 1],
                                   accum_out=psum_p[:, n:n + 1]).then_inc(s["prob_ready"], 1)
                if not first:
                    act.wait_ge(sent, j * (16 * PT))
                act.activation(rows_out[:], xn[:], ACT.Copy).then_inc(s["rows_ready"], 1)

            contexts(0, True)
            turned(0)
            contexts(1, False)
            gates_rows(0, True)
            contexts(2, False)
            turned(1)
            with act.Fori(1, PAIRS - 2) as j:
                gates_rows(j, False)
                contexts(j + 2, False)
                turned(j + 1)
            gates_rows(PAIRS - 2, False)
            turned(PAIRS - 1)
            gates_rows(PAIRS - 1, False)

        @block.vector
        def _(dve):
            step = Steps(dve, sem("dve"), c.passed)

            def add_norm(j, first):
                dve.wait_ge(s["o_made"], j + 1)
                hj = pair_tiles(c.h, j)
                dve.tensor_tensor(hj.rearrange("p (s t) d -> p s (t d)", s=2), c.ps[:, O:O + 2, :],
                                  hj.rearrange("p (s t) d -> p s (t d)", s=2), ALU.add).then_inc(s["o_added"], 1)
                wait_apart(dve, c.passed, s["o_added"], j + 1)

                def free():
                    if not first:
                        dve.wait_ge(s["rows_ready"], j)

                pair_norm(dve, step, lambda n: xn[:, n:n + 1, :], lambda n: pair_tiles(c.h, j, n), norm, s["x2_ready"],
                          free)

            def choose(j):
                dve.wait_ge(s["l_made"], j + 1)
                step(dve.tensor_copy(w.logits[:], c.bank[LOGITS][:, 0:PT * EXP].rearrange(
                    "p (t e) -> p t e", t=PT)))
                dve.wait_ge(s["kept"], j + 1)
                pair_route(dve, step, w, 1)
                dve.tensor_scalar(nbest[:], w.best[:, :, 0], -1.0, None, ALU.mult).then_inc(s["nbest_ready"], 1)
                dve.tensor_tensor(w.hot[:, 0], c.iota8[:].unsqueeze(1).to_broadcast([P, PT, EXP]),
                                  w.expert[:, 0, :].unsqueeze(2).to_broadcast([P, PT, EXP]),
                                  ALU.is_equal).then_inc(s["took_ready"], 1)

            def place(j, first):
                dve.wait_ge(s["prob_ready"], PT * (j + 1))
                step.run(dve.reciprocal(psum_p[:], psum_p[:]))
                step.run(dve.tensor_scalar(tv[:], psum_p[:], 1e-8, None, ALU.add))
                step.run(dve.reciprocal(tv[:], tv[:]))
                step(dve.tensor_tensor(tv[:], tv[:], psum_p[:], ALU.mult))
                dve.wait_ge(s["r_made"], j + 1)
                if not first:
                    dve.wait_ge(sent, j * (16 * PT))
                pair_places(dve, step, w, 1, c.base1, c.bank[RANKS], REGION, None, None, s["slots_ready"])

            step.begin(0)
            add_norm(0, True)
            choose(0)
            add_norm(1, False)
            place(0, True)
            start = step.n
            with dve.Fori(1, PAIRS - 1) as j:
                step.begin((j - 1) * SELECT_STEPS + start)
                choose(j)
                add_norm(j + 1, False)
                place(j, False)
                assert step.n == SELECT_STEPS, step.n
            step.begin((PAIRS - 2) * SELECT_STEPS + start)
            choose(PAIRS - 1)
            place(PAIRS - 1, False)


def moe1(nc, c, a):
    with ExitStack() as ctx:
        sb, sem = scope(nc, ctx, "moe1")
        UN, MT = MOE1_FLIGHT, MOE1_TILES
        HC = HID1 // P
        count_i = sb("count_i", [P, EXP], I32)
        tiles_i = sb("tiles_i", [P, EXP], I32)
        tail_i = sb("tail_i", [P, EXP], I32)
        tiles = sb("tiles", [P, EXP])
        cum = sb("cum", [P, EXP])
        past = sb("past", [P, MT, EXP])
        ej = sb("ej", [P, MT])
        before = sb("before", [P, MT])
        row = sb("row", [P, MT])
        row_in = sb("row_in", [P, MT], I32)
        hot = sb("hot", [P, TILES, EXP])
        first = sb("first", [P, TILES])
        e_i = sb("e_i", [P, MT], I32)
        q4 = range(UN)
        x = [sb(f"x{q}", [P, D]) for q in q4]
        xT = [sb(f"xT{q}", [P, DC, P]) for q in q4]
        g = [sb(f"g{q}", [P, HID1]) for q in q4]
        gT = [sb(f"gT{q}", [P, HC, P]) for q in q4]
        y = [sb(f"y{q}", [P, D]) for q in q4]
        tables = sem("tables")
        tails = sem("tails")
        loaded = [sem(f"loaded{q}") for q in q4]
        stored = sem("stored")
        names = "x_turned xT_ready h_made g_ready g_turned gT_ready y_made y_ready y_stored".split()
        s = {n: sem(n) for n in names}
        block = ctx.enter_context(nc.Block())

        def done(i, q):
            return i * UN + q + 1

        @block.sync
        def _(sp):
            sp.wait_ge(tables, 1)
            for e in range(EXP):
                r = sp.value_load(tail_i[0:1, e:e + 1], min_val=e * REGION, max_val=e * REGION + N)
                sp.dma_start(a.xg1[bass.ds(r, P), :], c.zero[:, 0:D]).then_inc(tails, 16)
            sp.wait_ge(tails, 16 * EXP)

            def load(t, q):
                r = sp.value_load(row_in[0:1, bass.ds(t, 1)] if not isinstance(t, int) else row_in[0:1, t:t + 1],
                                  min_val=0, max_val=EXP * REGION)
                sp.dma_start(x[q][:], a.xg1[bass.ds(r, P), :]).then_inc(loaded[q], 16)

            for q in q4:
                load(q, q)
            with sp.Fori(0, MT // UN - 1) as i:
                for q in q4:
                    sp.wait_ge(s["x_turned"], done(i, q))
                    load((i + 1) * UN + q, q)

        @block.gpsimd
        def _(pool):
            pool.sem_inc(s["y_stored"], UN)
            with pool.Fori(0, MT // UN) as i:
                for q in q4:
                    pool.wait_ge(s["y_ready"], done(i, q) + UN)
                    pool.dma_start(a.y1[bass.ds((i * UN + q) * P, P), :], y[q][:]).then_inc(stored, 16)
                    pool.wait_ge(stored, 16 * done(i, q))
                    pool.sem_inc(s["y_stored"], 1)

        @block.tensor
        def _(pe):
            def bank(q, k):
                return c.bank[2 * q + k]

            pe.wait_ge(tables, 1)
            with pe.Fori(0, MT // UN) as i:
                e = [pe.value_load(e_i[0:1, bass.ds(i * UN + q, 1)], min_val=0, max_val=EXP - 1) for q in q4]
                for q in q4:
                    pe.wait_ge(loaded[q], 16 * (i + 1))
                    for k in range(DC):
                        ins = pe.transpose(bank(q, 0)[:, k * P:(k + 1) * P], x[q][:, k * P:(k + 1) * P], c.ident[:])
                    ins.then_inc(s["x_turned"], 1)
                for q in q4:
                    pe.wait_ge(s["xT_ready"], done(i, q))
                    pe.wait_ge(s["y_ready"], i * UN + q + 1)
                    for k in range(DC):
                        ins = pe.matmul(bank(q, 1)[:], xT[q][:, k, :], c.W1[:, bass.ds(e[q] * DC + k, 1), :],
                                        start=k == 0, stop=k == DC - 1)
                    ins.then_inc(s["h_made"], 1)
                for q in q4:
                    pe.wait_ge(s["g_ready"], done(i, q))
                    for k in range(HC):
                        ins = pe.transpose(bank(q, 0)[:, k * P:(k + 1) * P], g[q][:, k * P:(k + 1) * P], c.ident[:])
                    ins.then_inc(s["g_turned"], 1)
                for q in q4:
                    pe.wait_ge(s["gT_ready"], done(i, q))
                    for k in range(HC):
                        ins = pe.matmul(bank(q, 1)[:, 0:D], gT[q][:, k, :], c.W2[:, bass.ds(e[q] * HC + k, 1), :],
                                        start=k == 0, stop=k == HC - 1)
                    ins.then_inc(s["y_made"], 1)

        @block.scalar
        def _(act):
            act.sem_inc(s["y_ready"], UN)
            with act.Fori(0, MT // UN) as i:
                for q in q4:
                    act.wait_ge(s["h_made"], done(i, q))
                    act.activation(g[q][:], c.bank[2 * q + 1][:], ACT.Gelu).then_inc(s["g_ready"], 1)
                for q in q4:
                    act.wait_ge(s["y_made"], done(i, q))
                    act.wait_ge(s["y_stored"], done(i, q))
                    act.activation(y[q][:], c.bank[2 * q + 1][:, 0:D], ACT.Copy).then_inc(s["y_ready"], 1)

        @block.vector
        def _(dve):
            step = Steps(dve, sem("dve"), c.passed)
            step.run(dve.tensor_copy(count_i[:], c.base1[:]))
            step.run(dve.tensor_scalar(tiles[:], c.base1[:], float(P - 1), None, ALU.add))
            step.run(dve.tensor_copy(tiles_i[:], tiles[:]))
            step.run(dve.tensor_scalar(tiles_i[:], tiles_i[:], 7, None, ALU.logical_shift_right))
            step.run(dve.tensor_copy(tiles[:], tiles_i[:]))
            step.run(dve.tensor_copy(cum[:], tiles[:]))
            for e in range(1, EXP):
                step.run(dve.tensor_tensor(cum[:, e:e + 1], cum[:, e - 1:e], tiles[:, e:e + 1], ALU.add))
            step.run(dve.tensor_tensor(past[:], c.tile_no[:].unsqueeze(2).to_broadcast([P, MT, EXP]),
                                       cum[:].unsqueeze(1).to_broadcast([P, MT, EXP]), ALU.is_ge))
            step.run(dve.tensor_reduce(ej[:], past[:], AX.X, ALU.add))
            step.run(dve.tensor_tensor(past[:], past[:], tiles[:].unsqueeze(1).to_broadcast([P, MT, EXP]), ALU.mult))
            step.run(dve.tensor_reduce(before[:], past[:], AX.X, ALU.add))
            step.run(dve.tensor_tensor(before[:], c.tile_no[:], before[:], ALU.subtract))
            step.run(dve.tensor_scalar(before[:], before[:], float(P), None, ALU.mult))
            step.run(dve.scalar_tensor_tensor(row[:], ej[:], float(REGION), before[:], ALU.mult, ALU.add))
            step.run(dve.tensor_scalar(row_in[:], row[:], float(EXP * REGION), None, ALU.min))
            step.run(dve.tensor_scalar(e_i[:], ej[:], float(EXP - 1), None, ALU.min))
            step.run(dve.tensor_tensor(hot[:], c.iota8[:].unsqueeze(1).to_broadcast([P, TILES, EXP]),
                                       c.expert1[:].rearrange("p b t -> p (b t)").unsqueeze(2)
                                       .to_broadcast([P, TILES, EXP]), ALU.is_equal))
            step.run(dve.tensor_tensor(tiles[:], cum[:], tiles[:], ALU.subtract))
            step.run(dve.tensor_tensor(hot[:], hot[:], tiles[:].unsqueeze(1).to_broadcast([P, TILES, EXP]), ALU.mult))
            step.run(dve.tensor_reduce(first[:], hot[:], AX.X, ALU.add))
            step.run(dve.scalar_tensor_tensor(c.place1[:].rearrange("p b t -> p (b t)"), first[:], float(P),
                                              c.rank1[:].rearrange("p b t -> p (b t)"), ALU.mult, ALU.add))
            step.run(dve.scalar_tensor_tensor(cum[:], c.iota8[:], float(REGION), c.base1[:], ALU.mult, ALU.add))
            dve.tensor_copy(tail_i[:], cum[:]).then_inc(tables, 1)
            with dve.Fori(0, MT // UN) as i:
                for q in q4:
                    dve.wait_ge(s["x_turned"], done(i, q))
                    dve.tensor_copy(xT[q][:].rearrange("p k t -> p (k t)"), c.bank[2 * q][:, 0:D])\
                        .then_inc(s["xT_ready"], 1)
                for q in q4:
                    dve.wait_ge(s["g_turned"], done(i, q))
                    dve.tensor_copy(gT[q][:].rearrange("p k t -> p (k t)"), c.bank[2 * q][:])\
                        .then_inc(s["gT_ready"], 1)


def back(nc, c, a):
    with ExitStack() as ctx:
        sb, sem = scope(nc, ctx, "back")
        two = range(2)
        yrow = [sb(f"yrow{q}", [P, PT, D]) for q in two]
        o = [sb(f"o{q}", [P, PT, D]) for q in two]
        place_now = [sb(f"place_now{q}", [P, PT], U32) for q in two]
        t2 = sb("t2", [P, PT])
        norm = PairNorm(sb, "norm")
        fetched = [sem(f"fetched{q}") for q in two]
        stored = [sem(f"stored{q}") for q in two]
        names = "placed scaled normed out_ready".split()
        s = {n: sem(n) for n in names}
        block = ctx.enter_context(nc.Block())

        @block.sync
        def _(sp):
            for q in two:
                sp.sem_inc(stored[q], 1)
            with sp.Fori(0, PAIRS // 2) as i:
                for q in two:
                    sp.wait_ge(s["out_ready"], i * 2 + q + 1)
                    sp.dma_start(a.out[bass.ds(i * 4 + q * 2, 2)].rearrange("b (t p) d -> p (b t) d", p=P), o[q][:])\
                        .then_inc(stored[q], 16)
            for q in two:
                sp.wait_ge(stored[q], 16 * (PAIRS // 2) + 1)

        @block.gpsimd
        def _(pool):
            def fetch(j, q):
                pool.tensor_copy(place_now[q][:].unsqueeze(1), c.place1[:, bass.ds(j, 1), :]
                                 if not isinstance(j, int) else c.place1[:, j:j + 1, :]).then_inc(s["placed"], 1)
                wait_apart(pool, c.passed, s["placed"], j + 1)
                for n in range(PT):
                    pool.indirect_dma_start(yrow[q][:, n, :], None, a.y1,
                                            bass.IndirectOffsetOnAxis(ap=place_now[q][:, n:n + 1], axis=0),
                                            bounds_check=MOE1_TILES * P - 1, oob_is_err=False)\
                        .then_inc(fetched[q], 16)

            fetch(0, 0)
            fetch(1, 1)
            with pool.Fori(0, PAIRS // 2 - 1) as i:
                for q in two:
                    pool.wait_ge(s["normed"], i * 2 + q + 1)
                    fetch(i * 2 + q + 2, q)

        @block.vector
        def _(dve):
            step = Steps(dve, sem("dve"), c.passed)
            with dve.Fori(0, PAIRS // 2) as i:
                step.begin(i * BACK_STEPS)
                for q in two:
                    j = i * 2 + q
                    y, tv = yrow[q], c.topv[:, bass.ds(j, 1), :]
                    dve.wait_ge(fetched[q], (i + 1) * (16 * PT))
                    for n in range(PT):
                        step(dve.bn_stats(norm.stats[:, n, :], y[:, n, :]))
                    step(dve.tensor_copy(t2[:].unsqueeze(1), tv))
                    step.wait_apart()
                    for n in range(PT):
                        step(dve.bn_aggr(norm.mv[:, n, :], norm.stats[:, n, :]))
                    step.wait()
                    step.run(dve.tensor_tensor(norm.var[:], norm.mv[:, :, 1], t2[:], ALU.mult))
                    step.run(dve.tensor_tensor(norm.var[:], norm.var[:], t2[:], ALU.mult))
                    step.run(dve.tensor_scalar(norm.var[:], norm.var[:], LN_EPS, None, ALU.add))
                    rsqrt(dve, step, norm.rstd[:], norm.var[:], norm.tmp[:])
                    step.run(dve.tensor_tensor(norm.rstd[:], norm.rstd[:], t2[:], ALU.mult))
                    dve.wait_ge(stored[q], 16 * i + 1)
                    for n in range(PT):
                        dve.tensor_scalar(o[q][:, n, :], y[:, n, :], norm.mv[:, n, 0:1], norm.rstd[:, n:n + 1],
                                          ALU.subtract, ALU.mult).then_inc(s["scaled"], 1)
                    dve.wait_ge(s["scaled"], (j + 1) * PT)
                    dve.sem_inc(s["normed"], 1)
                    step.run(dve.tensor_tensor(o[q][:], o[q][:], c.gamma[:].unsqueeze(1).to_broadcast([P, PT, D]),
                                               ALU.mult))
                    dve.tensor_tensor(o[q][:], o[q][:], pair_tiles(c.h, j), ALU.add).then_inc(s["out_ready"], 1)
                assert step.n == BACK_STEPS, step.n


def lm_tower(nc, ins, out):
    a = Chip()
    a.out = out
    a.x = ins["x"]
    a.emb = [ins[f"L0_tok_emb_{i}"] for i in range(4)]
    a.proj = [ins[f"L0_tok_proj_{i}"] for i in range(4)]
    a.QK, a.VO = ins["L0_attn_QK"], ins["L0_attn_VO"]
    a.Wr, a.br = ins["L0_ffn_Wr"], ins["L0_ffn_br"]
    a.W1, a.b1, a.W2, a.b2 = (ins[f"L0_ffn_{n}"] for n in ("W1", "b1", "W2", "b2"))
    a.w_qkv, a.b_qkv, a.w_out, a.b_out, a.omega, a.nodes, a.qw = (
        ins[f"L1_attn_{n}"] for n in ("w_qkv", "b_qkv", "w_out", "b_out", "omega", "quad_nodes", "quad_weights"))
    a.gate_w, a.ew1, a.ew2, a.gamma, a.beta = (
        ins[f"L1_ffn_{n}"] for n in ("gate_w", "expert_w1", "expert_w2", "ln_gamma", "ln_beta"))
    a.xg0 = nc.dram_tensor("rows_moe2", [EXP * CAP, D], F32, kind="Internal").ap()
    a.y0 = nc.dram_tensor("out_moe2", [EXP * CAP + 1, D], F32, kind="Internal").ap()
    a.xg1 = nc.dram_tensor("rows_moe1", [EXP * REGION + P, D], F32, kind="Internal").ap()
    a.y1 = nc.dram_tensor("out_moe1", [MOE1_TILES * P, D], F32, kind="Internal").ap()
    c = Chip()
    with ExitStack() as ctx:
        sb, sem = scope(nc, ctx, "all")
        c.passed = sem("passed")
        MT = MOE1_TILES
        c.ps = ctx.enter_context(nc.psum_tensor("banks", [P, 8, 512], F32))
        c.bank = [c.ps[:, k, :] for k in range(8)]
        c.h = sb("h", [P, TILES, D])
        c.zero = sb("zero", [P, D])
        c.ident, c.ones, c.before = (sb(n, [P, P]) for n in ("ident", "ones", "before"))
        c.causal = sb("causal", [P, 3, P])
        c.iota8 = sb("iota8", [P, EXP])
        c.tile_no = sb("tile_no", [P, MT])
        c.place0 = sb("place0", [P, PAIRS, 2 * PT], U32)
        c.gates = sb("gates", [P, PAIRS, 2 * PT])
        c.expert1, c.rank1 = sb("expert1", [P, PAIRS, 2 * TT]), sb("rank1", [P, PAIRS, 2 * TT])
        c.place1 = sb("place1", [P, PAIRS, 2 * TT], U32)
        c.topv = sb("topv", [P, PAIRS, 2 * TT])
        c.base0, c.base1 = sb("base0", [P, EXP]), sb("base1", [P, EXP])
        c.Wr, c.br = sb("Wr", [P, DC, EXP]), sb("br", [P, EXP])
        c.wqkvT, c.bqkv = sb("wqkvT", [P, DC, 3 * D]), sb("bqkv", [P, 3 * D])
        c.woutT, c.bout = sb("woutT", [P, DC, D]), sb("bout", [P, D])
        c.omega = sb("omega", [P, HEADS // 2, P])
        c.nodes, c.qw = sb("nodes", [P, 2]), sb("qw", [P, 2])
        c.f_scale, c.f_shift, c.f_weight = (sb(n, [P, 1]) for n in ("f_scale", "f_shift", "f_weight"))
        c.b1T = sb("b1T", [P, EXP * HID0 // P])
        c.gateT = sb("gateT", [P, DC, EXP])
        c.gamma, c.beta = sb("gamma", [P, D]), sb("beta", [P, D])
        with ExitStack() as early:
            sb, _ = scope(nc, early, "early")
            c.cat = sb("cat", [P, PT, CAT])
            c.token_row = sb("token_row", [P, 4, TILES], U32)
            c.projT = sb("projT", [P, KC, D])
            c.QK, c.VO = sb("QK", [P, DC, D]), sb("VO", [P, DC, D])
            setup(nc, c, a)
            front(nc, c, a)
        moe2(nc, c, a)
        with ExitStack() as late:
            sb, _ = scope(nc, late, "late")
            c.wide = sb("wide", [P, B, DC * 2 * T])
            c.zT = c.wide[:].rearrange("p b (k t) -> p b k t", k=DC)
            c.ctx = c.wide[:, 0:B // 2, :].rearrange("p b (s d) -> p (b s) d", d=D)
            c.W1 = c.wide[:, B // 2:B, :].rearrange("p b (s d) -> p (b s) d", d=HID1)
            c.vmem = sb("vmem", [P, B * TT * HEADS * (HD + 1)])
            c.vone = c.vmem[:].rearrange("p (b t h e) -> p b t h e", b=B, t=TT, h=HEADS)
            c.W2 = c.vmem[:, 0:HID1 // P * EXP * D].rearrange("p (k d) -> p k d", d=D)
            prepare(nc, c, a)
            heads(nc, c, a)
            select(nc, c, a)
            moe1(nc, c, a)
            back(nc, c, a)


_INS = ['x', 'L0_tok_emb_0', 'L0_tok_emb_1', 'L0_tok_emb_2', 'L0_tok_emb_3', 'L0_tok_proj_0', 'L0_tok_proj_1',
        'L0_tok_proj_2', 'L0_tok_proj_3', 'L0_attn_QK', 'L0_attn_VO', 'L0_ffn_Wr', 'L0_ffn_br', 'L0_ffn_W1',
        'L0_ffn_b1', 'L0_ffn_W2', 'L0_ffn_b2', 'L1_attn_w_qkv', 'L1_attn_b_qkv', 'L1_attn_w_out', 'L1_attn_b_out',
        'L1_attn_omega', 'L1_attn_quad_nodes', 'L1_attn_quad_weights', 'L1_ffn_gate_w', 'L1_ffn_expert_w1',
        'L1_ffn_expert_w2', 'L1_ffn_ln_gamma', 'L1_ffn_ln_beta']


def kernel(**inputs):
    import numpy as _np
    import concourse.bacc as _bacc
    from concourse import mybir as _mybir
    from concourse.bass_utils import run_bass_kernel_spmd as _run

    nc = _bacc.Bacc("TRN2", target_bir_lowering=False, num_devices=1)
    arrays, args = {}, {}
    for name in _INS:
        arr = _np.ascontiguousarray(inputs[name])
        arrays[f"in_{name}_dram"] = arr
        args[name] = nc.dram_tensor(f"in_{name}_dram", arr.shape, _mybir.dt.from_np(arr.dtype), kind="ExternalInput").ap()
    out = nc.dram_tensor("out_0_dram", (B, T, D), _mybir.dt.from_np(_np.dtype("float32")), kind="ExternalOutput").ap()
    lm_tower(nc, args, out)
    r = _run(nc, [arrays], core_ids=[0])
    return r.results[0]["out_0_dram"]
```

```python
from contextlib import ExitStack

import concourse.bass as bass
from concourse import mybir

F32 = mybir.dt.float32
I32 = mybir.dt.int32
U32 = mybir.dt.uint32
ALU = mybir.AluOpType
ACT = mybir.ActivationFunctionType
AX = mybir.AxisListType

P = 128
B, T, D = 16, 256, 256
PAIRS = B // 2
TT = T // P
PT = 2 * TT
N = B * T
TILES = N // P
DC = D // P
CUTS = [0, 5000, 10000, 50000, 267735]
EMB_D = [256, 64, 64, 16]
EMB_AT = [0, 256, 320, 384]
CAT = 512
KC = CAT // P
NOWHERE = 1 << 20
EXP = 8
HID0, CAP = 1024, N * 2 // EXP
HID1 = 512
HEADS, HD, FEAT = 16, 16, 32
NF = 2 * FEAT
REGION = N + P
MOE1_FLIGHT = 4
MOE1_TILES = -(-((N + EXP * (P - 1)) // P) // MOE1_FLIGHT) * MOE1_FLIGHT
LN_EPS = 1e-5
ATT_SCALE = 1.0 / D ** 0.5
EMB_SCALE = float(D) ** 0.5
RSQRT_MAGIC = 0x5F3759DF
EXP_LO, EXP_HI = 2.061153622438558e-09, 485165195.4097903
FRONT_STEPS, LINEAR_STEPS, BACK_STEPS = 77, 174, 68


def turn(j, p):
    return 2 * j + p + 1


def wait_apart(eng, passed, sem, value):
    eng.wait_ge(sem, value)
    eng.sem_inc(passed, 1)


class Steps:

    def __init__(self, eng, sem, passed):
        self.eng, self.sem, self.passed, self.base, self.n = eng, sem, passed, 0, 0

    def begin(self, base):
        self.base, self.n = base, 0

    def __call__(self, ins):
        ins.then_inc(self.sem, 1)
        self.n += 1

    def wait(self):
        self.eng.wait_ge(self.sem, self.base + self.n)

    def wait_apart(self):
        wait_apart(self.eng, self.passed, self.sem, self.base + self.n)

    def run(self, ins):
        self(ins)
        self.wait()


class Chip:
    pass


def rsqrt_guess(dve, step, out, val):
    step.run(dve.tensor_scalar(out.bitcast(I32), val.bitcast(I32), 1, None, ALU.logical_shift_right))
    step.run(dve.tensor_scalar(out.bitcast(I32), out.bitcast(I32), -1.0, float(RSQRT_MAGIC), ALU.mult, ALU.add))


def rsqrt_refine(dve, step, out, val, tmp):
    step.run(dve.scalar_tensor_tensor(tmp, out, -0.5, out, ALU.mult, ALU.mult))
    step.run(dve.tensor_tensor(tmp, tmp, val, ALU.mult))
    step.run(dve.scalar_tensor_tensor(out, tmp, 1.5, out, ALU.add, ALU.mult))


def rsqrt(dve, step, out, val, tmp):
    rsqrt_guess(dve, step, out, val)
    for _ in range(3):
        rsqrt_refine(dve, step, out, val, tmp)


def scope(nc, ctx, prefix):
    def sb(name, shape, dt=F32):
        return ctx.enter_context(nc.sbuf_tensor(f"{prefix}_{name}", shape, dt))

    def sem(name):
        return ctx.enter_context(nc.semaphore(f"{prefix}_{name}"))

    return sb, sem


def rows(ap):
    n = ap.shape[0]
    return ap.rearrange("(a n) -> a n", a=1).to_broadcast([P, n])


def setup(nc, c, a):
    with ExitStack() as ctx:
        sb, sem = scope(nc, ctx, "set")
        ids = sb("ids", [TILES, P], I32)
        ids_f = sb("ids_f", [TILES, P])
        idt = sb("idt", [P, TILES])
        sel = [sb(f"sel{n}", [P, 4, TILES]) for n in range(2)]
        ids_loaded = sem("ids_loaded")
        ids_float = sem("ids_float")
        consts = sem("consts")
        ident_ready = sem("ident_ready")
        turned = sem("turned")
        block = ctx.enter_context(nc.Block())

        @block.sync
        def _(sp):
            sp.dma_start(ids[:], a.x.rearrange("b (u p) -> (b u) p", p=P)).then_inc(ids_loaded, 16)
            sp.wait_ge(ids_loaded, 16)

        @block.gpsimd
        def _(pool):
            pool.memset(c.ident[:], 0.0).then_inc(consts, 1)
            pool.memset(c.ones[:], 1.0).then_inc(consts, 1)
            pool.wait_ge(consts, 2)
            pool.affine_select(out=c.ident[:], in_=c.ident[:], compare_op=ALU.not_equal, fill=1.0, base=0,
                               pattern=[[-1, P]], channel_multiplier=1).then_inc(ident_ready, 1)
            pool.iota(c.iota8[:], [[1, EXP]], base=0, channel_multiplier=0,
                      allow_small_or_imprecise_dtypes=True)
            pool.iota(c.tile_no[:], [[1, MOE1_TILES]], base=0, channel_multiplier=0,
                      allow_small_or_imprecise_dtypes=True)
            pool.affine_select(out=c.before[:], in_=c.ones[:], compare_op=ALU.is_gt, fill=0.0, base=0,
                               pattern=[[1, P]], channel_multiplier=-1)
            for b in (0, 2):
                pool.affine_select(out=c.causal[:, b, :], in_=c.ones[:], compare_op=ALU.is_ge, fill=0.0, base=0,
                                   pattern=[[1, P]], channel_multiplier=-1)
            pool.tensor_copy(c.causal[:, 1, :], c.ones[:])
            pool.memset(c.omega[:], 0.0).then_inc(consts, 1)
            pool.wait_ge(consts, 3)

        @block.tensor
        def _(pe):
            pe.wait_ge(ident_ready, 1)
            pe.wait_ge(ids_float, 1)
            pe.transpose(c.bank[7][:, 0:TILES], ids_f[:], c.ident[0:TILES, 0:TILES]).then_inc(turned, 1)

        @block.vector
        def _(dve):
            step = Steps(dve, sem("dve"), c.passed)
            step(dve.memset(c.proj[:], 0.0))
            step(dve.memset(c.cat[:], 0.0))
            step(dve.memset(c.zero[:], 0.0))
            step(dve.memset(c.base0[:], 0.0))
            step(dve.memset(c.base1[:], 0.0))
            dve.wait_ge(ids_loaded, 16)
            dve.tensor_copy(ids_f[:], ids[:]).then_inc(ids_float, 1)
            step(dve.memset(c.zeros[:], 0.0))
            dve.wait_ge(turned, 1)
            step.run(dve.tensor_copy(idt[:], c.bank[7][:, 0:TILES]))
            for i in range(4):
                step(dve.tensor_scalar(sel[0][:, i, :], idt[:], float(CUTS[i]), None, ALU.is_ge))
                step(dve.tensor_scalar(sel[1][:, i, :], idt[:], float(CUTS[i + 1]), None, ALU.is_lt))
            step.wait()
            step.run(dve.tensor_tensor(sel[0][:], sel[0][:], sel[1][:], ALU.mult))
            for i in range(4):
                step(dve.tensor_scalar(sel[1][:, i, :], idt[:], -float(CUTS[i] + NOWHERE), None, ALU.add))
            step.wait()
            step.run(dve.tensor_tensor(sel[0][:], sel[0][:], sel[1][:], ALU.mult))
            step.run(dve.tensor_scalar(c.token_row[:], sel[0][:], float(NOWHERE), None, ALU.add))


def first(i):
    return isinstance(i, int) and i == 0


def pair_tiles(ap, j, n=None):
    if n is None:
        return ap[:, bass.ds(j * PT, PT), :] if not isinstance(j, int) else ap[:, j * PT:(j + 1) * PT, :]
    return ap[:, bass.ds(j * PT + n, 1), :] if not isinstance(j, int) else ap[:, j * PT + n:j * PT + n + 1, :]


def two_tiles(ap, j, p):
    return ap[:, bass.ds(j * PT + p * TT, TT), :] if not isinstance(j, int) else \
        ap[:, j * PT + p * TT:j * PT + (p + 1) * TT, :]


class PairNorm:

    def __init__(self, sb, name):
        self.stats = sb(f"{name}_stats", [P, PT, 6])
        self.mv = sb(f"{name}_mv", [P, PT, 2])
        self.var = sb(f"{name}_var", [P, PT])
        self.rstd = sb(f"{name}_rstd", [P, PT])
        self.tmp = sb(f"{name}_tmp", [P, PT])


def pair_norm(dve, step, out, x, w, last, before_out=None):
    for n in range(PT):
        step(dve.bn_stats(w.stats[:, n, :], x(n)))
    step.wait_apart()
    for n in range(PT):
        step(dve.bn_aggr(w.mv[:, n, :], w.stats[:, n, :]))
    step.wait()
    step.run(dve.tensor_scalar(w.var[:], w.mv[:, :, 1], LN_EPS, None, ALU.add))
    rsqrt(dve, step, w.rstd[:], w.var[:], w.tmp[:])
    if before_out is not None:
        before_out()
    for n in range(PT):
        ins = dve.tensor_scalar(out(n), x(n), w.mv[:, n, 0:1], w.rstd[:, n:n + 1], ALU.subtract, ALU.mult)
        if n == PT - 1:
            ins.then_inc(last, 1)
        else:
            step(ins)


class PairRouting:

    def __init__(self, sb, K):
        self.best = sb("best", [P, PT, 8])
        self.best_at = sb("best_at", [P, PT, 8], U32)
        self.expert = sb("expert", [P, K, PT])
        self.hot = sb("hot", [P, K, PT, EXP])
        self.took = sb("took", [P, PT, EXP])
        self.sums = sb("sums", [P, PT + 1, EXP])
        self.two_sum = sb("two_sum", [P, EXP])
        self.pos = sb("pos", [P, PT, EXP])
        self.taken = sb("taken", [P, K, PT, EXP])
        self.rank = sb("rank", [P, K * PT])
        self.slot = sb("slot", [P, K * PT])
        self.slot_i = sb("slot_i", [P, K * PT], U32)
        self.logits = sb("logits", [P, PT, EXP])


def pair_route(dve, step, w, K):
    step.wait_apart()
    for n in range(PT):
        step(dve.max(w.best[:, n, :], w.logits[:, n, :]))
    step.wait_apart()
    for n in range(PT):
        step(dve.max_index(w.best_at[:, n, :], w.best[:, n, :], w.logits[:, n, :]))
    step.wait()
    step.run(dve.tensor_copy(w.expert[:], w.best_at[:, :, 0:K].rearrange("p t k -> p k t")))


def pair_sums(dve, step, w, took, done):
    step(dve.tensor_copy(w.sums[:, 1, :], took[:, 0, :]))
    step(dve.tensor_tensor(w.sums[:, 2, :], took[:, 0, :], took[:, 1, :], ALU.add))
    step(dve.tensor_tensor(w.two_sum[:], took[:, 2, :], took[:, 3, :], ALU.add))
    step.wait()
    step(dve.tensor_tensor(w.sums[:, 3, :], w.sums[:, 2, :], took[:, 2, :], ALU.add))
    step(dve.tensor_tensor(w.sums[:, 4, :], w.sums[:, 2, :], w.two_sum[:], ALU.add))
    step.wait()
    dve.sem_inc(done, 1)


def pair_ranks(pe, c, psum, w, took):
    pe.matmul(psum[:, 0:(PT + 1) * EXP], c.ones[:], w.sums[:].rearrange("p n e -> p (n e)"), start=True, stop=False)
    return pe.matmul(psum[:, 0:PT * EXP], c.before[:], took.rearrange("p n e -> p (n e)"), start=False, stop=True)


def pair_places(dve, step, w, K, base, psum, stride, limit, dump, done):
    step.run(dve.tensor_tensor(w.pos[:], psum[:, 0:PT * EXP].rearrange("p (t e) -> p t e", t=PT),
                               base[:].unsqueeze(1).to_broadcast([P, PT, EXP]), ALU.add))
    step(dve.tensor_tensor(base[:], base[:], psum[:, PT * EXP:(PT + 1) * EXP], ALU.add))
    for k in range(K):
        step(dve.tensor_tensor(w.taken[:, k], w.hot[:, k], w.pos[:], ALU.mult))
    step.wait()
    step.run(dve.tensor_reduce(w.rank[:], w.taken[:].rearrange("p k t e -> p (k t) e"), AX.X, ALU.add))
    ex = w.expert[:].rearrange("p k t -> p (k t)")
    step.run(dve.scalar_tensor_tensor(w.slot[:], ex, float(stride), w.rank[:], ALU.mult, ALU.add))
    if limit is None:
        dve.tensor_copy(w.slot_i[:], w.slot[:]).then_inc(done, 1)
        return
    step.run(dve.tensor_scalar(w.rank[:], w.rank[:], float(limit), None, ALU.is_lt))
    step.run(dve.scalar_tensor_tensor(w.slot[:], w.slot[:], -float(dump), w.rank[:], ALU.add, ALU.mult))
    dve.tensor_scalar(w.slot_i[:], w.slot[:], float(dump), None, ALU.add).then_inc(done, 1)


def turn_tiles(pe, c, psum, x, chunks):
    for k in range(chunks):
        for t in range(TT):
            ins = pe.transpose(psum[:, k * T + t * P:k * T + (t + 1) * P], x[:, t, k * P:(k + 1) * P], c.ident[:])
    return ins


def front(nc, c, a):
    with ExitStack() as ctx:
        sb, sem = scope(nc, ctx, "front")
        two = range(2)
        row_now = sb("row_now", [P, 4, PT], U32)
        catT = [sb(f"catT{q}", [P, KC, T]) for q in two]
        xn_next = sb("xn_next", [P, PT, D])
        xn = sb("xn", [P, PT, D])
        xn2 = sb("xn2", [P, PT, D])
        rows_out = sb("rows_out", [P, PT, D])
        xT = [sb(f"xT{q}", [P, DC, T]) for q in two]
        x2T = [sb(f"x2T{q}", [P, DC, T]) for q in two]
        qT = [sb(f"qT{q}", [P, DC, T]) for q in two]
        prob = [sb(f"prob{q}", [P, TT, T]) for q in two]
        probT = [sb(f"probT{q}", [P, TT, T]) for q in two]
        avT = [sb(f"avT{q}", [P, DC, T]) for q in two]
        norm, norm2 = PairNorm(sb, "norm"), PairNorm(sb, "norm2")
        smax = sb("smax", [P, PT])
        nmax = sb("nmax", [P, PT])
        total = sb("total", [P, PT])
        w = PairRouting(sb, 2)
        gap = sb("gap", [P, PT])
        egap = sb("egap", [P, PT])
        gate = sb("gate", [P, 2, PT])
        SEMS = ("indexed cleared cat_turned catT_ready emb_ready h_ready x_ready x_kept x_turned xT_ready "
                "q_made qT_ready s_made nmax_ready prob_ready p_turned pT_ready av_made avT_ready o_made o_part o_added "
                "x2_ready x2_turned x2T_ready rows_ready l_made took_ready r_made slots_ready gap_ready egap_ready "
                "kept").split()
        s = {n: sem(n) for n in SEMS}
        gathered = sem("gathered")
        wqkv = sb("wqkv", [P, 6, D])
        wout = sb("wout", [P, DC, D])
        gate_w = sb("gate_w", [EXP, D])
        b1 = sb("b1", [EXP * HID0 // P, P])
        feature_tmp = [sb(f"feature_tmp{n}", [P, 2]) for n in range(4)]
        proj_loaded, attn_loaded, turn_loaded, nodes_loaded, late_loaded, rows_zeroed = (
            sem(n) for n in ("proj_loaded", "attn_loaded", "turn_loaded", "nodes_loaded", "late_loaded",
                             "rows_zeroed"))
        w_turned, w_moved = sem("w_turned"), sem("w_moved")
        jobs = [(c.projT[:, k, m * P:(m + 1) * P], c.proj[:, m, k * P:(k + 1) * P])
                for m in range(DC) for k in range(KC)]
        proj_jobs = len(jobs)
        jobs += [(c.wqkvT[:, k, m * P:(m + 1) * P], wqkv[:, m, k * P:(k + 1) * P])
                 for m in range(6) for k in range(DC)]
        jobs += [(c.woutT[:, k, m * P:(m + 1) * P], wout[:, m, k * P:(k + 1) * P])
                 for m in range(DC) for k in range(DC)]
        jobs += [(c.gateT[:, k, :], gate_w[:, k * P:(k + 1) * P]) for k in range(DC)]
        jobs += [(c.b1T[:], b1[:])]
        sent = sem("sent")
        block = ctx.enter_context(nc.Block())
        Q, S, E, X = 0, 2, 4, 6

        def flat(x):
            return x[:].rearrange("p k t -> p (k t)")

        @block.sync
        def _(sp):
            for i in range(4):
                sp.dma_start(c.proj[:, :, EMB_AT[i]:EMB_AT[i] + EMB_D[i]],
                             a.proj[i].rearrange("(u p) d -> p u d", p=P)).then_inc(proj_loaded, 16)
            for buf, src in ((c.QK, a.QK), (c.VO, a.VO), (c.Wr, a.Wr)):
                sp.dma_start(buf[:], src.rearrange("(k p) n -> p k n", p=P)).then_inc(attn_loaded, 16)
            sp.dma_start(c.br[:], rows(a.br)).then_inc(attn_loaded, 16)
            sp.dma_start(wqkv[:], a.w_qkv.rearrange("(u p) d -> p u d", p=P)).then_inc(turn_loaded, 16)
            sp.dma_start(wout[:], a.w_out.rearrange("(u p) d -> p u d", p=P)).then_inc(turn_loaded, 16)
            sp.dma_start(gate_w[:], a.gate_w).then_inc(turn_loaded, 16)
            sp.dma_start(b1[:], a.b1.rearrange("e (m p) -> (e m) p", p=P)).then_inc(turn_loaded, 16)
            sp.dma_start(c.nodes[:], rows(a.nodes)).then_inc(nodes_loaded, 16)
            sp.dma_start(c.qw[:], rows(a.qw)).then_inc(nodes_loaded, 16)
            sp.wait_ge(gathered, 16 * 4 * PT)
            per = 2048 // D * P
            for i in range(EXP * CAP // per):
                sp.dma_start(a.xg0[i * per:(i + 1) * per, :].rearrange("(p r) d -> p (r d)", p=P),
                             c.zeros[:]).then_inc(rows_zeroed, 16)
            sp.dma_start(a.y0[EXP * CAP:EXP * CAP + 1, :], c.zeros[0:1, 0:D]).then_inc(late_loaded, 16)
            sp.dma_start(a.xg1[EXP * REGION:EXP * REGION + P, :], c.zeros[:, 0:D]).then_inc(late_loaded, 16)
            for buf, src in ((c.bqkv, a.b_qkv), (c.bout, a.b_out), (c.gamma, a.gamma), (c.beta, a.beta)):
                sp.dma_start(buf[:], rows(src)).then_inc(late_loaded, 16)
            for h in range(HEADS):
                r0 = HD * (h % 8)
                hh = h % 2
                sp.dma_start(c.omega[r0:r0 + HD, h // 2, hh * NF:(hh + 1) * NF].rearrange(
                    "d (r m) -> d r m", r=2), a.omega[:, h].rearrange("r d m -> d r m")).then_inc(late_loaded, 16)
            sp.wait_ge(late_loaded, 16 * (6 + HEADS))

        @block.gpsimd
        def _(pool):
            def gather(j):
                wait_apart(pool, c.passed, s["indexed"], j + 1)
                wait_apart(pool, c.passed, s["cleared"], j + 1)
                for i in range(4):
                    for n in range(PT):
                        pool.indirect_dma_start(
                            c.cat[:, n, EMB_AT[i]:EMB_AT[i] + EMB_D[i]], None, a.emb[i],
                            bass.IndirectOffsetOnAxis(ap=row_now[:, i, n:n + 1], axis=0),
                            bounds_check=CUTS[i + 1] - CUTS[i] - 1, oob_is_err=False).then_inc(gathered, 16)

            def send(j):
                wait_apart(pool, c.passed, s["rows_ready"], j + 1)
                wait_apart(pool, c.passed, s["slots_ready"], j + 1)
                for k in two:
                    for n in range(PT):
                        pool.indirect_dma_start(
                            a.xg0, bass.IndirectOffsetOnAxis(ap=w.slot_i[:, k * PT + n:k * PT + n + 1], axis=0),
                            rows_out[:, n, :], None, bounds_check=EXP * CAP - 1,
                            oob_is_err=False).then_inc(sent, 16)
                pool.tensor_copy(c.place0[:, bass.ds(j, 1), :], w.slot_i[:].unsqueeze(1))
                pool.tensor_copy(c.gates[:, bass.ds(j, 1), :], gate[:].rearrange("p (a k) n -> p a (k n)", a=1))\
                    .then_inc(s["kept"], 1)

            with pool.Fori(0, 3) as j:
                gather(j)
            pool.wait_ge(rows_zeroed, 16 * (EXP * CAP * D // (2048 * P)))
            with pool.Fori(1, PAIRS - 2) as j:
                gather(j + 2)
                send(j - 1)
            with pool.Fori(PAIRS - 3, PAIRS) as j:
                send(j)
            pool.wait_ge(sent, 16 * 2 * PT * PAIRS)

        @block.tensor
        def _(pe):
            def turn_rows(j, p):
                if p == 0:
                    pe.wait_ge(gathered, (j + 1) * (16 * 4 * PT))
                    if not first(j):
                        pe.wait_ge(s["h_ready"], turn(j - 1, 1))
                else:
                    pe.wait_ge(s["catT_ready"], turn(j, 0))
                for k in range(KC):
                    for t in range(TT):
                        ins = pe.transpose(c.bank[E + k // 2][:, (k % 2) * T + t * P:(k % 2) * T + (t + 1) * P],
                                           c.cat[:, p * TT + t, k * P:(k + 1) * P], c.ident[:])
                ins.then_inc(s["cat_turned"], 1)

            def embed(j, p):
                pe.wait_ge(s["catT_ready"], turn(j, 1))
                for t in range(TT):
                    for k in range(KC):
                        ins = pe.matmul(c.bank[E + p][:, t * D:(t + 1) * D], catT[p][:, k, t * P:(t + 1) * P],
                                        c.projT[:, k, :], start=k == 0, stop=k == KC - 1)
                ins.then_inc(s["emb_ready"], 1)

            def turn_x(j):
                pe.wait_ge(s["x_ready"], j + 1)
                for p in two:
                    turn_tiles(pe, c, c.bank[S + p], xn_next[:, p * TT:(p + 1) * TT], DC).then_inc(s["x_turned"], 1)

            def queries(j):
                if not first(j):
                    pe.wait_ge(s["o_added"], j)
                for p in two:
                    pe.wait_ge(s["xT_ready"], turn(j, p))
                    for m in range(DC):
                        for k in range(DC):
                            ins = pe.matmul(c.bank[Q + p][:, m * T:(m + 1) * T], c.QK[:, k, m * P:(m + 1) * P],
                                            xT[p][:, k, :], start=k == 0, stop=k == DC - 1)
                    ins.then_inc(s["q_made"], 1)

            def scores(j):
                for p in two:
                    pe.wait_ge(s["qT_ready"], turn(j, p))
                    for t in range(TT):
                        for k in range(DC):
                            ins = pe.matmul(c.bank[S + p][:, t * T:(t + 1) * T], qT[p][:, k, t * P:(t + 1) * P],
                                            xT[p][:, k, :], start=k == 0, stop=k == DC - 1)
                ins.then_inc(s["s_made"], 1)

            def turn_x2(j):
                if not first(j):
                    pe.wait_ge(s["slots_ready"], j)
                pe.wait_ge(s["x2_ready"], j + 1)
                for p in two:
                    turn_tiles(pe, c, c.bank[X + p], xn2[:, p * TT:(p + 1) * TT], DC).then_inc(s["x2_turned"], 1)

            def router(j):
                pe.wait_ge(s["x2T_ready"], turn(j, 1))
                for n in range(PT):
                    for k in range(DC):
                        t = n % TT
                        ins = pe.matmul(c.bank[X][:, n * EXP:(n + 1) * EXP], x2T[n // TT][:, k, t * P:(t + 1) * P],
                                        c.Wr[:, k, :], start=k == 0, stop=k == DC - 1)
                ins.then_inc(s["l_made"], 1)

            def average(j):
                for p in two:
                    pe.wait_ge(s["prob_ready"], j * PT + (p + 1) * TT)
                    turn_tiles(pe, c, c.bank[Q + p], prob[p], TT).then_inc(s["p_turned"], 1)
                for p in two:
                    pe.wait_ge(s["pT_ready"], turn(j, p))
                    if p == 0:
                        pe.wait_ge(s["x_kept"], j + 1)
                    for m in range(DC):
                        for k in range(TT):
                            ins = pe.matmul(c.bank[S + p][:, m * T:(m + 1) * T],
                                            xn[:, p * TT + k, m * P:(m + 1) * P],
                                            probT[p][:, k, :], start=k == 0, stop=k == TT - 1)
                    ins.then_inc(s["av_made"], 1)

            def project(j):
                for p in two:
                    pe.wait_ge(s["avT_ready"], turn(j, p))
                    for t in range(TT):
                        for k in range(DC):
                            ins = pe.matmul(c.bank[Q + p][:, t * D:(t + 1) * D], avT[p][:, k, t * P:(t + 1) * P],
                                            c.VO[:, k, :], start=k == 0, stop=k == DC - 1)
                ins.then_inc(s["o_made"], 1)

            def ranks(j):
                pe.wait_ge(s["took_ready"], j + 1)
                pair_ranks(pe, c, c.bank[X + 1], w, w.took[:]).then_inc(s["r_made"], 1)

            def pair(j, before, after):
                queries(j)
                if after:
                    turn_rows(j + 1, 0)
                scores(j)
                if after:
                    turn_rows(j + 1, 1)
                if before:
                    turn_x2(j - 1)
                if after:
                    embed(j + 1, 0)
                if before:
                    router(j - 1)
                if after:
                    embed(j + 1, 1)
                average(j)
                project(j)
                if after:
                    turn_x(j + 1)
                if before:
                    ranks(j - 1)

            pe.wait_ge(proj_loaded, 16 * 4)
            for n in range(0, len(jobs), 4):
                if n == proj_jobs:
                    pe.wait_ge(turn_loaded, 16 * 4)
                if n >= 28:
                    pe.wait_ge(w_moved, n - 24)
                for k, (dst, src) in enumerate(jobs[n:n + 4]):
                    m = src.shape[0]
                    ins = pe.transpose(c.bank[n // 4 % 7][:, k * P:k * P + m], src, c.ident[0:m, 0:m])
                ins.then_inc(w_turned, 1)
            pe.wait_ge(w_moved, len(jobs))
            turn_rows(0, 0)
            turn_rows(0, 1)
            embed(0, 0)
            embed(0, 1)
            turn_x(0)
            pe.wait_ge(attn_loaded, 16 * 4)
            pair(0, False, True)
            pair(1, True, True)
            with pe.Fori(2, PAIRS - 1) as j:
                pair(j, True, True)
            pair(PAIRS - 1, True, False)
            turn_x2(PAIRS - 1)
            router(PAIRS - 1)
            ranks(PAIRS - 1)

        @block.scalar
        def _(act):
            def copy_rows(j, p):
                act.wait_ge(s["cat_turned"], turn(j, p))
                if not first(j):
                    act.wait_ge(s["emb_ready"], turn(j - 1, p))
                act.activation(catT[p][:].rearrange("p (b k) t -> p b (k t)", b=2), c.ps[:, E:E + 2, :], ACT.Copy)\
                    .then_inc(s["catT_ready"], 1)

            def hidden(j, p):
                wait_apart(act, c.passed, s["emb_ready"], turn(j, p))
                act.activation(two_tiles(c.h, j, p), c.bank[E + p][:].rearrange("p (t d) -> p t d", t=TT), ACT.Copy,
                               scale=EMB_SCALE).then_inc(s["h_ready"], 1)

            def copy_x(j):
                for p in two:
                    act.wait_ge(s["x_turned"], turn(j, p))
                    act.activation(flat(xT[p]), c.bank[S + p][:], ACT.Copy).then_inc(s["xT_ready"], 1)
                if not first(j):
                    act.wait_ge(s["av_made"], turn(j - 1, 1))
                act.activation(xn[:], xn_next[:], ACT.Copy).then_inc(s["x_kept"], 1)

            def rows_copy(j):
                if not first(j):
                    act.wait_ge(sent, j * (16 * 2 * PT))
                act.activation(rows_out[:], xn2[:], ACT.Copy).then_inc(s["rows_ready"], 1)

            def copy_x2(j):
                for p in two:
                    act.wait_ge(s["x2_turned"], turn(j, p))
                    act.activation(flat(x2T[p]), c.bank[X + p][:], ACT.Copy).then_inc(s["x2T_ready"], 1)

            def egaps(j):
                act.wait_ge(s["gap_ready"], j + 1)
                act.activation(egap[:], gap[:], ACT.Exp).then_inc(s["egap_ready"], 1)

            def pair(j, before, after):
                for p in two:
                    act.wait_ge(s["q_made"], turn(j, p))
                    act.activation(flat(qT[p]), c.bank[Q + p][:], ACT.Copy).then_inc(s["qT_ready"], 1)
                if after:
                    copy_rows(j + 1, 0)
                    copy_rows(j + 1, 1)
                act.wait_ge(s["nmax_ready"], j + 1)
                for n in range(PT):
                    t = n % TT
                    act.activation(prob[n // TT][:, t, :], c.bank[S + n // TT][:, t * T:(t + 1) * T], ACT.Exp,
                                   bias=nmax[:, n:n + 1], scale=ATT_SCALE,
                                   accum_out=total[:, n:n + 1]).then_inc(s["prob_ready"], 1)
                if before:
                    copy_x2(j - 1)
                if after:
                    hidden(j + 1, 0)
                    hidden(j + 1, 1)
                for p in two:
                    act.wait_ge(s["p_turned"], turn(j, p))
                    act.activation(flat(probT[p]), c.bank[Q + p][:], ACT.Copy).then_inc(s["pT_ready"], 1)
                if before:
                    egaps(j - 1)
                for p in two:
                    act.wait_ge(s["av_made"], turn(j, p))
                    act.activation(flat(avT[p]), c.bank[S + p][:], ACT.Copy).then_inc(s["avT_ready"], 1)
                if before:
                    rows_copy(j - 1)
                if after:
                    copy_x(j + 1)

            copy_rows(0, 0)
            copy_rows(0, 1)
            hidden(0, 0)
            hidden(0, 1)
            copy_x(0)
            pair(0, False, True)
            pair(1, True, True)
            with act.Fori(2, PAIRS - 1) as j:
                pair(j, True, True)
            pair(PAIRS - 1, True, False)
            copy_x2(PAIRS - 1)
            rows_copy(PAIRS - 1)
            egaps(PAIRS - 1)

        @block.vector
        def _(dve):
            step = Steps(dve, sem("dve"), c.passed)

            def index(j):
                at = bass.ds(j * PT, PT) if not isinstance(j, int) else slice(j * PT, (j + 1) * PT)
                dve.tensor_copy(row_now[:], c.token_row[:, :, at]).then_inc(s["indexed"], 1)

            def clear(j):
                dve.wait_ge(s["cat_turned"], turn(j - 1, 1))
                dve.memset(c.cat[:, :, 0:400], 0.0).then_inc(s["cleared"], 1)
                index(j)

            def norm_x(j):
                wait_apart(dve, c.passed, s["h_ready"], turn(j, 1))

                def free():
                    if not first(j):
                        dve.wait_ge(s["x_kept"], j)
                        dve.wait_ge(s["x_turned"], turn(j - 1, 1))
                pair_norm(dve, step, lambda n: xn_next[:, n:n + 1, :], lambda n: pair_tiles(c.h, j, n), norm,
                          s["x_ready"], free)

            def maxima(j):
                dve.wait_ge(s["s_made"], j + 1)
                step.run(dve.tensor_reduce(smax[:], c.ps[:, S:S + 2, :].rearrange("p s (t u) -> p (s t) u", t=TT),
                                           AX.X, ALU.max))
                dve.tensor_scalar(nmax[:], smax[:], -ATT_SCALE, None, ALU.mult).then_inc(s["nmax_ready"], 1)

            def add_norm(j):
                step.run(dve.reciprocal(total[:], total[:]))
                dve.wait_ge(s["o_made"], j + 1)
                for n in range(PT):
                    hn = pair_tiles(c.h, j, n)
                    t = n % TT
                    dve.scalar_tensor_tensor(
                        hn, c.bank[Q + n // TT][:, t * D:(t + 1) * D].unsqueeze(1), total[:, n:n + 1], hn,
                        ALU.mult, ALU.add).then_inc(s["o_part"], 1)
                wait_apart(dve, c.passed, s["o_part"], (j + 1) * PT)
                dve.sem_inc(s["o_added"], 1)

                def free():
                    if not first(j):
                        dve.wait_ge(s["rows_ready"], j)
                pair_norm(dve, step, lambda n: xn2[:, n:n + 1, :], lambda n: pair_tiles(c.h, j, n), norm2,
                          s["x2_ready"], free)

            def choose(j):
                dve.wait_ge(s["l_made"], j + 1)
                step(dve.tensor_tensor(w.logits[:], c.bank[X][:, 0:PT * EXP].rearrange("p (t e) -> p t e", t=PT),
                                       c.br[:].unsqueeze(1).to_broadcast([P, PT, EXP]), ALU.add))
                pair_route(dve, step, w, 2)
                dve.tensor_tensor(gap[:], w.best[:, :, 1], w.best[:, :, 0], ALU.subtract).then_inc(s["gap_ready"], 1)
                for k in two:
                    step(dve.tensor_tensor(w.hot[:, k], c.iota8[:].unsqueeze(1).to_broadcast([P, PT, EXP]),
                                           w.expert[:, k, :].unsqueeze(2).to_broadcast([P, PT, EXP]),
                                           ALU.is_equal))
                step.wait()
                step.run(dve.tensor_tensor(w.took[:], w.hot[:, 0], w.hot[:, 1], ALU.add))
                pair_sums(dve, step, w, w.took, s["took_ready"])

            def place(j):
                if not first(j):
                    dve.wait_ge(s["kept"], j)
                    dve.wait_ge(sent, j * (16 * 2 * PT))
                dve.wait_ge(s["egap_ready"], j + 1)
                step.run(dve.tensor_scalar(gap[:], egap[:], 1.0, None, ALU.add))
                step.run(dve.reciprocal(gate[:, 0, :], gap[:]))
                step(dve.tensor_tensor(gate[:, 1, :], gate[:, 0, :], egap[:], ALU.mult))
                dve.wait_ge(s["r_made"], j + 1)
                pair_places(dve, step, w, 2, c.base0, c.bank[X + 1], CAP, CAP, EXP * CAP, s["slots_ready"])

            index(0)
            dve.sem_inc(s["cleared"], 1)
            for n in range(0, len(jobs), 4):
                dve.wait_ge(w_turned, n // 4 + 1)
                for k, (dst, src) in enumerate(jobs[n:n + 4]):
                    m = src.shape[0]
                    dve.tensor_copy(dst, c.bank[n // 4 % 7][:, k * P:k * P + m]).then_inc(w_moved, 1)
            step.begin(0)
            dve.wait_ge(nodes_loaded, 16 * 2)
            clip, root, tmp, big = feature_tmp
            for src, scale, dst in ((c.nodes, 2.0, c.f_scale), (c.qw, 1.0, c.f_weight)):
                step.run(dve.tensor_scalar(clip[:], src[:], 0.0, scale, ALU.max, ALU.mult))
                step.run(dve.tensor_scalar(big[:], clip[:], 1e-30, None, ALU.max))
                rsqrt(dve, step, root[:], big[:], tmp[:])
                step.run(dve.tensor_tensor(root[:], root[:], clip[:], ALU.mult))
                f = 1.0 if dst is c.f_scale else 1.0 / FEAT
                for g in range(4):
                    step(dve.tensor_scalar(dst[g * 32:(g + 1) * 32, :], root[g * 32:(g + 1) * 32, g % 2:g % 2 + 1],
                                           f, None, ALU.mult))
                step.wait()
            for g in range(4):
                step(dve.tensor_scalar(c.f_shift[g * 32:(g + 1) * 32, :],
                                       c.nodes[g * 32:(g + 1) * 32, g % 2:g % 2 + 1], -1.0, None, ALU.mult))
            dve.wait_ge(attn_loaded, 16 * 4)
            step(dve.memset(w.sums[:, 0, :], 0.0))
            clear(1)
            norm_x(0)
            maxima(0)
            clear(2)
            norm_x(1)
            add_norm(0)

            def pair(j):
                maxima(j)
                clear(j + 2)
                choose(j - 1)
                norm_x(j + 1)
                add_norm(j)
                place(j - 1)

            pair(1)
            start = step.n
            with dve.Fori(2, PAIRS - 2) as j:
                step.begin((j - 2) * FRONT_STEPS + start)
                pair(j)
                assert step.n == FRONT_STEPS, step.n
            step.begin((PAIRS - 4) * FRONT_STEPS + start)
            for j in (PAIRS - 2, PAIRS - 1):
                maxima(j)
                choose(j - 1)
                if j == PAIRS - 2:
                    norm_x(j + 1)
                add_norm(j)
                place(j - 1)
            choose(PAIRS - 1)
            place(PAIRS - 1)


def moe2(nc, c, a):
    with ExitStack() as ctx:
        sb, sem = scope(nc, ctx, "moe2")
        two = range(2)
        G = 512
        GROUPS = CAP // G
        GT = G // P
        HC = HID0 // P
        W1 = [sb(f"W1{q}", [P, DC, HID0]) for q in two]
        W2 = [sb(f"W2{q}", [P, HC, D]) for q in two]
        b2 = [sb(f"b2{q}", [P, D]) for q in two]
        x = [sb(f"x{q}", [P, GT, D]) for q in two]
        xT = [sb(f"xT{q}", [P, DC, G]) for q in two]
        hT = [sb(f"hT{q}", [P, HC, G]) for q in two]
        y = [sb(f"y{q}", [P, GT, D]) for q in two]
        w_loaded = [sem(f"w_loaded{q}") for q in two]
        x_loaded = [sem(f"x_loaded{q}") for q in two]
        stored = sem("stored")
        names = "x_turned xT_left xT_right h_made h_ready y_made y_ready y_stored".split()
        s = {n: sem(n) for n in names}
        EXPERTS = EXP // 2
        block = ctx.enter_context(nc.Block())

        def unit(j, p, g):
            return j * (2 * GROUPS) + p * GROUPS + g

        @block.sync
        def _(sp):
            def load_w(e, p):
                def of(ap):
                    return ap[bass.ds(e, 1)] if not isinstance(e, int) else ap[e:e + 1]
                sp.dma_start(W1[p][:], of(a.W1).rearrange("e (k p) n -> p (e k) n", p=P)).then_inc(w_loaded[p], 16)
                sp.dma_start(W2[p][:], of(a.W2).rearrange("e (k p) n -> p (e k) n", p=P)).then_inc(w_loaded[p], 16)
                sp.dma_start(b2[p][:], of(a.b2).to_broadcast([P, D])).then_inc(w_loaded[p], 16)

            def load_x(u, g):
                r = bass.ds(u * G, G) if not isinstance(u, int) else slice(u * G, (u + 1) * G)
                sp.dma_start(x[g][:], a.xg0[r, :].rearrange("(t p) d -> p t d", p=P)).then_inc(x_loaded[g], 16)

            load_x(0, 0)
            load_w(0, 0)
            load_x(1, 1)
            load_w(1, 1)

            def pair(j, more):
                for g in range(GROUPS):
                    sp.wait_ge(s["x_turned"], unit(j, 0, g) + 1)
                    load_x(unit(j, 1, g), g)
                if not more:
                    return
                for p in two:
                    if p == 0:
                        for g in range(GROUPS):
                            sp.wait_ge(s["x_turned"], unit(j, 1, g) + 1)
                            load_x(unit(j + 1, 0, g), g)
                            if g == 0:
                                sp.wait_ge(s["y_ready"], unit(j, 1, 0) * GT + 1)
                                load_w((j + 1) * 2, 0)
                    else:
                        sp.wait_ge(s["y_ready"], unit(j + 1, 0, 0) * GT + 1)
                        load_w((j + 1) * 2 + 1, 1)

            with sp.Fori(0, EXPERTS - 1) as j:
                pair(j, True)
            pair(EXPERTS - 1, False)

        @block.gpsimd
        def _(pool):
            pool.sem_inc(s["y_stored"], 2)
            with pool.Fori(0, EXPERTS) as j:
                for p in two:
                    for g in range(GROUPS):
                        u = unit(j, p, g)
                        pool.wait_ge(s["y_ready"], (u + 1) * GT + 1)
                        pool.dma_start(a.y0[bass.ds(u * G, G), :].rearrange("(t p) d -> p t d", p=P), y[g][:])\
                            .then_inc(stored, 16)
                        pool.wait_ge(stored, (u + 1) * 16)
                        pool.sem_inc(s["y_stored"], 1)

        @block.tensor
        def _(pe):
            with pe.Fori(0, EXPERTS) as j:
                def turn_x(p, g):
                    pe.wait_ge(x_loaded[g], 16 * (2 * j + p + 1))
                    for k in range(DC):
                        for t in range(GT):
                            ins = pe.transpose(c.bank[k][:, t * P:(t + 1) * P], x[g][:, t, k * P:(k + 1) * P],
                                               c.ident[:])
                    ins.then_inc(s["x_turned"], 1)

                for p in two:
                    pe.wait_ge(w_loaded[p], 48 * (j + 1))
                    for g in range(GROUPS):
                        u = unit(j, p, g)
                        if (p, g) == (0, 0):
                            turn_x(0, 0)
                        pe.wait_ge(s["xT_left"], u + 1)
                        pe.wait_ge(s["xT_right"], u + 1)
                        for m in range(HC):
                            if m >= 3:
                                pe.wait_ge(s["h_ready"], u * HC + m - 2)
                            for k in range(DC):
                                ins = pe.matmul(c.bank[2 + m % 3][:], W1[p][:, k, m * P:(m + 1) * P], xT[g][:, k, :],
                                                start=k == 0, stop=k == DC - 1)
                            ins.then_inc(s["h_made"], 1)
                        if (p, g) != (1, 1):
                            turn_x(p + (g + 1) // GROUPS, (g + 1) % GROUPS)
                        pe.wait_ge(s["h_ready"], (u + 1) * HC)
                        for t in range(GT):
                            pe.wait_ge(s["y_ready"], u * GT + max(t - 1, 0) + 1)
                            for k in range(HC):
                                ins = pe.matmul(c.bank[6 + t % 2][:, 0:D], hT[g][:, k, t * P:(t + 1) * P], W2[p][:, k, :],
                                                start=k == 0, stop=k == HC - 1)
                            ins.then_inc(s["y_made"], 1)

        @block.scalar
        def _(act):
            with act.Fori(0, EXPERTS) as j:
                def move(p, g):
                    u = unit(j, p, g)
                    act.wait_ge(s["x_turned"], u + 1)
                    act.activation(xT[g][:, 1, :], c.bank[1][:], ACT.Copy).then_inc(s["xT_right"], 1)

                for p in two:
                    for g in range(GROUPS):
                        u = unit(j, p, g)
                        if (p, g) == (0, 0):
                            move(0, 0)
                        for m in range(HC):
                            wait_apart(act, c.passed, s["h_made"], u * HC + m + 1)
                            act.activation(hT[g][:, m, :], c.bank[2 + m % 3][:], ACT.Gelu,
                                           bias=c.b1T[:, bass.ds((2 * j + p) * HC + m, 1)])\
                                .then_inc(s["h_ready"], 1)
                        if (p, g) != (1, 1):
                            move(p + (g + 1) // GROUPS, (g + 1) % GROUPS)

        @block.vector
        def _(dve):
            dve.sem_inc(s["y_ready"], 1)
            with dve.Fori(0, EXPERTS) as j:
                def move(p, g):
                    u = unit(j, p, g)
                    dve.wait_ge(s["x_turned"], u + 1)
                    dve.tensor_copy(xT[g][:, 0, :], c.bank[0][:]).then_inc(s["xT_left"], 1)

                for p in two:
                    dve.wait_ge(w_loaded[p], 48 * (j + 1))
                    for g in range(GROUPS):
                        u = unit(j, p, g)
                        if (p, g) == (0, 0):
                            move(0, 0)
                        if (p, g) != (1, 1):
                            move(p + (g + 1) // GROUPS, (g + 1) % GROUPS)
                        dve.wait_ge(s["y_stored"], u + 1)
                        for t in range(GT):
                            dve.wait_ge(s["y_made"], u * GT + t + 1)
                            dve.tensor_tensor(y[g][:, t, :], c.bank[6 + t % 2][:, 0:D], b2[p][:], ALU.add)\
                                .then_inc(s["y_ready"], 1)


def linear(nc, c, a):
    with ExitStack() as ctx:
        sb, sem = scope(nc, ctx, "lin")
        two = range(2)
        GP = HEADS // 2
        UNITS = 2 * GP
        RING, AT_RING, LEAD = 4, 2, 4
        V1 = HD + 1
        HALF = GP // 2
        yrow = sb("yrow", [P, 2 * PT, D])
        place_now = sb("place_now", [P, 2 * PT], U32)
        gate_now = sb("gate_now", [P, 2 * PT])
        xn = sb("xn", [P, PT, D])
        xT = [sb(f"xT{p}", [P, DC, T]) for p in two]
        qk = sb("qk", [P, 2, TT, 2 * D])
        sq = [sb(f"sq{p}", [P, TT, 2 * D]) for p in two]
        NG = TT * 2 * HEADS
        ss, rn, rtmp = (sb(n, [P, 2 * NG]) for n in ("ss", "rn", "rtmp"))
        norm = PairNorm(sb, "norm")
        shift = sb("shift", [P, PT])
        ctxT = [sb(f"ctxT{p}", [P, DC, T]) for p in two]
        x2n = sb("x2n", [P, PT, D])
        x2T = [sb(f"x2T{p}", [P, DC, T]) for p in two]
        lT = sb("lT", [EXP, PT * P])
        rows_out = sb("rows_out", [P, PT, D])
        norm2 = PairNorm(sb, "norm2")
        shift2 = sb("shift2", [P, PT])
        w = PairRouting(sb, 1)
        MT = MOE1_TILES
        tiles_i = sb("tiles_i", [P, EXP], I32)
        tail_i = sb("tail_i", [P, EXP], I32)
        past = sb("past", [P, MT, EXP])
        ej = sb("ej", [P, MT])
        before = sb("before", [P, MT])
        row = sb("row", [P, MT])
        nbest = sb("nbest", [P, PT])
        prob = sb("prob", [P, PT, EXP])
        psum_p = sb("psum_p", [P, PT])
        tv = sb("tv", [P, PT])
        placed = sb("placed", [P, PT])
        ctxv = [sb(f"ctxv{q}", [P, PT, D]) for q in two]
        zT = [sb(f"zT{q}", [P, 2, DC, 2 * T]) for q in two]
        vone = [sb(f"vone{q}", [P, 2, TT, HEADS, V1]) for q in two]
        ex = [sb(f"ex{n}", [P, 2 * T]) for n in range(RING)]
        pr2 = [sb(f"pr2{n}", [P, 2 * T]) for n in range(RING)]
        feat = [sb(f"feat{n}", [P, 2 * T]) for n in range(RING)]
        attn = [sb(f"attn{n}", [P, 2, 3, P]) for n in range(AT_RING)]
        den = sb("den", [P, TT, HEADS // 2])
        SEMS = ("copied weighted rows_summed h_summed length_known norm_known x_ready bout_added "
                "x_turned xT_ready qk_made qk_ready v_made v_ready sq_ready sq_read z_ready z_turned zT_ready "
                "ctx_turned ctxT_ready o_made o_added norm2_known x2_ready x2_turned x2T_ready rows_ready "
                "lT_made lT_ready l_made logits_ready nbest_ready prob_ready took_ready r_made slots_ready kept rows_sent beta_added "
                "f_made ex_ready pr2_ready clipped feat_ready a_made a_masked av_made ctx_ready").split()
        s = {n: sem(n) for n in SEMS}
        fetched = sem("fetched")
        sent = sem("sent")
        w_loaded = sem("w_loaded")
        tails_known = sem("tails_known")
        tails = sem("tails")
        block = ctx.enter_context(nc.Block())
        F_BANK, A_BANKS, AV_BANK = c.bank[0], 2, c.bank[6]
        E = (c.bank[1], c.bank[7])

        AHEAD = {"ex_ready": 1, "pr2_ready": 1, "feat_ready": RING, "a_made": RING, "a_masked": 2,
                 "av_made": AT_RING, "ctx_ready": 1, "rows_sent": 1}

        def made(j, u, name=None):
            return j * UNITS + u + 1 + AHEAD.get(name, 0)

        def freed(j, u):
            return j * UNITS + u + 1

        def a_banks(u):
            return c.ps[:, A_BANKS + 2 * (u % 2):A_BANKS + 2 + 2 * (u % 2), :]

        def parity(q, u):
            return (q + u // UNITS) % 2

        def zero_tails(engine, half):
            engine.wait_ge(tails_known, 1)
            for e in range(half * EXP // 2, (half + 1) * EXP // 2):
                r = engine.value_load(tail_i[0:1, e:e + 1], min_val=e * REGION, max_val=e * REGION + N)
                engine.dma_start(a.xg1[bass.ds(r, P), :], c.zero[:, 0:D]).then_inc(tails, 16)

        @block.sync
        def _(sp):
            sp.wait_ge(s["x_ready"], 3)
            for e in range(EXP):
                sp.dma_start(c.W1[:, DC * e:DC * (e + 1), :], a.ew1[e].rearrange("(k p) n -> p k n", p=P))\
                    .then_inc(w_loaded, 16)
            sp.wait_ge(w_loaded, 16 * EXP)
            zero_tails(sp, 0)
            sp.wait_ge(tails, 16 * EXP)

        @block.gpsimd
        def _(pool):
            def fetch(j):
                at = bass.ds(j, 1) if not isinstance(j, int) else slice(j, j + 1)
                pool.tensor_copy(place_now[:].unsqueeze(1), c.place0[:, at, :])
                pool.tensor_copy(gate_now[:].unsqueeze(1), c.gates[:, at, :]).then_inc(s["copied"], 1)
                wait_apart(pool, c.passed, s["copied"], j + 1)
                for n in range(2 * PT):
                    pool.indirect_dma_start(
                        yrow[:, n, :], None, a.y0,
                        bass.IndirectOffsetOnAxis(ap=place_now[:, n:n + 1], axis=0),
                        bounds_check=EXP * CAP, oob_is_err=False).then_inc(fetched, 16)

            def add_experts(j):
                wait_apart(pool, c.passed, s["weighted"], (j + 1) * (2 * PT))
                pool.tensor_tensor(yrow[:, 0:PT, :], yrow[:, 0:PT, :], yrow[:, PT:2 * PT, :], ALU.add)\
                    .then_inc(s["rows_summed"], 1)
                wait_apart(pool, c.passed, s["rows_summed"], j + 1)
                hj = pair_tiles(c.h, j)
                pool.tensor_tensor(hj, hj, yrow[:, 0:PT, :], ALU.add).then_inc(s["h_summed"], 1)

            def add_bout(j):
                wait_apart(pool, c.passed, s["x_ready"], j + 1)
                hj = pair_tiles(c.h, j)
                pool.tensor_tensor(hj, hj, c.bout[:].unsqueeze(1).to_broadcast([P, PT, D]), ALU.add)\
                    .then_inc(s["bout_added"], 1)

            def unit_vectors(j):
                wait_apart(pool, c.passed, s["length_known"], j + 1)
                for p in two:
                    z = qk[:, p].rearrange("p t (g e) -> p (t g) e", e=HD)
                    pool.tensor_tensor(z, z, rn[:, p * NG:(p + 1) * NG].unsqueeze(2).to_broadcast([P, NG, HD]),
                                       ALU.mult).then_inc(s["z_ready"], 1)

            def refetch(j):
                wait_apart(pool, c.passed, s["h_summed"], j)
                fetch(j)

            def send(j):
                wait_apart(pool, c.passed, s["slots_ready"], j + 1)
                wait_apart(pool, c.passed, s["rows_ready"], j + 1)
                at = bass.ds(j, 1) if not isinstance(j, int) else slice(j, j + 1)
                pool.tensor_copy(c.expert1[:, at, :], placed[:].unsqueeze(1))
                pool.tensor_copy(c.rank1[:, at, :], w.rank[:].unsqueeze(1))
                pool.tensor_copy(c.topv[:, at, :], tv[:].unsqueeze(1)).then_inc(s["kept"], 1)
                for n in range(PT):
                    pool.indirect_dma_start(a.xg1, bass.IndirectOffsetOnAxis(ap=w.slot_i[:, n:n + 1], axis=0),
                                            rows_out[:, n, :], None, bounds_check=EXP * REGION - 1,
                                            oob_is_err=False).then_inc(sent, 16)

            def count_sent(j):
                pool.wait_ge(s["kept"], j + 1)
                pool.wait_ge(sent, (j + 1) * (16 * PT))
                pool.sem_inc(s["rows_sent"], 1)

            def add_beta(j):
                wait_apart(pool, c.passed, s["x2_ready"], j + 1)
                hj = pair_tiles(c.h, j)
                pool.tensor_tensor(hj, hj, c.beta[:].unsqueeze(1).to_broadcast([P, PT, D]), ALU.add)\
                    .then_inc(s["beta_added"], 1)

            def pair(j, place, finish, prepare, after, fetching):
                if after:
                    add_experts(j + 2)
                if place:
                    send(j - 2)
                if prepare:
                    unit_vectors(j + 1)
                if fetching:
                    refetch(j + 3)
                if finish:
                    add_beta(j - 1)
                if place:
                    count_sent(j - 2)
                if after:
                    add_bout(j + 2)

            fetch(0)
            add_experts(0)
            refetch(1)
            add_bout(0)
            unit_vectors(0)
            add_experts(1)
            refetch(2)
            add_bout(1)
            pair(0, False, False, True, True, True)
            pair(1, False, True, True, True, True)
            with pool.Fori(2, PAIRS - 3) as j:
                pair(j, True, True, True, True, True)
            pair(PAIRS - 3, True, True, True, True, False)
            pair(PAIRS - 2, True, True, True, False, False)
            pair(PAIRS - 1, True, True, False, False, False)
            send(PAIRS - 2)
            add_beta(PAIRS - 1)
            count_sent(PAIRS - 2)
            send(PAIRS - 1)
            pool.wait_ge(s["bout_added"], PAIRS)
            pool.wait_ge(s["beta_added"], PAIRS)
            pool.wait_ge(sent, 16 * PT * PAIRS)

        @block.tensor
        def _(pe):
            def products(j, q, u):
                p, g = u % UNITS // GP, u % GP
                if u % HALF == 0:
                    pe.wait_ge(s["zT_ready"], (j + u // UNITS) * 4 + p * 2 + g // HALF + 1)
                pe.wait_ge(s["ex_ready"], freed(j, u))
                pe.wait_ge(s["pr2_ready"], freed(j, u))
                pe.matmul(F_BANK, c.omega[:, g, :], zT[parity(q, u)][:, p, g // HALF, :],
                          start=True, stop=True).then_inc(s["f_made"], 1)

            def scores(j, u):
                pe.wait_ge(s["feat_ready"], made(j, u, "feat_ready"))
                pe.wait_ge(s["a_masked"], freed(j, u))
                f = feat[u % RING]
                for hh in two:
                    r = slice(NF * hh, NF * (hh + 1))
                    out = a_banks(u)[:, hh, :]
                    pe.matmul(out[:, 0:T], f[r, T:T + P], f[r, 0:T], start=True, stop=True)
                    ins = pe.matmul(out[:, T:T + P], f[r, T + P:2 * T], f[r, P:T], start=True, stop=True)
                ins.then_inc(s["a_made"], 1)

            def values(j, q, u):
                p, g = u // GP, u % GP
                pe.wait_ge(s["a_masked"], made(j, u, "a_masked"))
                if u % HALF == 0:
                    pe.wait_ge(s["ctx_ready"], j * (UNITS // HALF) + u // HALF + 1)
                at, v = attn[u % AT_RING], vone[q]
                for hh in two:
                    head = 2 * g + hh
                    k = head % HEADS % (2 * HALF)
                    out = [AV_BANK[:, (t * 2 * HALF + k) * V1:(t * 2 * HALF + k + 1) * V1] for t in two]
                    pe.matmul(out[0], at[:, hh, 0, :], v[:, p, 0, head, :], start=True, stop=True)
                    pe.matmul(out[1], at[:, hh, 1, :], v[:, p, 0, head, :], start=True, stop=False)
                    ins = pe.matmul(out[1], at[:, hh, 2, :], v[:, p, 1, head, :], start=False, stop=True)
                ins.then_inc(s["av_made"], 1)

            def turn_x(j):
                pe.wait_ge(s["x_ready"], j + 1)
                if not first(j):
                    pe.wait_ge(s["zT_ready"], j * 4)
                for p in two:
                    turn_tiles(pe, c, E[p], xn[:, p * TT:(p + 1) * TT], DC).then_inc(s["x_turned"], 1)

            def make_qk(j, p):
                for t in two:
                    if p == 0:
                        pe.wait_ge(s["xT_ready"], turn(j, t))
                    else:
                        pe.wait_ge(s["qk_ready"], j * 4 + t + 1)
                    for k in range(DC):
                        ins = pe.matmul(E[t][:], xT[p][:, k, t * P:(t + 1) * P], c.wqkvT[:, k, 0:2 * D],
                                        start=k == 0, stop=k == DC - 1)
                    ins.then_inc(s["qk_made"], 1)

            def make_v(j):
                for p in two:
                    pe.wait_ge(s["qk_ready"], j * 4 + 3 + p)
                    for t in range(TT):
                        for k in range(DC):
                            ins = pe.matmul(E[p][:, t * D:(t + 1) * D], xT[p][:, k, t * P:(t + 1) * P],
                                            c.wqkvT[:, k, 2 * D:3 * D], start=k == 0, stop=k == DC - 1)
                    ins.then_inc(s["v_made"], 1)

            def turn_z(j, p):
                pe.wait_ge(s["z_ready"], turn(j, p))
                for k in range(DC):
                    if p == 0:
                        pe.wait_ge(s["v_ready"], turn(j, k))
                    else:
                        pe.wait_ge(s["zT_ready"], j * 4 + k + 1)
                    for part in two:
                        for t in range(TT):
                            col = part * D + k * P
                            ins = pe.transpose(E[k][:, part * T + t * P:part * T + (t + 1) * P],
                                               qk[:, p, t, col:col + P], c.ident[:])
                    ins.then_inc(s["z_turned"], 1)

            def turn_context(j, q):
                pe.wait_ge(s["ctx_ready"], j * (UNITS // HALF) + UNITS // HALF + AHEAD["ctx_ready"])
                for p in two:
                    turn_tiles(pe, c, E[p], ctxv[q][:, p * TT:(p + 1) * TT], DC).then_inc(s["ctx_turned"], 1)

            def project(j):
                for p in two:
                    pe.wait_ge(s["ctxT_ready"], turn(j, p))
                    for t in range(TT):
                        for k in range(DC):
                            ins = pe.matmul(E[p][:, t * D:(t + 1) * D], ctxT[p][:, k, t * P:(t + 1) * P],
                                            c.woutT[:, k, :], start=k == 0, stop=k == DC - 1)
                    ins.then_inc(s["o_made"], 1)

            def turn_x2(j):
                pe.wait_ge(s["x2_ready"], j + 1)
                for p in two:
                    turn_tiles(pe, c, E[p], x2n[:, p * TT:(p + 1) * TT], DC).then_inc(s["x2_turned"], 1)

            def router(j):
                pe.wait_ge(s["x2T_ready"], turn(j, 1))
                for p in two:
                    for k in range(DC):
                        ins = pe.matmul(E[0][0:EXP, p * T:(p + 1) * T], c.gateT[:, k, :], x2T[p][:, k, :],
                                        start=k == 0, stop=k == DC - 1)
                ins.then_inc(s["lT_made"], 1)

            def turn_logits(j):
                wait_apart(pe, c.passed, s["lT_ready"], j + 1)
                for n in range(PT):
                    ins = pe.transpose(E[1][:, n * EXP:(n + 1) * EXP], lT[:, n * P:(n + 1) * P],
                                       c.ident[0:EXP, 0:EXP])
                ins.then_inc(s["l_made"], 1)

            def ranks(j):
                pe.wait_ge(s["took_ready"], j + 1)
                pair_ranks(pe, c, E[1], w, w.hot[:, 0]).then_inc(s["r_made"], 1)

            def pair(j, q, place, finish, prepare, after):
                early = 0 if prepare else 1
                for u in range(UNITS):
                    if u + LEAD < UNITS or prepare:
                        products(j, q, u + LEAD)
                    if u + 2 < UNITS or prepare:
                        scores(j, u + 2)
                    if finish and u + early == 15:
                        turn_logits(j - 1)
                    values(j, q, u)
                    if prepare and u == 1:
                        make_qk(j + 1, 0)
                    if prepare and u == 3:
                        make_qk(j + 1, 1)
                    if place and u == 4:
                        if prepare:
                            pe.wait_ge(s["qk_ready"], (j + 1) * 4 + 4)
                        ranks(j - 2)
                    if prepare and u == 5:
                        if place:
                            pe.wait_ge(s["slots_ready"], j - 1)
                        make_v(j + 1)
                    if finish and u + early == 7:
                        if prepare:
                            pe.wait_ge(s["v_ready"], turn(j + 1, 1))
                        elif place:
                            pe.wait_ge(s["slots_ready"], j - 1)
                        turn_context(j - 1, 1 - q)
                    if finish and u + early == 8:
                        project(j - 1)
                    if prepare and u == 10:
                        if finish:
                            pe.wait_ge(s["o_added"], j)
                        turn_z(j + 1, 0)
                    if prepare and u == 12:
                        turn_z(j + 1, 1)
                    if finish and u + early == 13:
                        if prepare:
                            pe.wait_ge(s["zT_ready"], (j + 1) * 4 + 4)
                        turn_x2(j - 1)
                    if finish and u + early == 14:
                        router(j - 1)
                    if after and u == 15:
                        if finish:
                            pe.wait_ge(s["logits_ready"], j)
                        turn_x(j + 2)

            turn_x(0)
            make_qk(0, 0)
            make_qk(0, 1)
            make_v(0)
            turn_z(0, 0)
            turn_z(0, 1)
            for u in range(LEAD):
                products(0, 0, u)
                if u >= 2:
                    scores(0, u - 2)
            turn_x(1)
            pair(0, 0, False, False, True, True)
            pair(1, 1, False, True, True, True)
            with pe.Fori(1, PAIRS // 2 - 1) as i:
                for q in two:
                    pair(i * 2 + q, q, True, True, True, True)
            pair(PAIRS - 2, 0, True, True, True, False)
            pair(PAIRS - 1, 1, True, True, False, False)
            pe.wait_ge(s["logits_ready"], PAIRS - 1)
            turn_context(PAIRS - 1, 1)
            project(PAIRS - 1)
            pe.wait_ge(s["o_added"], PAIRS)
            ranks(PAIRS - 2)
            pe.wait_ge(s["slots_ready"], PAIRS - 1)
            turn_x2(PAIRS - 1)
            router(PAIRS - 1)
            turn_logits(PAIRS - 1)
            ranks(PAIRS - 1)

        @block.scalar
        def _(act):
            def feature_parts(j, u):
                act.wait_ge(s["f_made"], made(j, u))
                act.wait_ge(s["feat_ready"], freed(j, u))
                act.activation(ex[u % RING][:], F_BANK, ACT.Exp, scale=c.f_scale[:], bias=c.f_shift[:])\
                    .then_inc(s["ex_ready"], 1)
                act.activation(pr2[u % RING][:], F_BANK, ACT.Square).then_inc(s["pr2_ready"], 1)

            def normed(j):
                act.wait_ge(s["norm_known"], j + 1)
                if not first(j):
                    wait_apart(act, c.passed, s["x_turned"], turn(j - 1, 1))
                for n in range(PT):
                    ins = act.activation(xn[:, n:n + 1, :], pair_tiles(c.h, j, n), ACT.Identity,
                                         scale=norm.rstd[:, n:n + 1], bias=shift[:, n:n + 1])
                ins.then_inc(s["x_ready"], 1)

            def copy_x(j):
                if not first(j):
                    act.wait_ge(s["v_made"], turn(j - 1, 1))
                for p in two:
                    act.wait_ge(s["x_turned"], turn(j, p))
                    act.activation(xT[p][:].rearrange("p k t -> p (k t)"), E[p][:], ACT.Copy)\
                        .then_inc(s["xT_ready"], 1)

            def weigh(j, k):
                if k == 0:
                    act.wait_ge(fetched, (j + 1) * (16 * 2 * PT))
                for n in range(k * PT, (k + 1) * PT):
                    act.activation(yrow[:, n, :], yrow[:, n, :], ACT.Copy, scale=gate_now[:, n:n + 1])\
                        .then_inc(s["weighted"], 1)

            def squares(j, p):
                act.wait_ge(s["qk_ready"], j * 4 + 2 * p + 2)
                if not first(j):
                    act.wait_ge(s["sq_read"], turn(j - 1, p))
                act.activation(sq[p][:], qk[:, p], ACT.Square).then_inc(s["sq_ready"], 1)

            def copy_z(j, p, q):
                if p == 0 and not isinstance(j, int):
                    act.wait_ge(s["f_made"], made(j - 1, 0))
                for k in range(DC):
                    act.wait_ge(s["z_turned"], j * 4 + p * 2 + k + 1)
                    act.activation(zT[q][:, p, k, :], E[k][:], ACT.Copy).then_inc(s["zT_ready"], 1)

            def copy_context(j):
                for p in two:
                    act.wait_ge(s["ctx_turned"], turn(j, p))
                    act.activation(ctxT[p][:].rearrange("p k t -> p (k t)"), E[p][:], ACT.Copy)\
                        .then_inc(s["ctxT_ready"], 1)

            def normed2(j):
                if not first(j):
                    wait_apart(act, c.passed, s["rows_ready"], j)
                wait_apart(act, c.passed, s["norm2_known"], j + 1)
                for n in range(PT):
                    ins = act.activation(x2n[:, n:n + 1, :], pair_tiles(c.h, j, n), ACT.Identity,
                                         scale=norm2.rstd[:, n:n + 1], bias=shift2[:, n:n + 1])
                ins.then_inc(s["x2_ready"], 1)

            def copy_x2(j):
                for p in two:
                    act.wait_ge(s["x2_turned"], turn(j, p))
                    act.activation(x2T[p][:].rearrange("p k t -> p (k t)"), E[p][:], ACT.Copy)\
                        .then_inc(s["x2T_ready"], 1)

            def copy_logits(j):
                act.wait_ge(s["lT_made"], j + 1)
                act.activation(lT[:], E[0][0:EXP, :], ACT.Copy).then_inc(s["lT_ready"], 1)

            def logits(j):
                act.wait_ge(s["l_made"], j + 1)
                act.activation(w.logits[:], E[1][:, 0:PT * EXP].rearrange("p (t e) -> p t e", t=PT), ACT.Copy)\
                    .then_inc(s["logits_ready"], 1)

            def gates_rows(j):
                act.wait_ge(s["nbest_ready"], j + 1)
                for n in range(PT):
                    act.activation(prob[:, n, :], w.logits[:, n, :], ACT.Exp, bias=nbest[:, n:n + 1],
                                   accum_out=psum_p[:, n:n + 1]).then_inc(s["prob_ready"], 1)
                act.wait_ge(s["rows_sent"], j + AHEAD["rows_sent"])
                act.activation(rows_out[:], x2n[:], ACT.Copy).then_inc(s["rows_ready"], 1)

            def pair(j, q, place, finish, prepare, after):
                early = 0 if prepare else 1
                for u in range(UNITS):
                    if u + LEAD < UNITS or prepare:
                        feature_parts(j, u + LEAD)
                    if place and u == 2:
                        gates_rows(j - 2)
                    if after and u in (1, 2):
                        weigh(j + 2, u - 1)
                    if prepare and u in (3, 5):
                        squares(j + 1, u // 4)
                    if finish and u + early == 8:
                        copy_context(j - 1)
                    if finish and u + early == 12:
                        normed2(j - 1)
                    if prepare and u in (10, 12):
                        copy_z(j + 1, u // 12, 1 - q)
                    if finish and u + early == 13:
                        copy_x2(j - 1)
                    if after and u == 14:
                        normed(j + 2)
                    if finish and u + early == 15:
                        logits(j - 1)
                    if after and u == 15:
                        copy_x(j + 2)
                    if finish and u + early == 14:
                        copy_logits(j - 1)

            for name in ("ex_ready", "pr2_ready", "rows_sent"):
                act.sem_inc(s[name], AHEAD[name])
            for k in two:
                weigh(0, k)
            normed(0)
            copy_x(0)
            squares(0, 0)
            squares(0, 1)
            for k in two:
                weigh(1, k)
            copy_z(0, 0, 0)
            copy_z(0, 1, 0)
            for u in range(LEAD):
                if u == 3:
                    normed(1)
                feature_parts(0, u)
            copy_x(1)
            pair(0, 0, False, False, True, True)
            pair(1, 1, False, True, True, True)
            with act.Fori(1, PAIRS // 2 - 1) as i:
                for q in two:
                    pair(i * 2 + q, q, True, True, True, True)
            pair(PAIRS - 2, 0, True, True, True, False)
            pair(PAIRS - 1, 1, True, True, False, False)
            copy_context(PAIRS - 1)
            gates_rows(PAIRS - 2)
            normed2(PAIRS - 1)
            copy_x2(PAIRS - 1)
            copy_logits(PAIRS - 1)
            logits(PAIRS - 1)
            gates_rows(PAIRS - 1)
            zero_tails(act, 1)

        @block.vector
        def _(dve):
            step = Steps(dve, sem("dve"), c.passed)

            def features(j, u):
                dve.wait_ge(s["ex_ready"], made(j, u, "ex_ready"))
                dve.tensor_scalar(ex[u % RING][:], ex[u % RING][:], EXP_LO, EXP_HI, ALU.max, ALU.min)\
                    .then_inc(s["clipped"], 1)
                dve.wait_ge(s["clipped"], made(j, u))
                dve.wait_ge(s["pr2_ready"], made(j, u, "pr2_ready"))
                dve.wait_ge(s["a_made"], freed(j, u))
                dve.scalar_tensor_tensor(feat[u % RING][:], ex[u % RING][:], c.f_weight[:], pr2[u % RING][:],
                                         ALU.mult, ALU.mult).then_inc(s["feat_ready"], 1)

            def mask(j, u):
                dve.wait_ge(s["a_made"], made(j, u, "a_made"))
                dve.wait_ge(s["av_made"], freed(j, u))
                dve.tensor_tensor(
                    attn[u % AT_RING][:].rearrange("p h b t -> p h (b t)"), a_banks(u)[:, :, 0:3 * P],
                    c.causal[:].rearrange("p b t -> p (b t)").unsqueeze(1).to_broadcast([P, 2, 3 * P]),
                    ALU.mult).then_inc(s["a_masked"], 1)

            def context(j, q, part):
                dve.wait_ge(s["av_made"], made(j, part * HALF + HALF - 1, "av_made"))
                av = AV_BANK[:, 0:TT * 2 * HALF * V1].rearrange("p (t h e) -> p t h e", t=TT, e=V1)
                step.run(dve.tensor_scalar(den[:], av[:, :, :, HD], 1e-6, None, ALU.max))
                step.run(dve.reciprocal(den[:], den[:]))
                out = ctxv[q][:, part // 2 * TT:(part // 2 + 1) * TT, part % 2 * P:(part % 2 + 1) * P]
                dve.tensor_tensor(out.rearrange("p t (h e) -> p t h e", e=HD), av[:, :, :, 0:HD],
                                  den[:].unsqueeze(3).to_broadcast([P, TT, HEADS // 2, HD]), ALU.mult)\
                    .then_inc(s["ctx_ready"], 1)

            def statistics(j, norm):
                for n in range(PT):
                    step(dve.bn_stats(norm.stats[:, n, :], pair_tiles(c.h, j, n)))
                step.wait_apart()
                for n in range(PT):
                    step(dve.bn_aggr(norm.mv[:, n, :], norm.stats[:, n, :]))
                step.wait()
                step.run(dve.tensor_scalar(norm.var[:], norm.mv[:, :, 1], LN_EPS, None, ALU.add))

            def summed(j):
                wait_apart(dve, c.passed, s["h_summed"], j + 1)

            def norm_scale(j, norm, shift, normed, known):
                if not first(j):
                    dve.wait_ge(normed, j)
                rsqrt(dve, step, norm.rstd[:], norm.var[:], norm.tmp[:])
                dve.scalar_tensor_tensor(shift[:], norm.mv[:, :, 0], -1.0, norm.rstd[:], ALU.mult, ALU.mult)\
                    .then_inc(known, 1)

            def add_bias(j, p):
                if p == 0 and not first(j):
                    dve.wait_ge(s["z_turned"], j * 4)
                for t in two:
                    dve.wait_ge(s["qk_made"], j * 4 + p * 2 + t + 1)
                    dve.tensor_tensor(qk[:, p, t, :], E[t][:], c.bqkv[:, 0:2 * D], ALU.add)\
                        .then_inc(s["qk_ready"], 1)

            def add_v_bias(j, q):
                for p in two:
                    dve.wait_ge(s["v_made"], turn(j, p))
                    dve.tensor_tensor(vone[q][:, p, :, :, 0:HD], E[p][:].rearrange("p (t h e) -> p t h e", t=TT, e=HD),
                                      c.bqkv[:, 2 * D:3 * D].rearrange("p (a h e) -> p a h e", a=1, e=HD)
                                      .to_broadcast([P, TT, HEADS, HD]), ALU.add).then_inc(s["v_ready"], 1)

            def sum_squares(j, p):
                dve.wait_ge(s["sq_ready"], turn(j, p))
                dve.tensor_reduce(ss[:, p * NG:(p + 1) * NG], sq[p][:].rearrange("p t (g e) -> p (t g) e", e=HD),
                                  AX.X, ALU.add).then_inc(s["sq_read"], 1)

            def length(j, part):
                if part == 0:
                    dve.wait_ge(s["sq_read"], turn(j, 1))
                    step.run(dve.tensor_scalar(ss[:], ss[:], 1e-24, None, ALU.max))
                    rsqrt_guess(dve, step, rn[:], ss[:])
                    rsqrt_refine(dve, step, rn[:], ss[:], rtmp[:])
                else:
                    rsqrt_refine(dve, step, rn[:], ss[:], rtmp[:])
                    rsqrt_refine(dve, step, rn[:], ss[:], rtmp[:])
                    dve.sem_inc(s["length_known"], 1)

            def add_output(j):
                hj = pair_tiles(c.h, j)
                for p in two:
                    hp = two_tiles(c.h, j, p)
                    dve.wait_ge(s["o_made"], turn(j, p))
                    step(dve.tensor_tensor(hp, E[p][:].rearrange("p (t d) -> p t d", t=TT), hp, ALU.add))
                step.wait_apart()
                dve.sem_inc(s["o_added"], 1)

            def choose(j):
                dve.wait_ge(s["logits_ready"], j + 1)
                pair_route(dve, step, w, 1)
                dve.tensor_scalar(nbest[:], w.best[:, :, 0], -1.0, None, ALU.mult).then_inc(s["nbest_ready"], 1)
                step.run(dve.tensor_tensor(w.hot[:, 0], c.iota8[:].unsqueeze(1).to_broadcast([P, PT, EXP]),
                                           w.expert[:, 0, :].unsqueeze(2).to_broadcast([P, PT, EXP]),
                                           ALU.is_equal))
                pair_sums(dve, step, w, w.hot[:, 0], s["took_ready"])

            def place(j):
                dve.wait_ge(s["prob_ready"], PT * (j + 1))
                dve.wait_ge(s["rows_sent"], j + AHEAD["rows_sent"])
                step(dve.tensor_copy(placed[:], w.expert[:, 0, :]))
                step.run(dve.reciprocal(psum_p[:], psum_p[:]))
                step.run(dve.tensor_scalar(tv[:], psum_p[:], 1e-8, None, ALU.add))
                step.run(dve.reciprocal(tv[:], tv[:]))
                step(dve.tensor_tensor(tv[:], tv[:], psum_p[:], ALU.mult))
                dve.wait_ge(s["r_made"], j + 1)
                pair_places(dve, step, w, 1, c.base1, E[1], REGION, None, None, s["slots_ready"])

            def pair(j, q, placing, finish, prepare, after):
                early = 0 if prepare else 1
                for u in range(UNITS):
                    mask(j, u)
                    if u == 0 and (finish or not first(j)):
                        context(j - 1, 1 - q, UNITS // HALF - 1)
                    if u and u % HALF == 0:
                        context(j, q, u // HALF - 1)
                    if u + 3 < UNITS or prepare:
                        features(j, u + 3)
                    if prepare and u in (2, 4):
                        add_bias(j + 1, u // 4)
                    if placing and u == 1:
                        choose(j - 2)
                    if placing and u == 5:
                        place(j - 2)
                    if prepare and u == 4:
                        sum_squares(j + 1, 0)
                    if prepare and u == 6:
                        add_v_bias(j + 1, 1 - q)
                        sum_squares(j + 1, 1)
                    if prepare and u in (7, 8):
                        length(j + 1, u - 7)
                    if after and u == 12:
                        summed(j + 2)
                        statistics(j + 2, norm)
                    if finish and u + early == 9:
                        add_output(j - 1)
                    if finish and u + early == 10:
                        statistics(j - 1, norm2)
                    if finish and u + early == 11:
                        norm_scale(j - 1, norm2, shift2, s["x2_ready"], s["norm2_known"])
                    if after and u == 13:
                        norm_scale(j + 2, norm, shift, s["x_ready"], s["norm_known"])

            step.begin(0)
            step(dve.memset(w.sums[:, 0, :], 0.0))
            for q in two:
                step.run(dve.memset(vone[q][:], 1.0))
            for name in ("feat_ready", "a_masked", "a_made", "av_made", "ctx_ready"):
                dve.sem_inc(s[name], AHEAD[name])
            summed(0)
            statistics(0, norm)
            norm_scale(0, norm, shift, s["x_ready"], s["norm_known"])
            for p in two:
                add_bias(0, p)
            for p in two:
                sum_squares(0, p)
            for part in two:
                length(0, part)
            add_v_bias(0, 0)
            features(0, 0)
            summed(1)
            statistics(1, norm)
            features(0, 1)
            norm_scale(1, norm, shift, s["x_ready"], s["norm_known"])
            features(0, 2)
            pair(0, 0, False, False, True, True)
            pair(1, 1, False, True, True, True)
            start = step.n
            with dve.Fori(1, PAIRS // 2 - 1) as i:
                step.begin((i - 1) * LINEAR_STEPS + start)
                for q in two:
                    pair(i * 2 + q, q, True, True, True, True)
                assert step.n == LINEAR_STEPS, step.n
            step.begin((PAIRS // 2 - 2) * LINEAR_STEPS + start)
            pair(PAIRS - 2, 0, True, True, True, False)
            pair(PAIRS - 1, 1, True, True, False, False)
            context(PAIRS - 1, 1, UNITS // HALF - 1)
            choose(PAIRS - 2)
            add_output(PAIRS - 1)
            statistics(PAIRS - 1, norm2)
            norm_scale(PAIRS - 1, norm2, shift2, s["x2_ready"], s["norm2_known"])
            place(PAIRS - 2)
            choose(PAIRS - 1)
            place(PAIRS - 1)
            step.run(dve.scalar_tensor_tensor(c.tiles_to[:], c.iota8[:], float(REGION), c.base1[:], ALU.mult, ALU.add))
            dve.tensor_copy(tail_i[:], c.tiles_to[:]).then_inc(tails_known, 1)
            dve.wait_ge(tails_known, 1)
            step.run(dve.tensor_scalar(c.tiles[:], c.base1[:], float(P - 1), None, ALU.add))
            step.run(dve.tensor_copy(tiles_i[:], c.tiles[:]))
            step.run(dve.tensor_scalar(tiles_i[:], tiles_i[:], 7, None, ALU.logical_shift_right))
            step.run(dve.tensor_copy(c.tiles[:], tiles_i[:]))
            step.run(dve.tensor_copy(c.tiles_to[:], c.tiles[:]))
            for e in range(1, EXP):
                step.run(dve.tensor_tensor(c.tiles_to[:, e:e + 1], c.tiles_to[:, e - 1:e], c.tiles[:, e:e + 1], ALU.add))
            step.run(dve.tensor_tensor(past[:], c.tile_no[:].unsqueeze(2).to_broadcast([P, MT, EXP]),
                                       c.tiles_to[:].unsqueeze(1).to_broadcast([P, MT, EXP]), ALU.is_ge))
            step.run(dve.tensor_reduce(ej[:], past[:], AX.X, ALU.add))
            step.run(dve.tensor_tensor(past[:], past[:], c.tiles[:].unsqueeze(1).to_broadcast([P, MT, EXP]), ALU.mult))
            step.run(dve.tensor_reduce(before[:], past[:], AX.X, ALU.add))
            step.run(dve.tensor_tensor(before[:], c.tile_no[:], before[:], ALU.subtract))
            step.run(dve.tensor_scalar(before[:], before[:], float(P), None, ALU.mult))
            step.run(dve.scalar_tensor_tensor(row[:], ej[:], float(REGION), before[:], ALU.mult, ALU.add))
            step.run(dve.tensor_scalar(c.row_in[:], row[:], float(EXP * REGION), None, ALU.min))
            dve.tensor_scalar(c.e_i[:], ej[:], float(EXP - 1), None, ALU.min)


def moe1(nc, c, a):
    with ExitStack() as ctx:
        sb, sem = scope(nc, ctx, "moe1")
        UN, MT = MOE1_FLIGHT, MOE1_TILES
        HC = HID1 // P
        hot = sb("hot", [P, TILES, EXP])
        first = sb("first", [P, TILES])
        q4 = range(UN)
        x = [sb(f"x{q}", [P, D]) for q in q4]
        xT = [sb(f"xT{q}", [P, DC, P]) for q in q4]
        g = [sb(f"g{q}", [P, HID1]) for q in q4]
        gT = [sb(f"gT{q}", [P, HC, P]) for q in q4]
        y = [sb(f"y{q}", [P, D]) for q in q4]
        W2 = sb("W2", [P, HC * EXP, D])
        w_loaded = [sem(f"w_loaded{e}") for e in range(EXP)]
        experts_ready = sem("experts_ready")
        loaded = [sem(f"loaded{q}") for q in q4]
        stored = sem("stored")
        names = "x_turned xT_ready h_made g_ready g_turned gT_ready y_made y_ready y_stored".split()
        s = {n: sem(n) for n in names}
        block = ctx.enter_context(nc.Block())

        def done(i, q):
            return i * UN + q + 1

        @block.sync
        def _(sp):
            def load(t, q):
                r = sp.value_load(c.row_in[0:1, bass.ds(t, 1)] if not isinstance(t, int) else c.row_in[0:1, t:t + 1],
                                  min_val=0, max_val=EXP * REGION)
                sp.dma_start(x[q][:], a.xg1[bass.ds(r, P), :]).then_inc(loaded[q], 16)

            for q in q4:
                load(q, q)
            def load_weights(e):
                sp.dma_start(W2[:, HC * e:HC * (e + 1), :], a.ew2[e].rearrange("(k p) n -> p k n", p=P))\
                    .then_inc(w_loaded[e], 16)

            load_weights(0)
            load_weights(1)
            for q in q4:
                sp.wait_ge(s["x_turned"], done(0, q))
                load(UN + q, q)
            for e in range(2, EXP):
                load_weights(e)
            for e in range(EXP):
                sp.wait_ge(w_loaded[e], 16)
                sp.sem_inc(experts_ready, 1)
            with sp.Fori(1, MT // UN - 1) as i:
                for q in q4:
                    sp.wait_ge(s["x_turned"], done(i, q))
                    load((i + 1) * UN + q, q)

        @block.gpsimd
        def _(pool):
            pool.sem_inc(s["y_stored"], UN)
            with pool.Fori(0, MT // UN) as i:
                for q in q4:
                    pool.wait_ge(s["y_ready"], done(i, q) + UN)
                    pool.dma_start(a.y1[bass.ds((i * UN + q) * P, P), :], y[q][:]).then_inc(stored, 16)
                    pool.wait_ge(stored, 16 * done(i, q))
                    pool.sem_inc(s["y_stored"], 1)

        @block.tensor
        def _(pe):
            def bank(q, k):
                return c.bank[2 * q + k]

            with pe.Fori(0, MT // UN) as i:
                e = [pe.value_load(c.e_i[0:1, bass.ds(i * UN + q, 1)], min_val=0, max_val=EXP - 1) for q in q4]
                for q in q4:
                    pe.wait_ge(loaded[q], 16 * (i + 1))
                    for k in range(DC):
                        ins = pe.transpose(bank(q, 0)[:, k * P:(k + 1) * P], x[q][:, k * P:(k + 1) * P], c.ident[:])
                    ins.then_inc(s["x_turned"], 1)
                for q in q4:
                    pe.wait_ge(s["xT_ready"], done(i, q))
                    pe.wait_ge(s["y_ready"], i * UN + q + 1)
                    for k in range(DC):
                        ins = pe.matmul(bank(q, 1)[:], xT[q][:, k, :], c.W1[:, bass.ds(e[q] * DC + k, 1), :],
                                        start=k == 0, stop=k == DC - 1)
                    ins.then_inc(s["h_made"], 1)
                for q in q4:
                    pe.wait_ge(s["g_ready"], done(i, q))
                    for k in range(HC):
                        ins = pe.transpose(bank(q, 0)[:, k * P:(k + 1) * P], g[q][:, k * P:(k + 1) * P], c.ident[:])
                    ins.then_inc(s["g_turned"], 1)
                for q in q4:
                    wait_apart(pe, c.passed, experts_ready, e[q] + 1)
                    pe.wait_ge(s["gT_ready"], done(i, q))
                    for k in range(HC):
                        ins = pe.matmul(bank(q, 1)[:, 0:D], gT[q][:, k, :], W2[:, bass.ds(e[q] * HC + k, 1), :],
                                        start=k == 0, stop=k == HC - 1)
                    ins.then_inc(s["y_made"], 1)

        @block.scalar
        def _(act):
            act.sem_inc(s["y_ready"], UN)
            with act.Fori(0, MT // UN) as i:
                for q in q4:
                    act.wait_ge(s["h_made"], done(i, q))
                    act.activation(g[q][:], c.bank[2 * q + 1][:], ACT.Gelu).then_inc(s["g_ready"], 1)
                for q in q4:
                    act.wait_ge(s["y_made"], done(i, q))
                    act.wait_ge(s["y_stored"], done(i, q))
                    act.activation(y[q][:], c.bank[2 * q + 1][:, 0:D], ACT.Copy).then_inc(s["y_ready"], 1)

        @block.vector
        def _(dve):
            step = Steps(dve, sem("dve"), c.passed)
            step.run(dve.tensor_tensor(hot[:], c.iota8[:].unsqueeze(1).to_broadcast([P, TILES, EXP]),
                                       c.expert1[:].rearrange("p b t -> p (b t)").unsqueeze(2)
                                       .to_broadcast([P, TILES, EXP]), ALU.is_equal))
            step.run(dve.tensor_tensor(c.tiles[:], c.tiles_to[:], c.tiles[:], ALU.subtract))
            step.run(dve.tensor_tensor(hot[:], hot[:], c.tiles[:].unsqueeze(1).to_broadcast([P, TILES, EXP]), ALU.mult))
            step.run(dve.tensor_reduce(first[:], hot[:], AX.X, ALU.add))
            step.run(dve.scalar_tensor_tensor(c.place1[:].rearrange("p b t -> p (b t)"), first[:], float(P),
                                              c.rank1[:].rearrange("p b t -> p (b t)"), ALU.mult, ALU.add))
            with dve.Fori(0, MT // UN) as i:
                for q in q4:
                    dve.wait_ge(s["x_turned"], done(i, q))
                    dve.tensor_copy(xT[q][:].rearrange("p k t -> p (k t)"), c.bank[2 * q][:, 0:D])\
                        .then_inc(s["xT_ready"], 1)
                for q in q4:
                    dve.wait_ge(s["g_turned"], done(i, q))
                    dve.tensor_copy(gT[q][:].rearrange("p k t -> p (k t)"), c.bank[2 * q][:])\
                        .then_inc(s["gT_ready"], 1)


def back(nc, c, a):
    with ExitStack() as ctx:
        sb, sem = scope(nc, ctx, "back")
        two = range(2)
        TWOS = PAIRS // 2
        yrow = [[sb(f"yrow{r}{q}", [P, PT, D]) for q in two] for r in two]
        place_now = [[sb(f"place_now{r}{q}", [P, PT], U32) for q in two] for r in two]
        o = [sb(f"o{q}", [P, PT, D]) for q in two]
        stats, mv = sb("stats", [P, 2 * PT, 6]), sb("mv", [P, 2 * PT, 2])
        t, var, root, tmp, rstd, shift = (sb(n, [P, 2 * PT]) for n in ("t", "var", "root", "tmp", "rstd", "shift"))
        fetched = [[sem(f"fetched{r}{q}") for q in two] for r in two]
        stored = [sem(f"stored{q}") for q in two]
        names = "placed rstd_ready normed out_ready".split()
        s = {n: sem(n) for n in names}
        block = ctx.enter_context(nc.Block())

        @block.sync
        def _(sp):
            for q in two:
                sp.sem_inc(stored[q], 1)
            with sp.Fori(0, TWOS) as m:
                for q in two:
                    sp.wait_ge(s["out_ready"], m * 2 + q + 1)
                    sp.dma_start(a.out[bass.ds(m * 4 + q * 2, 2)].rearrange("b (t p) d -> p (b t) d", p=P), o[q][:])\
                        .then_inc(stored[q], 16)
            for q in two:
                sp.wait_ge(stored[q], 16 * TWOS + 1)

        @block.gpsimd
        def _(pool):
            def fetch(j, r, q):
                pool.tensor_copy(place_now[r][q][:].unsqueeze(1), c.place1[:, bass.ds(j, 1), :]
                                 if not isinstance(j, int) else c.place1[:, j:j + 1, :]).then_inc(s["placed"], 1)
                wait_apart(pool, c.passed, s["placed"], j + 1)
                for n in range(PT):
                    pool.indirect_dma_start(yrow[r][q][:, n, :], None, a.y1,
                                            bass.IndirectOffsetOnAxis(ap=place_now[r][q][:, n:n + 1], axis=0),
                                            bounds_check=MOE1_TILES * P - 1, oob_is_err=False)\
                        .then_inc(fetched[r][q], 16)

            for j in range(4):
                fetch(j, j // 2, j % 2)
            with pool.Fori(0, TWOS // 2 - 1) as i:
                for r in two:
                    for q in two:
                        j = i * 4 + r * 2 + q
                        pool.wait_ge(s["normed"], (j + 1) * PT)
                        fetch(j + 4, r, q)

        @block.scalar
        def _(act):
            with act.Fori(0, TWOS // 2) as i:
                for r in two:
                    m = i * 2 + r
                    act.wait_ge(s["rstd_ready"], m + 1)
                    for q in two:
                        act.wait_ge(stored[q], m * 16 + 1)
                        for n in range(PT):
                            k = q * PT + n
                            act.activation(o[q][:, n, :], yrow[r][q][:, n, :], ACT.Identity, scale=rstd[:, k:k + 1],
                                           bias=shift[:, k:k + 1]).then_inc(s["normed"], 1)

        @block.vector
        def _(dve):
            step = Steps(dve, sem("dve"), c.passed)

            def statistics(i, m, r):
                for q in two:
                    dve.wait_ge(fetched[r][q], (i + 1) * (16 * PT))
                    for n in range(PT):
                        step(dve.bn_stats(stats[:, q * PT + n, :], yrow[r][q][:, n, :]))
                step(dve.tensor_copy(t[:].rearrange("p (a n) -> p a n", a=2), c.topv[:, bass.ds(m * 2, 2), :]))
                step.wait_apart()
                for n in range(2 * PT):
                    step(dve.bn_aggr(mv[:, n, :], stats[:, n, :]))
                step.wait()
                step.run(dve.tensor_tensor(var[:], mv[:, :, 1], t[:], ALU.mult))
                step.run(dve.tensor_tensor(var[:], var[:], t[:], ALU.mult))
                step.run(dve.tensor_scalar(var[:], var[:], LN_EPS, None, ALU.add))
                rsqrt(dve, step, root[:], var[:], tmp[:])
                step.run(dve.tensor_tensor(rstd[:], root[:], t[:], ALU.mult))
                dve.scalar_tensor_tensor(shift[:], mv[:, :, 0], -1.0, rstd[:], ALU.mult, ALU.mult)\
                    .then_inc(s["rstd_ready"], 1)

            def scale_add(m):
                for q in two:
                    dve.wait_ge(s["normed"], (m * 2 + q + 1) * PT)
                    step.run(dve.tensor_tensor(o[q][:], o[q][:], c.gamma[:].unsqueeze(1).to_broadcast([P, PT, D]),
                                               ALU.mult))
                    dve.tensor_tensor(o[q][:], o[q][:], pair_tiles(c.h, m * 2 + q), ALU.add)\
                        .then_inc(s["out_ready"], 1)

            with dve.Fori(0, TWOS // 2) as i:
                step.begin(i * BACK_STEPS)
                for r in two:
                    m = i * 2 + r
                    statistics(i, m, r)
                    scale_add(m)
                assert step.n == BACK_STEPS, step.n


def lm_tower(nc, ins, out):
    a = Chip()
    a.out = out
    a.x = ins["x"]
    a.emb = [ins[f"L0_tok_emb_{i}"] for i in range(4)]
    a.proj = [ins[f"L0_tok_proj_{i}"] for i in range(4)]
    a.QK, a.VO = ins["L0_attn_QK"], ins["L0_attn_VO"]
    a.Wr, a.br = ins["L0_ffn_Wr"], ins["L0_ffn_br"]
    a.W1, a.b1, a.W2, a.b2 = (ins[f"L0_ffn_{n}"] for n in ("W1", "b1", "W2", "b2"))
    a.w_qkv, a.b_qkv, a.w_out, a.b_out, a.omega, a.nodes, a.qw = (
        ins[f"L1_attn_{n}"] for n in ("w_qkv", "b_qkv", "w_out", "b_out", "omega", "quad_nodes", "quad_weights"))
    a.gate_w, a.ew1, a.ew2, a.gamma, a.beta = (
        ins[f"L1_ffn_{n}"] for n in ("gate_w", "expert_w1", "expert_w2", "ln_gamma", "ln_beta"))
    a.xg0 = nc.dram_tensor("rows_moe2", [EXP * CAP, D], F32, kind="Internal").ap()
    a.y0 = nc.dram_tensor("out_moe2", [EXP * CAP + 1, D], F32, kind="Internal").ap()
    a.xg1 = nc.dram_tensor("rows_moe1", [EXP * REGION + P, D], F32, kind="Internal").ap()
    a.y1 = nc.dram_tensor("out_moe1", [MOE1_TILES * P, D], F32, kind="Internal").ap()
    c = Chip()
    with ExitStack() as ctx:
        sb, sem = scope(nc, ctx, "all")
        c.passed = sem("passed")
        MT = MOE1_TILES
        c.ps = ctx.enter_context(nc.psum_tensor("banks", [P, 8, 512], F32))
        c.bank = [c.ps[:, k, :] for k in range(8)]
        c.h = sb("h", [P, TILES, D])
        c.zero = sb("zero", [P, D])
        c.ident, c.ones, c.before = (sb(n, [P, P]) for n in ("ident", "ones", "before"))
        c.causal = sb("causal", [P, 3, P])
        c.iota8 = sb("iota8", [P, EXP])
        c.tile_no = sb("tile_no", [P, MT])
        c.place0 = sb("place0", [P, PAIRS, 2 * PT], U32)
        c.gates = sb("gates", [P, PAIRS, 2 * PT])
        c.expert1, c.rank1 = sb("expert1", [P, PAIRS, 2 * TT]), sb("rank1", [P, PAIRS, 2 * TT])
        c.tiles, c.tiles_to = sb("tiles", [P, EXP]), sb("tiles_to", [P, EXP])
        c.row_in, c.e_i = sb("row_in", [P, MT], I32), sb("e_i", [P, MT], I32)
        c.place1 = sb("place1", [P, PAIRS, 2 * TT], U32)
        c.topv = sb("topv", [P, PAIRS, 2 * TT])
        c.base0, c.base1 = sb("base0", [P, EXP]), sb("base1", [P, EXP])
        c.Wr, c.br = sb("Wr", [P, DC, EXP]), sb("br", [P, EXP])
        c.wqkvT, c.bqkv = sb("wqkvT", [P, DC, 3 * D]), sb("bqkv", [P, 3 * D])
        c.woutT, c.bout = sb("woutT", [P, DC, D]), sb("bout", [P, D])
        c.omega = sb("omega", [P, HEADS // 2, P])
        c.nodes, c.qw = sb("nodes", [P, 2]), sb("qw", [P, 2])
        c.f_scale, c.f_shift, c.f_weight = (sb(n, [P, 1]) for n in ("f_scale", "f_shift", "f_weight"))
        c.b1T = sb("b1T", [P, EXP * HID0 // P])
        c.gateT = sb("gateT", [P, DC, EXP])
        c.gamma, c.beta = sb("gamma", [P, D]), sb("beta", [P, D])
        with ExitStack() as early:
            early_sb, _ = scope(nc, early, "early")
            c.cat = early_sb("cat", [P, PT, CAT])
            c.token_row = early_sb("token_row", [P, 4, TILES], U32)
            c.proj = early_sb("proj", [P, DC, CAT])
            c.projT = early_sb("projT", [P, KC, D])
            c.zeros = early_sb("zeros", [P, 2048])
            c.QK, c.VO = early_sb("QK", [P, DC, D]), early_sb("VO", [P, DC, D])
            setup(nc, c, a)
            front(nc, c, a)
        moe2(nc, c, a)
        c.W1 = sb("W1", [P, DC * EXP, HID1])
        linear(nc, c, a)
        moe1(nc, c, a)
        back(nc, c, a)


_INS = ['x', 'L0_tok_emb_0', 'L0_tok_emb_1', 'L0_tok_emb_2', 'L0_tok_emb_3', 'L0_tok_proj_0', 'L0_tok_proj_1',
        'L0_tok_proj_2', 'L0_tok_proj_3', 'L0_attn_QK', 'L0_attn_VO', 'L0_ffn_Wr', 'L0_ffn_br', 'L0_ffn_W1',
        'L0_ffn_b1', 'L0_ffn_W2', 'L0_ffn_b2', 'L1_attn_w_qkv', 'L1_attn_b_qkv', 'L1_attn_w_out', 'L1_attn_b_out',
        'L1_attn_omega', 'L1_attn_quad_nodes', 'L1_attn_quad_weights', 'L1_ffn_gate_w', 'L1_ffn_expert_w1',
        'L1_ffn_expert_w2', 'L1_ffn_ln_gamma', 'L1_ffn_ln_beta']


def kernel(**inputs):
    import numpy as _np
    import concourse.bacc as _bacc
    from concourse import mybir as _mybir
    from concourse.bass_utils import run_bass_kernel_spmd as _run

    nc = _bacc.Bacc("TRN2", target_bir_lowering=False, num_devices=1)
    arrays, args = {}, {}
    for name in _INS:
        arr = _np.ascontiguousarray(inputs[name])
        arrays[f"in_{name}_dram"] = arr
        args[name] = nc.dram_tensor(f"in_{name}_dram", arr.shape, _mybir.dt.from_np(arr.dtype), kind="ExternalInput").ap()
    out = nc.dram_tensor("out_0_dram", (B, T, D), _mybir.dt.from_np(_np.dtype("float32")), kind="ExternalOutput").ap()
    lm_tower(nc, args, out)
    r = _run(nc, [arrays], core_ids=[0])
    return r.results[0]["out_0_dram"]
```
